# Optimizing a Trainium2 kernel written in Bass

```python
import numpy as np
import jax
import jax.numpy as jnp

def _softmax(x, axis=-1):
    return jax.nn.softmax(x, axis=axis)

def _gelu(x):
    return jax.nn.gelu(x, approximate=True)

def _silu(x):
    return jax.nn.silu(x)

def _sigmoid(x):
    return jax.nn.sigmoid(x)

def _layernorm(x, axis=-1, eps=1e-05):
    m = jnp.mean(x, axis=axis, keepdims=True)
    v = jnp.var(x, axis=axis, keepdims=True)
    return (x - m) / jnp.sqrt(v + eps)

def _scatter_add(tgt, idx, src, axis=0):
    return tgt.at[idx].add(src)

def _segment_sum(src, seg, n):
    return jax.ops.segment_sum(src, seg, n)
kernel_name = 'mk_decoder_preln_d1_seqx_r4_d9ed11'

def setup_inputs(seed: int=0):
    np.random.seed(seed)
    _w = jnp.asarray

    def _rec_inputs():
        import jax
        import jax.numpy as jnp
        _rk = jax.random.key(seed)
        x = -0.0002928 + 1 * jax.random.normal(jax.random.fold_in(_rk, 1), (64, 128, 256), jnp.float32)
        _lenS = 128 - jax.random.randint(jax.random.fold_in(_rk, 7), (64,), 0, max(1, 128 // 4) + 1, jnp.int32)
        _lenS2 = 128 - jax.random.randint(jax.random.fold_in(_rk, 8), (64,), 0, max(1, 128 // 4) + 1, jnp.int32)
        _ctx_1024P = jax.random.normal(jax.random.fold_in(_rk, 11), (64, 16, 256), jnp.float32)
        _ctx_1024c = jax.random.dirichlet(jax.random.fold_in(_rk, 511), 0.3 * jnp.ones((16,), jnp.float32), (64, 128))
        _ctx_1024t = jnp.einsum('bsk,bkd->bsd', _ctx_1024c, _ctx_1024P)
        _ctx_1024t = _ctx_1024t * jax.lax.rsqrt(jnp.mean(jnp.square(_ctx_1024t)) + 1e-12) * 0.953939
        ctx_1024 = -1.39393e-06 + 0.999914 * (_ctx_1024t + 0.3 * jax.random.normal(jax.random.fold_in(_rk, 611), (64, 128, 256), jnp.float32))
        return (x, ctx_1024)
    x, ctx_1024 = _rec_inputs()

    def _L0_attn_setup():
        import jax, jax.numpy as jnp
        import numpy as np
        D_MODEL = 256
        N_HEADS = 16
        HEAD_DIM = D_MODEL // N_HEADS
        WINDOW = 128
        LOCAL_BLOCK = 64
        LATENT_TOKENS = 64
        LATENT_D = 64
        LATENT_HEADS = 4
        LATENT_HD = LATENT_D // LATENT_HEADS
        NEG = -1000000000.0

        def _local_attention(q, k, v):
            B, H, S, hd = q.shape
            bs = min(S, max(WINDOW, LOCAL_BLOCK))
            nb = S // bs
            w = WINDOW
            L = bs + w - 1
            k_pad = jnp.pad(k, ((0, 0), (0, 0), (w - 1, 0), (0, 0)))
            v_pad = jnp.pad(v, ((0, 0), (0, 0), (w - 1, 0), (0, 0)))
            starts = jnp.arange(nb) * bs
            idx = starts[:, None] + jnp.arange(L)[None, :]
            kb = k_pad[:, :, idx]
            vb = v_pad[:, :, idx]
            qb = q.reshape(B, H, nb, bs, hd)
            q_pos = starts[:, None] + jnp.arange(bs)[None, :]
            k_gpos = starts[:, None] + jnp.arange(L)[None, :] - (w - 1)
            dist = q_pos[:, :, None] - k_gpos[:, None, :]
            allowed = (dist > 0) & (dist <= w) & (k_gpos[:, None, :] >= 0)
            scale = 1.0 / np.sqrt(hd)
            scores = jnp.einsum('bhnqd,bhnkd->bhnqk', qb, kb) * scale
            scores = jnp.where(allowed, scores, NEG)
            attn = jax.nn.softmax(scores, axis=-1)
            attn = jnp.where(allowed.any(-1)[None, None, :, :, None], attn, 0.0)
            out = jnp.einsum('bhnqk,bhnkd->bhnqd', attn, vb)
            return out.reshape(B, H, S, hd)
        key = jax.random.key(seed)
        ks = jax.random.split(key, 14)
        B, S = (2, 1024)
        s = 0.02
        f32 = jnp.float32
        return {'x': jax.random.normal(ks[0], (B, S, D_MODEL), f32), 'qkv_w': jax.random.normal(ks[1], (D_MODEL, 3 * D_MODEL), f32) * s, 'qkv_b': jnp.zeros((3 * D_MODEL,), f32), 'rq_w': jax.random.normal(ks[2], (D_MODEL, LATENT_D), f32) * s, 'rq_b': jnp.zeros((LATENT_D,), f32), 'rkv_w': jax.random.normal(ks[3], (D_MODEL, 2 * LATENT_D), f32) * s, 'rkv_b': jnp.zeros((2 * LATENT_D,), f32), 'rout_w': jax.random.normal(ks[4], (LATENT_D, D_MODEL), f32) * s, 'rout_b': jnp.zeros((D_MODEL,), f32), 'out_w': jax.random.normal(ks[5], (D_MODEL, D_MODEL), f32) * s, 'out_b': jnp.zeros((D_MODEL,), f32), 'gl_w': jax.random.normal(ks[6], (HEAD_DIM, 1), f32) * s, 'gr_w': jax.random.normal(ks[7], (HEAD_DIM, 1), f32) * s}
    _L0_attn_all = _L0_attn_setup()
    _L0_attn_in = {k: v for k, v in _L0_attn_all.items() if k in ('qkv_w', 'qkv_b', 'rq_w', 'rq_b', 'rkv_w', 'rkv_b', 'rout_w', 'rout_b', 'out_w', 'out_b', 'gl_w', 'gr_w')}
    del _L0_attn_all

    def _L0_xattn_setup():
        import jax, jax.numpy as jnp
        import numpy as np
        NUM_HEADS = 16
        EMBED = 256
        ATTN = 256
        HEAD_DIM = ATTN // NUM_HEADS
        NEG = -2.0 ** 32 + 1.0
        LN_EPS = 1e-05

        def _layer_norm(x, gamma, beta):
            mu = jnp.mean(x, axis=-1, keepdims=True)
            var = jnp.mean(jnp.square(x - mu), axis=-1, keepdims=True)
            return (x - mu) * jax.lax.rsqrt(var + LN_EPS) * gamma + beta
        key = jax.random.key(seed)
        ks = jax.random.split(key, 12)
        B, S = (2, 512)
        scale_in = 1.0 / np.sqrt(EMBED)
        return {'query': jax.random.normal(ks[0], (B, S, EMBED), jnp.float32), 'key': jax.random.normal(ks[1], (B, S, EMBED), jnp.float32), 'value': jax.random.normal(ks[2], (B, S, EMBED), jnp.float32), 'Wq': jax.random.normal(ks[3], (EMBED, ATTN), jnp.float32) * scale_in, 'bq': jnp.zeros((ATTN,), jnp.float32), 'Wk': jax.random.normal(ks[4], (EMBED, ATTN), jnp.float32) * scale_in, 'bk': jnp.zeros((ATTN,), jnp.float32), 'Wv': jax.random.normal(ks[5], (EMBED, ATTN), jnp.float32) * scale_in, 'bv': jnp.zeros((ATTN,), jnp.float32), 'gamma': jnp.ones((ATTN,), jnp.float32), 'beta': jnp.zeros((ATTN,), jnp.float32)}
    _L0_xattn_all = _L0_xattn_setup()
    _L0_xattn_in = {k: v for k, v in _L0_xattn_all.items() if k in ('Wq', 'bq', 'Wk', 'bk', 'Wv', 'bv', 'gamma', 'beta')}
    del _L0_xattn_all

    def _L0_ffn_setup():
        import jax, jax.numpy as jnp
        import numpy as np
        D_MODEL = 256
        NUM_SLOTS = 64
        TOP_K = 8
        B, T = (4, 1024)

        def _forward(x, slot_init, slot_scale, w1, b1, w2, b2, gru_wih, gru_whh, gru_bih, gru_bhh, wv, bv, wo, bo, tau):
            Bn, Tn, D = x.shape
            Sn = slot_init.shape[0]
            S = jnp.broadcast_to((slot_init * slot_scale)[None], (Bn, Sn, D)).astype(x.dtype)
            slot_mean = S.mean(axis=1, keepdims=True)
            ctx = jnp.concatenate([x, jnp.broadcast_to(slot_mean, x.shape)], axis=-1)
            h = jax.nn.gelu(ctx @ w1.T + b1, approximate=False)
            route_logits = (h @ w2.T + b2) / (jnp.abs(tau) + 0.1)
            topk_vals, topk_idx = jax.lax.top_k(route_logits, TOP_K)
            topk_w = jax.nn.softmax(topk_vals, axis=-1)
            alpha = jnp.sum(topk_w[..., None] * jax.nn.one_hot(topk_idx, Sn, dtype=x.dtype), axis=-2)
            slot_input = jnp.einsum('bts,btd->bsd', alpha, x)
            slot_wsum = alpha.sum(axis=1) + 1e-08
            gi = (slot_input / slot_wsum[..., None]).reshape(Bn * Sn, D)
            hs = S.reshape(Bn * Sn, D)
            gx = gi @ gru_wih.T + gru_bih
            gh = hs @ gru_whh.T + gru_bhh
            xr, xz, xn = jnp.split(gx, 3, axis=-1)
            hr, hz, hn = jnp.split(gh, 3, axis=-1)
            r = jax.nn.sigmoid(xr + hr)
            z = jax.nn.sigmoid(xz + hz)
            n = jnp.tanh(xn + r * hn)
            h_new = (1.0 - z) * n + z * hs
            S_new = h_new.reshape(Bn, Sn, D)
            slot_values = S_new @ wv.T + bv
            out = jnp.einsum('bts,bsd->btd', alpha, slot_values)
            return out @ wo.T + bo
        key = jax.random.key(seed)
        ks = jax.random.split(key, 16)
        D, S = (D_MODEL, NUM_SLOTS)
        H = D // 2
        sc = lambda fan_in: 1.0 / np.sqrt(fan_in)
        inp = {'x': jax.random.normal(ks[0], (B, T, D), dtype=jnp.float32), 'slot_init': jax.random.normal(ks[1], (S, D), dtype=jnp.float32) * 0.1, 'slot_scale': jnp.ones((S, 1), dtype=jnp.float32), 'w1': jax.random.normal(ks[2], (H, 2 * D), dtype=jnp.float32) * sc(2 * D), 'b1': jnp.zeros((H,), dtype=jnp.float32), 'w2': jax.random.normal(ks[3], (S, H), dtype=jnp.float32) * sc(H), 'b2': jnp.zeros((S,), dtype=jnp.float32), 'gru_wih': jax.random.normal(ks[4], (3 * D, D), dtype=jnp.float32) * sc(D), 'gru_whh': jax.random.normal(ks[5], (3 * D, D), dtype=jnp.float32) * sc(D), 'gru_bih': jnp.zeros((3 * D,), dtype=jnp.float32), 'gru_bhh': jnp.zeros((3 * D,), dtype=jnp.float32), 'wv': jax.random.normal(ks[6], (D, D), dtype=jnp.float32) * sc(D), 'bv': jnp.zeros((D,), dtype=jnp.float32), 'wo': jax.random.normal(ks[7], (D, D), dtype=jnp.float32) * sc(D), 'bo': jnp.zeros((D,), dtype=jnp.float32), 'tau': jnp.ones((1,), dtype=jnp.float32)}
        return inp
    _L0_ffn_all = _L0_ffn_setup()
    _L0_ffn_in = {k: v for k, v in _L0_ffn_all.items() if k in ('slot_init', 'slot_scale', 'w1', 'b1', 'w2', 'b2', 'gru_wih', 'gru_whh', 'gru_bih', 'gru_bhh', 'wv', 'bv', 'wo', 'bo', 'tau')}
    del _L0_ffn_all
    return {'x': x, 'ctx_1024': ctx_1024, 'L0_attn_qkv_w': _L0_attn_in['qkv_w'], 'L0_attn_qkv_b': _L0_attn_in['qkv_b'], 'L0_attn_rq_w': _L0_attn_in['rq_w'], 'L0_attn_rq_b': _L0_attn_in['rq_b'], 'L0_attn_rkv_w': _L0_attn_in['rkv_w'], 'L0_attn_rkv_b': _L0_attn_in['rkv_b'], 'L0_attn_rout_w': _L0_attn_in['rout_w'], 'L0_attn_rout_b': _L0_attn_in['rout_b'], 'L0_attn_out_w': _L0_attn_in['out_w'], 'L0_attn_out_b': _L0_attn_in['out_b'], 'L0_attn_gl_w': _L0_attn_in['gl_w'], 'L0_attn_gr_w': _L0_attn_in['gr_w'], 'L0_xattn_Wq': _L0_xattn_in['Wq'], 'L0_xattn_bq': _L0_xattn_in['bq'], 'L0_xattn_Wk': _L0_xattn_in['Wk'], 'L0_xattn_bk': _L0_xattn_in['bk'], 'L0_xattn_Wv': _L0_xattn_in['Wv'], 'L0_xattn_bv': _L0_xattn_in['bv'], 'L0_xattn_gamma': _L0_xattn_in['gamma'], 'L0_xattn_beta': _L0_xattn_in['beta'], 'L0_ffn_slot_init': _L0_ffn_in['slot_init'], 'L0_ffn_slot_scale': _L0_ffn_in['slot_scale'], 'L0_ffn_w1': _L0_ffn_in['w1'], 'L0_ffn_b1': _L0_ffn_in['b1'], 'L0_ffn_w2': _L0_ffn_in['w2'], 'L0_ffn_b2': _L0_ffn_in['b2'], 'L0_ffn_gru_wih': _L0_ffn_in['gru_wih'], 'L0_ffn_gru_whh': _L0_ffn_in['gru_whh'], 'L0_ffn_gru_bih': _L0_ffn_in['gru_bih'], 'L0_ffn_gru_bhh': _L0_ffn_in['gru_bhh'], 'L0_ffn_wv': _L0_ffn_in['wv'], 'L0_ffn_bv': _L0_ffn_in['bv'], 'L0_ffn_wo': _L0_ffn_in['wo'], 'L0_ffn_bo': _L0_ffn_in['bo'], 'L0_ffn_tau': _L0_ffn_in['tau']}

def reference(x, ctx_1024, L0_attn_qkv_w, L0_attn_qkv_b, L0_attn_rq_w, L0_attn_rq_b, L0_attn_rkv_w, L0_attn_rkv_b, L0_attn_rout_w, L0_attn_rout_b, L0_attn_out_w, L0_attn_out_b, L0_attn_gl_w, L0_attn_gr_w, L0_xattn_Wq, L0_xattn_bq, L0_xattn_Wk, L0_xattn_bk, L0_xattn_Wv, L0_xattn_bv, L0_xattn_gamma, L0_xattn_beta, L0_ffn_slot_init, L0_ffn_slot_scale, L0_ffn_w1, L0_ffn_b1, L0_ffn_w2, L0_ffn_b2, L0_ffn_gru_wih, L0_ffn_gru_whh, L0_ffn_gru_bih, L0_ffn_gru_bhh, L0_ffn_wv, L0_ffn_bv, L0_ffn_wo, L0_ffn_bo, L0_ffn_tau):
    import jax
    import jax.numpy as jnp

    def _L0_attn_ref(x, qkv_w, qkv_b, rq_w, rq_b, rkv_w, rkv_b, rout_w, rout_b, out_w, out_b, gl_w, gr_w):
        import jax, jax.numpy as jnp
        import numpy as np
        D_MODEL = 256
        N_HEADS = 16
        HEAD_DIM = D_MODEL // N_HEADS
        WINDOW = 128
        LOCAL_BLOCK = 64
        LATENT_TOKENS = 64
        LATENT_D = 64
        LATENT_HEADS = 4
        LATENT_HD = LATENT_D // LATENT_HEADS
        NEG = -1000000000.0

        def _local_attention(q, k, v):
            B, H, S, hd = q.shape
            bs = min(S, max(WINDOW, LOCAL_BLOCK))
            nb = S // bs
            w = WINDOW
            L = bs + w - 1
            k_pad = jnp.pad(k, ((0, 0), (0, 0), (w - 1, 0), (0, 0)))
            v_pad = jnp.pad(v, ((0, 0), (0, 0), (w - 1, 0), (0, 0)))
            starts = jnp.arange(nb) * bs
            idx = starts[:, None] + jnp.arange(L)[None, :]
            kb = k_pad[:, :, idx]
            vb = v_pad[:, :, idx]
            qb = q.reshape(B, H, nb, bs, hd)
            q_pos = starts[:, None] + jnp.arange(bs)[None, :]
            k_gpos = starts[:, None] + jnp.arange(L)[None, :] - (w - 1)
            dist = q_pos[:, :, None] - k_gpos[:, None, :]
            allowed = (dist > 0) & (dist <= w) & (k_gpos[:, None, :] >= 0)
            scale = 1.0 / np.sqrt(hd)
            scores = jnp.einsum('bhnqd,bhnkd->bhnqk', qb, kb) * scale
            scores = jnp.where(allowed, scores, NEG)
            attn = jax.nn.softmax(scores, axis=-1)
            attn = jnp.where(allowed.any(-1)[None, None, :, :, None], attn, 0.0)
            out = jnp.einsum('bhnqk,bhnkd->bhnqd', attn, vb)
            return out.reshape(B, H, S, hd)
        B, S, D = x.shape
        qkv = x @ qkv_w + qkv_b
        q, k, v = jnp.split(qkv, 3, axis=-1)

        def heads(t):
            return t.reshape(B, S, N_HEADS, HEAD_DIM).transpose(0, 2, 1, 3)
        local = _local_attention(heads(q), heads(k), heads(v))
        chunk = -(-S // min(LATENT_TOKENS, S))
        nlat = S // chunk
        pooled = x.reshape(B, nlat, chunk, D).mean(axis=2)
        chunk_ids = jnp.arange(S) // chunk
        rq = (x @ rq_w + rq_b).reshape(B, S, LATENT_HEADS, LATENT_HD).transpose(0, 2, 1, 3)
        rkv = pooled @ rkv_w + rkv_b
        rk, rv = jnp.split(rkv, 2, axis=-1)
        rk = rk.reshape(B, nlat, LATENT_HEADS, LATENT_HD).transpose(0, 2, 1, 3)
        rv = rv.reshape(B, nlat, LATENT_HEADS, LATENT_HD).transpose(0, 2, 1, 3)
        lscale = 1.0 / np.sqrt(LATENT_HD)
        lscores = jnp.einsum('bhsd,bhld->bhsl', rq, rk) * lscale
        lat_allowed = jnp.arange(nlat)[None, :] < chunk_ids[:, None]
        lscores = jnp.where(lat_allowed[None, None], lscores, NEG)
        lattn = jax.nn.softmax(lscores, axis=-1)
        lattn = jnp.where(lat_allowed.any(-1)[None, None, :, None], lattn, 0.0)
        lat_out = jnp.einsum('bhsl,bhld->bhsd', lattn, rv)
        lat_out = lat_out.transpose(0, 2, 1, 3).reshape(B, S, LATENT_D)
        remote = lat_out @ rout_w + rout_b
        remote_h = remote.reshape(B, S, N_HEADS, HEAD_DIM).transpose(0, 2, 1, 3)
        gate = jax.nn.sigmoid(local @ gl_w + remote_h @ gr_w)
        mixed = gate * local + (1.0 - gate) * remote_h
        mixed = mixed.transpose(0, 2, 1, 3).reshape(B, S, D)
        return mixed @ out_w + out_b

    def _L0_xattn_ref(query, key, value, Wq, bq, Wk, bk, Wv, bv, gamma, beta):
        import jax, jax.numpy as jnp
        import numpy as np
        NUM_HEADS = 16
        EMBED = 256
        ATTN = 256
        HEAD_DIM = ATTN // NUM_HEADS
        NEG = -2.0 ** 32 + 1.0
        LN_EPS = 1e-05

        def _layer_norm(x, gamma, beta):
            mu = jnp.mean(x, axis=-1, keepdims=True)
            var = jnp.mean(jnp.square(x - mu), axis=-1, keepdims=True)
            return (x - mu) * jax.lax.rsqrt(var + LN_EPS) * gamma + beta
        B, S, _ = query.shape
        H, D = (NUM_HEADS, HEAD_DIM)
        q = jax.nn.relu(query @ Wq + bq)
        k = jax.nn.relu(key @ Wk + bk)
        v = jax.nn.relu(value @ Wv + bv)
        qh = q.reshape(B, S, H, D)
        kh = k.reshape(B, S, H, D)
        vh = v.reshape(B, S, H, D)
        scores = jnp.einsum('bqhd,bkhd->bhqk', qh, kh) / jnp.sqrt(jnp.float32(D))
        causal = jnp.tril(jnp.ones((S, S), jnp.bool_))
        scores = jnp.where(causal[None, None], scores, jnp.float32(NEG))
        probs = jax.nn.softmax(scores, axis=-1)
        out = jnp.einsum('bhqk,bkhd->bqhd', probs, vh).reshape(B, S, H * D)
        out = out + q
        return _layer_norm(out, gamma, beta)

    def _L0_ffn_ref(x, slot_init, slot_scale, w1, b1, w2, b2, gru_wih, gru_whh, gru_bih, gru_bhh, wv, bv, wo, bo, tau):
        import jax, jax.numpy as jnp
        import numpy as np
        D_MODEL = 256
        NUM_SLOTS = 64
        TOP_K = 8
        B, T = (4, 1024)

        def _forward(x, slot_init, slot_scale, w1, b1, w2, b2, gru_wih, gru_whh, gru_bih, gru_bhh, wv, bv, wo, bo, tau):
            Bn, Tn, D = x.shape
            Sn = slot_init.shape[0]
            S = jnp.broadcast_to((slot_init * slot_scale)[None], (Bn, Sn, D)).astype(x.dtype)
            slot_mean = S.mean(axis=1, keepdims=True)
            ctx = jnp.concatenate([x, jnp.broadcast_to(slot_mean, x.shape)], axis=-1)
            h = jax.nn.gelu(ctx @ w1.T + b1, approximate=False)
            route_logits = (h @ w2.T + b2) / (jnp.abs(tau) + 0.1)
            topk_vals, topk_idx = jax.lax.top_k(route_logits, TOP_K)
            topk_w = jax.nn.softmax(topk_vals, axis=-1)
            alpha = jnp.sum(topk_w[..., None] * jax.nn.one_hot(topk_idx, Sn, dtype=x.dtype), axis=-2)
            slot_input = jnp.einsum('bts,btd->bsd', alpha, x)
            slot_wsum = alpha.sum(axis=1) + 1e-08
            gi = (slot_input / slot_wsum[..., None]).reshape(Bn * Sn, D)
            hs = S.reshape(Bn * Sn, D)
            gx = gi @ gru_wih.T + gru_bih
            gh = hs @ gru_whh.T + gru_bhh
            xr, xz, xn = jnp.split(gx, 3, axis=-1)
            hr, hz, hn = jnp.split(gh, 3, axis=-1)
            r = jax.nn.sigmoid(xr + hr)
            z = jax.nn.sigmoid(xz + hz)
            n = jnp.tanh(xn + r * hn)
            h_new = (1.0 - z) * n + z * hs
            S_new = h_new.reshape(Bn, Sn, D)
            slot_values = S_new @ wv.T + bv
            out = jnp.einsum('bts,bsd->btd', alpha, slot_values)
            return out @ wo.T + bo
        return _forward(x, slot_init, slot_scale, w1, b1, w2, b2, gru_wih, gru_whh, gru_bih, gru_bhh, wv, bv, wo, bo, tau)
    x = x + _L0_attn_ref(_layernorm(x, axis=-1), L0_attn_qkv_w, L0_attn_qkv_b, L0_attn_rq_w, L0_attn_rq_b, L0_attn_rkv_w, L0_attn_rkv_b, L0_attn_rout_w, L0_attn_rout_b, L0_attn_out_w, L0_attn_out_b, L0_attn_gl_w, L0_attn_gr_w)
    x = x + _L0_xattn_ref(_layernorm(x, axis=-1), ctx_1024, ctx_1024, L0_xattn_Wq, L0_xattn_bq, L0_xattn_Wk, L0_xattn_bk, L0_xattn_Wv, L0_xattn_bv, L0_xattn_gamma, L0_xattn_beta)
    x = x + _L0_ffn_ref(_layernorm(x, axis=-1), L0_ffn_slot_init, L0_ffn_slot_scale, L0_ffn_w1, L0_ffn_b1, L0_ffn_w2, L0_ffn_b2, L0_ffn_gru_wih, L0_ffn_gru_whh, L0_ffn_gru_bih, L0_ffn_gru_bhh, L0_ffn_wv, L0_ffn_bv, L0_ffn_wo, L0_ffn_bo, L0_ffn_tau)
    return x

_drawn_inputs = setup_inputs


def setup_inputs(seed=0):
    import zlib

    import numpy as np

    out = dict(_drawn_inputs(seed))
    spreads = {'L0_attn_qkv_b': (0.0, 0.478),
     'L0_attn_rq_b': (0.0, 0.8),
     'L0_attn_rkv_b': (0.0, 0.8),
     'L0_attn_rout_b': (0.0, 0.468),
     'L0_attn_out_b': (0.0, 0.1),
     'L0_xattn_bq': (0.0, 0.1),
     'L0_xattn_bk': (0.0, 0.8),
     'L0_xattn_bv': (0.0, 0.1),
     'L0_xattn_gamma': (1.0, 0.2),
     'L0_xattn_beta': (0.0, 0.1),
     'L0_ffn_slot_scale': (1.0, 0.6),
     'L0_ffn_b1': (0.0, 0.519),
     'L0_ffn_b2': (0.0, 0.445),
     'L0_ffn_gru_bih': (0.0, 0.367),
     'L0_ffn_gru_bhh': (0.0, 0.549),
     'L0_ffn_bv': (0.0, 0.1),
     'L0_ffn_bo': (0.0, 0.1)}
    factors = {'L0_attn_qkv_w': 4.993,
     'L0_attn_rq_w': 8.0,
     'L0_attn_rkv_w': 8.0,
     'L0_attn_rout_w': 8.0,
     'L0_attn_gl_w': 8.0,
     'L0_attn_gr_w': 8.0,
     'L0_ffn_slot_init': 3.694,
     'L0_ffn_gru_whh': 8.0}
    for name, (base, spread) in spreads.items():
        noise = np.random.default_rng([zlib.crc32(name.encode()), seed]).standard_normal(out[name].shape)
        drawn = base * np.exp(spread * noise) if base else spread * noise
        out[name] = jnp.asarray(drawn.astype(out[name].dtype))
    for name, factor in factors.items():
        out[name] = (out[name] * factor).astype(out[name].dtype)
    return out
```

```python
from contextlib import ExitStack

import concourse.bass as bass
from concourse import mybir

F32 = mybir.dt.float32
BF16 = mybir.dt.bfloat16
ALU = mybir.AluOpType
ACT = mybir.ActivationFunctionType
AX = mybir.AxisListType

B, S, D = 64, 128, 256
C = D // 128
H, HD = 16, 16
LH, LAT = 4, S // 2
HW = 32
NPAIR = B // 2
PT = 2 * S
GROUPS = 8
NPROD = 6
SPLIT = NPROD * HD
STACK = SPLIT + 2
SLOTS, TOPK = 64, 8
LN_EPS = 1e-5
NEG = -1e30
MADE = 12
SCALE = float(HD) ** -0.5

Q_PART = (0, 0, 1, 1, 0, 2)
K_PART = (0, 1, 0, 1, 2, 0)


class At:

    def __init__(self, i, off):
        self.i, self.off = i, off

    @property
    def pair(self):
        return self.i * 2 + self.off

    @property
    def par(self):
        return self.off % 2

    def back(self, k=1):
        return At(self.i, self.off - k)

    def count(self, per, k):
        return self.i * (2 * per) + (self.off * per + k)

    def turn(self, per, k):
        return self.i * per + (self.off // 2 * per + k)


def wait(eng, sem, value):
    if isinstance(value, int) and value <= 0:
        return
    eng.wait_ge(sem, value)


def pairs(eng, step, last):
    step(At(0, 0))
    step(At(0, 1))
    with eng.Fori(0, NPAIR // 2 - 1) as i:
        step(At(i, 2))
        step(At(i, 3))
    for k in range(last):
        step(At(0, NPAIR + k))


def decoder(nc, a, out):
    with ExitStack() as ctx:
        def sem(name):
            return ctx.enter_context(nc.semaphore(name))

        def sb(name, shape, dt=F32):
            return ctx.enter_context(nc.sbuf_tensor(name, shape, dt))

        bank = [ctx.enter_context(nc.psum_tensor(f"bank{b}", [128, 512], F32)) for b in range(8)]
        x_sb = sb("x_sb", [128, B, D])
        ident = sb("ident", [128, 128])
        ident_bf = sb("ident_bf", [128, 128], BF16)
        with ExitStack() as scope:
            attentions(nc, scope, sem, a, bank, x_sb, ident, ident_bf)
        with ExitStack() as scope:
            slots(nc, scope, sem, a, out, bank, x_sb, ident)


def attentions(nc, scope, sem, a, bank, x_sb, ident, ident_bf):
    def sb(name, shape, dt=F32):
        return scope.enter_context(nc.sbuf_tensor(name, shape, dt))

    w_qk = [sb(f"w_qk_{p}", [128, C, 4, 128]) for p in "ab"]
    b_qk = [sb(f"b_qk_{p}", [128, 4]) for p in "ab"]
    w_v = [sb("w_v_a", [128, C, D + LH * HD]), sb("w_v_b", [128, C, D])]
    b_v = [sb("b_v_a", [128, D + LH * HD]), sb("b_v_b", [128, D])]
    w_lat = sb("w_lat", [128, C, 128])
    b_lat = sb("b_lat", [128, 1])
    w_rout = sb("w_rout", [128, D])
    b_rout = sb("b_rout", [128, D])
    w_out = sb("w_out", [128, C, D])
    b_out = sb("b_out", [128, D])
    gate_l = sb("gate_l", [128, HD])
    gate_r = sb("gate_r", [128, HD])
    gamma = sb("gamma", [128, D])
    beta = sb("beta", [128, D])
    ones_sq = sb("ones_sq", [128, 128])
    mask = [sb(f"mask_{p}", [128, 4, 128], BF16) for p in "ab"]
    mask_lat = sb("mask_lat", [128, LH, LAT], BF16)
    lat_rows = sb("lat_rows", [128, 1])

    stats = sb("stats", [128, 2, 6])
    moments = sb("moments", [128, 2, 2])
    var_eps = sb("var_eps", [128, 2])
    rstd = sb("rstd", [128, 2])
    minus_half = sb("minus_half", [128, 2])
    eps = sb("eps", [128, 2])
    xn = sb("xn", [128, 2, D])
    xn_t = sb("xn_t", [128, C, PT])
    qk_f = sb("qk_f", [128, 4, PT])
    qk_rest = sb("qk_rest", [128, 4, PT])
    qk_part = [sb(f"qk_part{i}", [128, 4, PT], BF16) for i in range(3)]
    lat_f = sb("lat_f", [128, PT])
    lat_raw = sb("lat_raw", [128, PT])
    lat_rest = sb("lat_rest", [128, PT])
    lat_part = [sb(f"lat_part{i}", [128, PT], BF16) for i in range(3)]
    q_stack = [sb(f"q_stack{i}", [128, H, PT], BF16) for i in range(2)]
    k_stack = [sb(f"k_stack{i}", [128, H, PT], BF16) for i in range(2)]
    rq_stack = [sb(f"rq_stack{i}", [128, LH, PT], BF16) for i in range(2)]
    rk_stack = [sb(f"rk_stack{i}", [128, LH, 2 * LAT], BF16) for i in range(2)]
    v_heads = [sb(f"v_heads{i}", [128, 2, H, HW]) for i in range(2)]
    rv_heads = [sb(f"rv_heads{i}", [128, 2, LH, HW]) for i in range(2)]
    neg_max = sb("neg_max", [128, 2, H])
    max_part = sb("max_part", [128, 2, 2, H], BF16)
    max_t = sb("max_t", [2 * H, PT], BF16)
    probs_t = [sb(f"probs_t{i}", [128, 4, 128]) for i in range(4)]
    av_t = [sb(f"av_t{i}", [128, 4, 128]) for i in range(2)]
    sums = sb("sums", [128, 2, H])
    inv = sb("inv", [128, 2, H])
    attn = sb("attn", [128, 2, D])
    lat_max = sb("lat_max", [128, 2, LH])
    lat_s = sb("lat_s", [128, 2, LH, LAT])
    lat_p = sb("lat_p", [128, 2, LH, LAT])
    lat_sum = sb("lat_sum", [128, 2, LH])
    lat_inv = sb("lat_inv", [128, 2, LH])
    lat_w = sb("lat_w", [128, 2, LH])
    lat_pd = sb("lat_pd", [128, 2, LH, LAT, 2])
    lat_pt = [sb(f"lat_pt{i}", [128, LH, 128]) for i in range(2)]
    lat_out = sb("lat_out", [128, PT])
    remote = sb("remote", [128, 2, D])
    remote_g = sb("remote_g", [128, 2, D])
    tmp = [sb(f"tmp{i}", [128, 2, D]) for i in range(4)]
    gate_z = sb("gate_z", [128, 2, H])
    gate_t = sb("gate_t", [128, 2, H])
    gate = sb("gate", [128, 2, H])
    mix_t = sb("mix_t", [128, 2, C, 128])
    x_bias = sb("x_bias", [128, 2, D])
    ctx_in = [x[:].rearrange("p t h l -> p t (h l)") for x in (lat_s, lat_p)]
    ctx_t, v_raw = remote_g[:], remote[:]
    q_tok = [x[:].rearrange("p (t a) n -> p t (a n)", t=2) for x in lat_pt]

    pool_turn, sp_turn = sem("pool_turn"), sem("sp_turn")
    loaded, made, made_v = sem("weights_loaded"), sem("consts_made_pool"), sem("consts_made_dve")

    with nc.Block() as block:
        loads = [
            (w_qk[0], a["attn_qk_w"]), (w_qk[1], a["xattn_qk_w"]),
            (b_qk[0], a["attn_qk_b"]), (b_qk[1], a["xattn_qk_b"]),
            (w_v[0], a["attn_v_w"]), (w_v[1], a["xattn_v_w"]),
            (w_lat, a["lat_w"]), (b_lat, a["lat_b"]), (w_out, a["attn_out_w"]),
        ]
        rows = [(b_v[0], a["attn_v_b"]), (b_v[1], a["xattn_v_b"]), (b_rout, a["attn_rout_b"]),
                (b_out, a["attn_out_b"]), (gate_l, a["attn_gl_w"]), (gate_r, a["attn_gr_w"]),
                (gamma, a["xattn_gamma"]), (beta, a["xattn_beta"])]

        @block.sync
        def _(sp):
            for tile, src in loads:
                sp.dma_start(tile[:], src).then_inc(loaded, 16)
            for tile, src in rows:
                sp.dma_start(tile[:], src.partition_broadcast(128)).then_inc(loaded, 16)
            sp.wait_ge(made_v, 1)
            for h in range(LH):
                sp.dma_start(w_rout[HW * h:HW * h + HD, :], a["attn_rout_w"][HD * h:HD * h + HD, :]).then_inc(loaded, 16)
            sp.wait_ge(loaded, 16 * (len(loads) + len(rows) + LH))

        @block.vector
        def _(dve):
            nc.vector.memset(w_rout[:], 0.0).then_inc(made_v, 1)
            for t in range(2):
                nc.vector.memset(v_heads[t][:], 0.0).then_inc(made_v, 1)
                nc.vector.memset(rv_heads[t][:], 0.0).then_inc(made_v, 1)
            nc.vector.memset(lat_rows[:], 0.5).then_inc(made_v, 1)
            nc.vector.memset(lat_f[:], 0.0).then_inc(made_v, 1)
            dve.wait_ge(made_v, 7)
            for t in range(2):
                nc.vector.memset(k_stack[t][SPLIT:STACK, :, :], 1.0).then_inc(made_v, 1)
                nc.vector.memset(v_heads[t][:, :, :, HD:HD + 1], 1.0).then_inc(made_v, 1)
            nc.vector.memset(lat_rows[0:2, :], 0.0).then_inc(made_v, 1)
            dve.wait_ge(made_v, 12)

        @block.gpsimd
        def _(pool):
            nc.gpsimd.memset(minus_half[:], -0.5)
            nc.gpsimd.memset(ones_sq[:], 1.0).then_inc(made, 1)
            nc.gpsimd.memset(mask[0][:], 0.0).then_inc(made, 1)
            nc.gpsimd.memset(mask[1][:], 0.0).then_inc(made, 1)
            nc.gpsimd.memset(mask_lat[:], 0.0).then_inc(made, 1)
            nc.gpsimd.memset(eps[:], LN_EPS).then_inc(made, 1)
            pool.wait_ge(made, 5)
            nc.gpsimd.affine_select(out=ident[:], in_=ones_sq[:], pattern=[[-1, 128]], compare_op=ALU.is_equal,
                                    fill=0.0, base=0, channel_multiplier=1).then_inc(made, 1)
            nc.gpsimd.affine_select(out=mask[0][:], in_=mask[0][:], pattern=[[0, 4], [-1, 128]], compare_op=ALU.is_ge,
                                    fill=NEG, base=-1, channel_multiplier=1).then_inc(made, 1)
            nc.gpsimd.affine_select(out=mask[1][:], in_=mask[1][:], pattern=[[0, 4], [-1, 128]], compare_op=ALU.is_ge,
                                    fill=NEG, base=0, channel_multiplier=1).then_inc(made, 1)
            nc.gpsimd.affine_select(out=mask_lat[:], in_=mask_lat[:], pattern=[[0, LH], [-2, LAT]], compare_op=ALU.is_ge,
                                    fill=NEG, base=-2, channel_multiplier=1).then_inc(made, 1)
            pool.wait_ge(made, 9)
            nc.gpsimd.memset(mask[0][0:1, :, 0:1], 0.0).then_inc(made, 1)
            nc.gpsimd.memset(mask_lat[0:2, :, 0:1], 0.0).then_inc(made, 1)
            nc.gpsimd.tensor_copy(ident_bf[:], ident[:]).then_inc(made, 1)
            pool.wait_ge(made, MADE)

    attn_phase(nc, sem, locals(), local=True)
    attn_phase(nc, sem, locals(), local=False)


def attn_phase(nc, sem, t, local):
    ph = 0 if local else 1
    P = "ab"[ph]
    a, bank, x_sb, ident, ident_bf = t["a"], t["bank"], t["x_sb"], t["ident"], t["ident_bf"]
    var_eps, minus_half, eps, pool_turn, sp_turn = (
        t[k] for k in ("var_eps", "minus_half", "eps", "pool_turn", "sp_turn"))
    (ctx_in, stats, moments, rstd, xn, xn_t, ctx_t, qk_f, qk_rest, qk_part, lat_f, lat_raw, lat_rest, lat_part) = (
        t[k] for k in ("ctx_in", "stats", "moments", "rstd", "xn", "xn_t", "ctx_t", "qk_f", "qk_rest", "qk_part",
                       "lat_f", "lat_raw", "lat_rest", "lat_part"))
    (q_stack, k_stack, rq_stack, rk_stack, v_heads, rv_heads, v_raw, neg_max, max_part, max_t, probs_t, av_t) = (
        t[k] for k in ("q_stack", "k_stack", "rq_stack", "rk_stack", "v_heads", "rv_heads", "v_raw", "neg_max",
                       "max_part", "max_t", "probs_t", "av_t"))
    (sums, inv, attn, lat_max, lat_s, lat_p, lat_sum, lat_inv, lat_w, lat_pd, lat_pt, lat_out, remote, remote_g) = (
        t[k] for k in ("sums", "inv", "attn", "lat_max", "lat_s", "lat_p", "lat_sum", "lat_inv", "lat_w", "lat_pd",
                       "lat_pt", "lat_out", "remote", "remote_g"))
    (tmp, gate_z, gate_t, gate, mix_t, x_bias, q_tok, gate_l, gate_r, lat_rows) = (
        t[k] for k in ("tmp", "gate_z", "gate_t", "gate", "mix_t", "x_bias", "q_tok", "gate_l", "gate_r", "lat_rows"))
    w_qk, b_qk, w_v, b_v, mask = (t[k][ph] for k in ("w_qk", "b_qk", "w_v", "b_v", "mask"))
    w_lat, b_lat, w_rout, b_rout, w_out, b_out, gamma, beta, mask_lat = (
        t[k] for k in ("w_lat", "b_lat", "w_rout", "b_rout", "w_out", "b_out", "gamma", "beta", "mask_lat"))

    tr_bank, proj_bank, score_bank, av_bank, back_bank, out_bank = (
        bank[0], bank[1:3], bank[3:5], bank[5], bank[6], bank[7])

    only_local = """lat_filled lat_evac lat_ready ls_filled lmax_done lsub_done lexp_done lsum_step lp_ready
        lpT_filled lpT_ready lo_filled lo_ready remote_filled remote_ready remote_gated z_in z_ready tanh_ready
        gate_ready mixed mixT_filled mixT_ready out_filled xb_ready""".split()
    only_context = "ctxT_filled ctxT_ready v_relu qT_filled qT_ready sum_ready norm_ready norm_step norm_eps norm_scaled".split()

    def s(name):
        return None if name in (only_context if local else only_local) else sem(f"{P}_{name}")

    x_loaded = [s(f"x_loaded{i}") for i in range(2)]
    ln_step, xn_ready = s("ln_step"), s("xn_ready")
    ln_eps, ln_scaled = s("ln_eps"), s("ln_scaled")
    norm_eps, norm_scaled = s("norm_eps"), s("norm_scaled")
    xnT_filled, xnT_ready = s("xnT_filled"), s("xnT_ready")
    ctxT_filled, ctxT_ready = s("ctxT_filled"), s("ctxT_ready")
    q_filled, k_filled, q_ready, k_ready = s("q_filled"), s("k_filled"), s("q_ready"), s("k_ready")
    lat_filled, lat_evac, lat_ready = s("lat_filled"), s("lat_evac"), s("lat_ready")
    v_filled, v_ready, v_relu = s("v_filled"), s("v_ready"), s("v_relu")
    part_h, part_r, part_m, part_l = s("part_h"), s("part_r"), s("part_m"), s("part_l")
    stacked = [s(f"stacked{i}") for i in range(2)]
    max_stacked = [s(f"max_stacked{i}") for i in range(2)]
    sc_filled, max_done = s("sc_filled"), s("max_done")
    max_step = s("max_step")
    maxT_filled, maxT_ready = s("maxT_filled"), s("maxT_ready")
    sct_filled, exp_done, masked = s("sct_filled"), s("exp_done"), s("masked")
    av_filled, av_ready = s("av_filled"), s("av_ready")
    back_filled, sum_step, attn_ready = s("back_filled"), s("sum_step"), s("attn_ready")
    ls_filled, lmax_done, lsub_done, lexp_done = s("ls_filled"), s("lmax_done"), s("lsub_done"), s("lexp_done")
    lsum_step, lp_ready = s("lsum_step"), s("lp_ready")
    lpT_filled, lpT_ready, lo_filled, lo_ready = s("lpT_filled"), s("lpT_ready"), s("lo_filled"), s("lo_ready")
    remote_filled, remote_ready, remote_gated = s("remote_filled"), s("remote_ready"), s("remote_gated")
    mix_step, z_in, z_ready, tanh_ready, gate_ready = (
        s("mix_step"), s("z_in"), s("z_ready"), s("tanh_ready"), s("gate_ready"))
    mixed, mixT_filled, mixT_ready = s("mixed"), s("mixT_filled"), s("mixT_ready")
    out_filled, xb_ready, x_done = s("out_filled"), s("xb_ready"), s("x_done")
    qT_filled, qT_ready = s("qT_filled"), s("qT_ready")
    sum_ready, norm_ready, norm_step = s("sum_ready"), s("norm_ready"), s("norm_step")

    nparts = 3 if local else 2
    STACKED = 16 * NPROD * (4 if local else 2)

    source = (a["x"] if local else a["ctx"]).rearrange("s p d -> p s d")

    with nc.Block() as block:

        @block.sync
        def _(sp):
            def load(at):
                if local:
                    dst = x_sb[:, bass.ds(at.i * 4 + 2 * at.off, 2), :]
                else:
                    wait(sp, ctxT_filled, at.count(1, -1))
                    dst = ctx_in[at.par]
                wait(sp, x_loaded[at.par], at.turn(16, 0))
                sp.dma_start(dst, source[:, bass.ds(at.i * 4 + 2 * at.off, 2), :]).then_inc(x_loaded[at.par], 16)

            def step(at):
                p = at.par
                wait(sp, av_filled, at.count(GROUPS, -GROUPS))
                if at.off >= 2:
                    sp.sem_inc(sp_turn, 1)
                which = ["q", "k"] + (["lat"] if local else [])
                for part, ready in ((0, part_h), (1, part_m), (2, part_l)):
                    for n, what in enumerate(which):
                        wait(sp, ready, at.count(nparts, n + 1))
                        for j in range(NPROD):
                            rows = slice(HD * j, HD * j + HD)
                            if what == "q" and Q_PART[j] == part:
                                sp.dma_start(q_stack[p][rows, :, :], qk_part[part][:, 0:2, :]).then_inc(stacked[p], 16)
                            if what == "k" and K_PART[j] == part:
                                sp.dma_start(k_stack[p][rows, :, :], qk_part[part][:, 2:4, :]).then_inc(stacked[p], 16)
                            if what == "lat" and Q_PART[j] == part:
                                sp.dma_start(rq_stack[p][rows, :, :], lat_part[part][0:64, :]).then_inc(stacked[p], 16)
                            if what == "lat" and K_PART[j] == part:
                                sp.dma_start(rk_stack[p][rows, :, :],
                                             lat_part[part][64:128, 0:2 * LAT]).then_inc(stacked[p], 16)
                wait(sp, maxT_ready, at.count(1, 1))
                sp.dma_start(q_stack[p][SPLIT:STACK, :, :], max_t[:]).then_inc(max_stacked[p], 16)

            load(At(0, 0))
            load(At(0, 1))

            load(At(0, 2))
            step(At(0, 0))
            load(At(0, 3))
            step(At(0, 1))
            with sp.Fori(0, NPAIR // 2 - 2) as i:
                load(At(i, 4))
                step(At(i, 2))
                load(At(i, 5))
                step(At(i, 3))
            step(At(0, NPAIR - 2))
            step(At(0, NPAIR - 1))
            for p in range(2):
                sp.wait_ge(max_stacked[p], 16 * (NPAIR // 2))

        @block.tensor
        def _(pe):
            def transpose_x(at):
                pe.wait_ge(xn_ready, at.count(1, 1))
                wait(pe, maxT_ready, at.count(1, 0))
                for tt in range(2):
                    for c in range(C):
                        mm = pe.transpose(tr_bank[:, c * PT + tt * S:c * PT + tt * S + S],
                                          xn[:, tt, 128 * c:128 * c + 128], ident[:])
                mm.then_inc(xnT_filled, 1)

            def transpose_ctx(at):
                pe.wait_ge(x_loaded[at.par], at.turn(16, 16))
                wait(pe, ctxT_ready, at.count(1, 0))
                for tt in range(2):
                    for c in range(C):
                        mm = pe.transpose(out_bank[:, c * PT + tt * S:c * PT + tt * S + S],
                                          ctx_in[at.par][:, tt, 128 * c:128 * c + 128], ident[:])
                mm.then_inc(ctxT_filled, 1)

            def project(dst, w, src, filled):
                for c in range(C):
                    mm = pe.matmul(dst, w(c), src[:, c, :], start=(c == 0), stop=(c == C - 1))
                return mm

            def project_q(at):
                pe.wait_ge(xnT_ready, at.count(1, 1))
                wait(pe, v_ready, at.count(2, 0))
                for g in range(2):
                    mm = project(proj_bank[0][:, g * PT:g * PT + PT], lambda c: w_qk[:, c, g, :], xn_t, None)
                mm.then_inc(q_filled, 1)

            def project_k(at):
                if not local:
                    pe.wait_ge(ctxT_ready, at.count(1, 1))
                wait(pe, v_ready, at.count(2, -1))
                for g in range(2):
                    mm = project(proj_bank[1][:, g * PT:g * PT + PT], lambda c: w_qk[:, c, 2 + g, :],
                                 xn_t if local else ctx_t, None)
                mm.then_inc(k_filled, 1)

            def project_lat(at):
                pe.wait_ge(q_ready, at.count(1, 1))
                project(proj_bank[0][:, 0:PT], lambda c: w_lat[:, c, :], xn_t, None).then_inc(lat_filled, 1)

            def project_v(at, tt):
                if tt == 0:
                    pe.wait_ge(k_ready, at.count(1, 1))
                elif local:
                    pe.wait_ge(lat_evac, at.count(1, 1))
                else:
                    pe.wait_ge(q_ready, at.count(1, 1))
                n = w_v.shape[2]
                src = xn_t if local else ctx_t
                for c in range(C):
                    mm = pe.matmul(proj_bank[1 - tt][:, 0:n], src[:, c, S * tt:S * tt + S], w_v[:, c, :],
                                   start=(c == 0), stop=(c == C - 1))
                mm.then_inc(v_filled, 1)

            def transpose_q(at):
                pe.wait_ge(q_ready, at.count(1, 1))
                wait(pe, attn_ready, at.count(2, -2))
                for tt in range(2):
                    for g in range(2):
                        mm = pe.transpose(back_bank[:, 256 * tt + 128 * g:256 * tt + 128 * g + 128],
                                          qk_f[:, g, S * tt:S * tt + S], ident[:])
                mm.then_inc(qT_filled, 1)

            def scores(at, g):
                tt, h0, dst = g // 4, 4 * (g % 4), score_bank[g % 2]
                if g >= 2:
                    pe.wait_ge(max_done, at.count(GROUPS, g - 1))
                else:
                    wait(pe, exp_done, at.count(GROUPS, 0))
                if g == 0:
                    pe.wait_ge(stacked[at.par], at.turn(STACKED, STACKED))
                pe.matmul(dst[:], ident_bf[:], mask[:].rearrange("p j k -> p (j k)"), start=True, stop=False, skip_group_check=True)
                for j in range(4):
                    mm = pe.matmul(dst[:, 128 * j:128 * j + 128], q_stack[at.par][0:SPLIT, h0 + j, S * tt:S * tt + S],
                                   k_stack[at.par][0:SPLIT, h0 + j, S * tt:S * tt + S],
                                   start=False, stop=(j == 3), skip_group_check=True)
                mm.then_inc(sc_filled, 1)

            def max_transpose(at):
                pe.wait_ge(max_step, at.count(2, 2))
                pe.wait_ge(xnT_ready, at.count(1, 1))
                dst = tr_bank[:].bitcast(BF16)
                for tt in range(2):
                    mm = pe.transpose(dst[0:2 * H, S * tt:S * tt + S],
                                      max_part[:, tt, :, :].rearrange("p a h -> p (a h)"), ident_bf[:])
                mm.then_inc(maxT_filled, 1)

            def lat_scores(at, tt):
                dst = score_bank[tt]
                pe.wait_ge(max_done, at.count(GROUPS, 7 + tt))
                pe.matmul(dst[:, 0:LH * LAT], ident_bf[:], mask_lat[:].rearrange("p h l -> p (h l)"), start=True, stop=False, skip_group_check=True)
                for h in range(LH):
                    mm = pe.matmul(dst[:, LAT * h:LAT * h + LAT], rq_stack[at.par][0:SPLIT, h, S * tt:S * tt + S],
                                   rk_stack[at.par][0:SPLIT, h, LAT * tt:LAT * tt + LAT],
                                   start=False, stop=(h == LH - 1), skip_group_check=True)
                mm.then_inc(ls_filled, 1)

            def lat_transpose(at, tt):
                if tt == 0:
                    pe.wait_ge(lp_ready, at.count(1, 1))
                    wait(pe, x_done, at.count(1, 0))
                else:
                    pe.wait_ge(lpT_ready, at.count(2, 1))
                for h in range(LH):
                    mm = pe.transpose(out_bank[:, 128 * h:128 * h + 128],
                                      lat_pd_view(tt, h), ident[:])
                mm.then_inc(lpT_filled, 1)

            def lat_pd_view(tt, h):
                return lat_pd[:, tt, h, :, :].rearrange("p l r -> p (l r)")

            def lat_values(at):
                pe.wait_ge(lpT_ready, at.count(2, 2))
                pe.wait_ge(v_ready, at.count(2, 2))
                for tt in range(2):
                    for h in range(LH):
                        mm = pe.matmul(out_bank[HW * h:HW * h + HW, S * tt:S * tt + S],
                                       rv_heads[at.par][:, tt, h, :], lat_pt[tt][:, h, :], start=True, stop=True,
                                       skip_group_check=True)
                mm.then_inc(lo_filled, 1)

            def remote_out(at):
                pe.wait_ge(lo_ready, at.count(1, 1))
                for tt in range(2):
                    mm = pe.matmul(out_bank[:, D * tt:D * tt + D], lat_out[:, S * tt:S * tt + S], w_rout[:],
                                   start=True, stop=True, skip_group_check=True)
                mm.then_inc(remote_filled, 1)

            def scores_t(at, g):
                tt, h0, dst = g // 4, 4 * (g % 4), score_bank[g % 2]
                if g >= 2:
                    pe.wait_ge(exp_done, at.count(GROUPS, g - 1))
                elif local:
                    pe.wait_ge(lsub_done, at.count(2, g + 1))
                else:
                    pe.wait_ge(max_done, at.count(GROUPS, 7 + g))
                if g == 0:
                    pe.wait_ge(max_stacked[at.par], at.turn(16, 16))
                for j in range(4):
                    mm = pe.matmul(dst[:, 128 * j:128 * j + 128], k_stack[at.par][0:STACK, h0 + j, S * tt:S * tt + S],
                                   q_stack[at.par][0:STACK, h0 + j, S * tt:S * tt + S],
                                   start=True, stop=True, skip_group_check=True)
                mm.then_inc(sct_filled, 1)

            def values(at, g):
                tt, h0 = g // 4, 4 * (g % 4)
                pe.wait_ge(masked, at.count(GROUPS, g + 1))
                if g == 0:
                    pe.wait_ge(v_ready if local else v_relu, at.count(2, 2))
                if g % 4 == 0:
                    wait(pe, av_ready, at.count(2, tt))
                for j in range(4):
                    mm = pe.matmul(av_bank[HW * j:HW * j + HW, 128 * (g % 4):128 * (g % 4) + 128],
                                   v_heads[at.par][:, tt, h0 + j, :], probs_t[g % 4][:, j, :],
                                   start=True, stop=True, skip_group_check=True)
                mm.then_inc(av_filled, 1)

            def back(at, tt):
                pe.wait_ge(av_ready, at.count(2, tt + 1))
                if tt == 1:
                    pe.wait_ge(attn_ready, at.count(2, 1))
                elif local:
                    wait(pe, mixT_ready, at.count(1, 0))
                else:
                    qT = 2 if at.off + 1 < NPAIR or not isinstance(at.i, int) else 1
                    pe.wait_ge(qT_ready, at.count(1, qT))
                for g in range(4):
                    mm = pe.transpose(back_bank[:, 128 * g:128 * g + 128], av_t[tt][:, g, :], ident[:])
                mm.then_inc(back_filled, 1)

            def mix_transpose(at):
                pe.wait_ge(mixed, at.count(1, 1))
                pe.wait_ge(attn_ready, at.count(2, 2))
                for tt in range(2):
                    for c in range(C):
                        mm = pe.transpose(back_bank[:, 256 * tt + 128 * c:256 * tt + 128 * c + 128],
                                          tmp[3][:, tt, 128 * c:128 * c + 128], ident[:])
                mm.then_inc(mixT_filled, 1)

            def project_out(at):
                pe.wait_ge(mixT_ready, at.count(1, 1))
                pe.wait_ge(remote_ready, at.count(1, 1))
                for tt in range(2):
                    for c in range(C):
                        mm = pe.matmul(out_bank[:, D * tt:D * tt + D], mix_t[:, tt, c, :], w_out[:, c, :],
                                       start=(c == 0), stop=(c == C - 1), skip_group_check=True)
                mm.then_inc(out_filled, 1)

            def step(at):
                has, prev = at.off < NPAIR or not isinstance(at.i, int), at.back()
                had = at.off > 0
                if has:
                    transpose_x(at)
                if local:
                    if had:
                        lat_transpose(prev, 0)
                    if has:
                        project_q(at)
                    if had:
                        lat_transpose(prev, 1)
                    if has:
                        project_k(at)
                    if had:
                        lat_values(prev)
                    if has:
                        project_lat(at)
                    if had:
                        remote_out(prev)
                    if has:
                        project_v(at, 0)
                        project_v(at, 1)
                elif has:
                    transpose_ctx(at)
                    project_q(at)
                    project_k(at)
                    project_v(at, 0)
                    project_v(at, 1)
                    transpose_q(at)
                if had:
                    for g in range(GROUPS):
                        scores_t(prev, g)
                        if g >= 2:
                            values(prev, g - 2)
                    back(prev, 0)
                    values(prev, 6)
                    values(prev, 7)
                for g in range(GROUPS):
                    if has:
                        scores(at, g)
                    if had and g == 1:
                        back(prev, 1)
                    if had and g == 5 and local:
                        mix_transpose(prev)
                if had and local:
                    project_out(prev)
                if has:
                    max_transpose(at)
                    if local:
                        lat_scores(at, 0)
                        lat_scores(at, 1)

            pairs(pe, step, 1)

        @block.scalar
        def _(act):
            def step(at):
                has, prev = at.off < NPAIR or not isinstance(at.i, int), at.back()
                had = at.off > 0

                def copy_lat_t(tt):
                    act.wait_ge(lpT_filled, prev.count(2, tt + 1))
                    wait(act, lo_filled, prev.count(1, 0))
                    nc.scalar.activation(lat_pt[tt][:].rearrange("p h t -> p (h t)"), out_bank[:],
                                         ACT.Copy).then_inc(lpT_ready, 1)

                def evac_qk(filled, ready, g0, reread):
                    act.wait_ge(filled, at.count(1, 1))
                    reread()
                    src = proj_bank[g0 // 2]
                    for g in range(2):
                        ins = nc.scalar.activation(qk_f[:, g0 + g, :], src[:, g * PT:g * PT + PT],
                                                   ACT.Identity if local else ACT.Relu,
                                                   bias=b_qk[:, g0 + g:g0 + g + 1])
                    ins.then_inc(ready, 1)

                if has:
                    act.wait_ge(xnT_filled, at.count(1, 1))
                    wait(act, v_filled if local else q_filled, at.count(2 if local else 1, 0))
                    nc.scalar.activation(xn_t[:].rearrange("p c t -> p (c t)"), tr_bank[:],
                                         ACT.Copy).then_inc(xnT_ready, 1)
                    if not local:
                        act.wait_ge(ctxT_filled, at.count(1, 1))
                        wait(act, v_filled, at.count(2, 0))
                        nc.scalar.activation(ctx_t.rearrange("p c t -> p (c t)"), out_bank[:],
                                             ACT.Copy).then_inc(ctxT_ready, 1)
                if local and had:
                    copy_lat_t(0)
                if has:
                    def q_reread():
                        wait(act, part_r, at.count(nparts, -nparts + 1))
                        if not local:
                            wait(act, qT_filled, at.count(1, 0))
                    evac_qk(q_filled, q_ready, 0, q_reread)
                if local and had:
                    copy_lat_t(1)
                if has:
                    evac_qk(k_filled, k_ready, 2, lambda: wait(act, part_r, at.count(nparts, -nparts + 2)))
                if local and had:
                    act.wait_ge(lo_filled, prev.count(1, 1))
                    wait(act, remote_filled, prev.count(1, 0))
                    nc.scalar.activation(lat_out[:], out_bank[:, 0:PT], ACT.Copy).then_inc(lo_ready, 1)
                if local and has:
                    act.wait_ge(lat_filled, at.count(1, 1))
                    wait(act, part_r, at.count(3, 0))
                    nc.scalar.activation(lat_f[0:64, :], proj_bank[0][0:64, 0:PT], ACT.Identity, bias=b_lat[0:64, :])
                    nc.scalar.activation(lat_raw[64:128, :], proj_bank[0][64:128, 0:PT], ACT.Identity,
                                         bias=b_lat[64:128, :]).then_inc(lat_evac, 1)
                if not local and has:
                    act.wait_ge(qT_filled, at.count(1, 1))
                    wait(act, sum_ready, at.count(1, -1))
                    for tt in range(2):
                        ins = nc.scalar.activation(
                            q_tok[at.par][:, tt, :].rearrange("p (hh g r) -> p g r hh", g=2, r=HD),
                            back_bank[:, 256 * tt:256 * tt + 256].rearrange("p (g r hh) -> p g r hh", g=2, r=HD),
                            ACT.Copy)
                    ins.then_inc(qT_ready, 1)

                def evac_av(tt):
                    act.wait_ge(av_filled, prev.count(GROUPS, 4 * tt + 4))
                    wait(act, back_filled, prev.count(2, tt - 1))
                    nc.scalar.activation(av_t[tt][:].rearrange("p g t -> p (g t)"), av_bank[:],
                                         ACT.Copy).then_inc(av_ready, 1)

                if had:
                    for g in range(GROUPS):
                        act.wait_ge(sct_filled, prev.count(GROUPS, g + 1))
                        wait(act, av_filled, prev.count(GROUPS, g - 3))
                        nc.scalar.activation(probs_t[g % 4][:].rearrange("p j t -> p (j t)"), score_bank[g % 2][:],
                                             ACT.Exp, scale=SCALE).then_inc(exp_done, 1)
                        if g == 5:
                            evac_av(0)
                    evac_av(1)
                    if local:
                        act.wait_ge(z_ready, prev.count(1, 1))
                        wait(act, gate_ready, prev.count(1, 0))
                        nc.scalar.activation(gate_t[:], gate_z[:], ACT.Tanh, scale=0.5).then_inc(tanh_ready, 1)
                        act.wait_ge(mixT_filled, prev.count(1, 1))
                        wait(act, out_filled, prev.count(1, 0))
                        nc.scalar.activation(mix_t[:].rearrange("p t c n -> p (t c n)"), back_bank[:],
                                             ACT.Copy).then_inc(mixT_ready, 1)
                if has:
                    act.wait_ge(maxT_filled, at.count(1, 1))
                    if at.par == 0:
                        wait(act, max_stacked[1], at.back().turn(16, 16))
                    else:
                        wait(act, max_stacked[0], at.back().turn(16, 16))
                    nc.scalar.activation(max_t[:], tr_bank[:].bitcast(BF16)[0:2 * H, 0:PT],
                                         ACT.Copy).then_inc(maxT_ready, 1)
                    if local:
                        act.wait_ge(lsub_done, at.count(2, 2))
                        wait(act, lp_ready, at.count(1, 0))
                        nc.scalar.activation(lat_p[:].rearrange("p t h l -> p (t h l)"),
                                             lat_s[:].rearrange("p t h l -> p (t h l)"),
                                             ACT.Exp, scale=0.5 * SCALE).then_inc(lexp_done, 1)

            pairs(act, step, 1)

        @block.vector
        def _(dve):
            def x_rows(at, tt):
                return x_sb[:, bass.ds(at.i * 4 + 2 * at.off + tt, 1), :].rearrange("p s d -> p (s d)")

            def x_pair(at):
                return x_sb[:, bass.ds(at.i * 4 + 2 * at.off, 2), :]

            def norm_stats(src, step):
                for tt in range(2):
                    ins = nc.vector.bn_stats(stats[:, tt, :], src(tt))
                ins.then_inc(step, 1)

            def norm_moments(step):
                for tt in range(2):
                    ins = nc.vector.bn_aggr(moments[:, tt, :], stats[:, tt, :])
                ins.then_inc(step, 1)

            def norm_scale(src, dst, done):
                for tt in range(2):
                    ins = nc.vector.tensor_scalar(dst[:, tt, :], src(tt), moments[:, tt, 0:1], rstd[:, tt:tt + 1],
                                                  ALU.subtract, ALU.mult)
                ins.then_inc(done, 1)

            def x_stats(at):
                if local:
                    dve.wait_ge(x_loaded[at.par], at.turn(16, 16))
                norm_stats(lambda tt: x_rows(at, tt), ln_step)

            def x_scale(at):
                dve.wait_ge(ln_scaled, at.count(1, 1))
                wait(dve, xnT_filled, at.count(1, 0))
                norm_scale(lambda tt: x_rows(at, tt), xn, xn_ready)

            def split(at, n, src, rest, part):
                nc.vector.tensor_copy(part[0], src).then_inc(part_h, 1)
                dve.wait_ge(part_h, at.count(nparts, n + 1))
                wait(dve, part_l, at.count(nparts, n + 1 - nparts))
                nc.vector.tensor_tensor(rest, src, part[0], ALU.subtract).then_inc(part_r, 1)
                dve.wait_ge(part_r, at.count(nparts, n + 1))
                nc.vector.tensor_copy(part[1], rest).then_inc(part_m, 1)

            def normalise(at, tt):
                dve.wait_ge(back_filled, at.count(2, tt + 1))
                src = back_bank[:].rearrange("p (h n) -> p h n", n=HW)
                nc.vector.tensor_scalar(sums[:, tt, :], src[:, :, HD], 1e-30, None, ALU.max).then_inc(sum_step, 1)
                dve.wait_ge(sum_step, at.count(4, 2 * tt + 1))
                nc.vector.reciprocal(inv[:, tt, :], sums[:, tt, :]).then_inc(sum_step, 1)
                dve.wait_ge(sum_step, at.count(4, 2 * tt + 2))
                if local:
                    wait(dve, mixed, at.count(1, 0))
                else:
                    wait(dve, sum_ready, at.count(1, 0))
                nc.vector.tensor_tensor(attn[:, tt, :].rearrange("p (h n) -> p h n", n=HD), src[:, :, 0:HD],
                                        inv[:, tt, :].unsqueeze(2).to_broadcast([128, H, HD]),
                                        ALU.mult).then_inc(attn_ready, 1)

            def row_max(at, g):
                tt, h0 = g // 4, 4 * (g % 4)
                dve.wait_ge(sc_filled, at.count(GROUPS, g + 1))
                nc.vector.tensor_reduce(neg_max[:, tt, h0:h0 + 4],
                                        score_bank[g % 2][:].rearrange("p (j k) -> p j k", k=128), AX.X, ALU.max,
                                        negate=True).then_inc(max_done, 1)

            def max_parts(at):
                dve.wait_ge(max_done, at.count(GROUPS, GROUPS))
                wait(dve, maxT_filled, at.count(1, 0))
                nc.vector.tensor_copy(max_part[:, :, 0, :], neg_max[:]).then_inc(max_step, 1)
                dve.wait_ge(max_step, at.count(2, 1))
                nc.vector.tensor_tensor(max_part[:, :, 1, :], neg_max[:], max_part[:, :, 0, :],
                                        ALU.subtract).then_inc(max_step, 1)

            def step(at):
                has, prev = at.off < NPAIR or not isinstance(at.i, int), at.back()
                had = at.off > 0
                if has:
                    wait(dve, stacked[1 - at.par], at.back().turn(STACKED, STACKED))
                    dve.wait_ge(q_ready, at.count(1, 1))
                    split(at, 0, qk_f[:, 0:2, :], qk_rest[:, 0:2, :], [p[:, 0:2, :] for p in qk_part])
                    dve.wait_ge(k_ready, at.count(1, 1))
                    split(at, 1, qk_f[:, 2:4, :], qk_rest[:, 2:4, :], [p[:, 2:4, :] for p in qk_part])
                    if local:
                        dve.wait_ge(lat_evac, at.count(1, 1))
                        two = lat_raw[64:128, :].rearrange("p (l r) -> p l r", r=2)
                        nc.vector.tensor_tensor(lat_f[64:128, 0:2 * LAT], two[:, :, 0], two[:, :, 1],
                                                ALU.add).then_inc(lat_ready, 1)
                        dve.wait_ge(lat_ready, at.count(1, 1))
                        split(at, 2, lat_f[:], lat_rest[:], [p[:] for p in lat_part])
                if local and had:
                    dve.wait_ge(remote_filled, prev.count(1, 1))
                    wait(dve, mixed, prev.count(1, 0))
                    nc.vector.tensor_tensor(remote[:], out_bank[:].rearrange("p (t d) -> p t d", t=2),
                                            b_rout[:].unsqueeze(1).to_broadcast([128, 2, D]),
                                            ALU.add).then_inc(remote_ready, 1)
                after = None
                if has and not (isinstance(at.i, int) and at.off == NPAIR - 1):
                    after = At(at.i, at.off + 1)
                    x_stats(after)
                if has:
                    if after:
                        dve.wait_ge(ln_step, after.count(2, 1))
                    wait(dve, av_filled if local else v_relu, at.count(GROUPS, -GROUPS) if local else at.count(2, 0))
                    for tt in range(2):
                        src = proj_bank[1 - tt]
                        dve.wait_ge(v_filled, at.count(2, tt + 1))
                        if local:
                            nc.vector.tensor_tensor(v_heads[at.par][:, tt, :, 0:HD],
                                                    src[:, 0:D].rearrange("p (h n) -> p h n", n=HD),
                                                    b_v[:, 0:D].rearrange("p (h n) -> p h n", n=HD), ALU.add)
                            nc.vector.tensor_tensor(rv_heads[at.par][:, tt, :, 0:HD],
                                                    src[:, D:].rearrange("p (h n) -> p h n", n=HD)[:, 0:LH, :],
                                                    b_v[:, D:].rearrange("p (h n) -> p h n", n=HD),
                                                    ALU.add).then_inc(v_ready, 1)
                        else:
                            nc.vector.tensor_tensor(v_raw[:, tt, :], src[:, 0:D], b_v[:], ALU.add).then_inc(v_ready, 1)
                        if tt == 0 and after:
                            norm_moments(ln_step)
                if after:
                    x_scale(after)
                if had:
                    normalise(prev, 0)
                for g in range(GROUPS):
                    if had and not local and g == 4:
                        dve.wait_ge(norm_step, prev.count(2, 1))
                    if has:
                        row_max(at, g)
                    if had and g == 1:
                        normalise(prev, 1)
                    if had and not local and g == 3:
                        dve.wait_ge(sum_ready, prev.count(1, 1))
                        norm_stats(lambda tt: tmp[0][:, tt, :], norm_step)
                    if had and not local and g == 4:
                        norm_moments(norm_step)
                    if had and not local and g == 6:
                        dve.wait_ge(norm_scaled, prev.count(1, 1))
                        wait(dve, x_done, prev.count(1, 0))
                        norm_scale(lambda tt: tmp[0][:, tt, :], tmp[1], norm_ready)
                    if had and local and g == 3:
                        dve.wait_ge(z_in, prev.count(1, 1))
                        wait(dve, tanh_ready, prev.count(1, 0))
                        nc.vector.tensor_reduce(gate_z[:].rearrange("p t h -> p (t h)"),
                                                tmp[1][:].rearrange("p t (h n) -> p (t h) n", n=HD), AX.X,
                                                ALU.add).then_inc(z_ready, 1)
                    if had and local and g == 4:
                        dve.wait_ge(tanh_ready, prev.count(1, 1))
                        wait(dve, mixed, prev.count(1, 0))
                        nc.vector.tensor_scalar(gate[:], gate_t[:], 0.5, 0.5, ALU.mult, ALU.add).then_inc(gate_ready, 1)
                if has:
                    max_parts(at)
                if local and had:
                    dve.wait_ge(out_filled, prev.count(1, 1))
                    dve.wait_ge(xb_ready, prev.count(1, 1))
                    nc.vector.tensor_tensor(x_pair(prev), out_bank[:].rearrange("p (t d) -> p t d", t=2), x_bias[:],
                                            ALU.add).then_inc(x_done, 1)
                if local and has:
                    for tt in range(2):
                        src = score_bank[tt][:, 0:LH * LAT].rearrange("p (h l) -> p h l", l=LAT)
                        dve.wait_ge(ls_filled, at.count(2, tt + 1))
                        nc.vector.tensor_reduce(lat_max[:, tt, :], src, AX.X, ALU.max).then_inc(lmax_done, 1)
                        dve.wait_ge(lmax_done, at.count(2, tt + 1))
                        wait(dve, lexp_done, at.count(1, 0))
                        nc.vector.tensor_tensor(lat_s[:, tt, :, :], src,
                                                lat_max[:, tt, :].unsqueeze(2).to_broadcast([128, LH, LAT]),
                                                ALU.subtract).then_inc(lsub_done, 1)
                    dve.wait_ge(lexp_done, at.count(1, 1))
                    nc.vector.tensor_reduce(lat_sum[:].rearrange("p t h -> p (t h)"),
                                            lat_p[:].rearrange("p t h l -> p (t h) l"), AX.X,
                                            ALU.add).then_inc(lsum_step, 1)
                    dve.wait_ge(lsum_step, at.count(3, 1))
                    nc.vector.reciprocal(lat_inv[:], lat_sum[:]).then_inc(lsum_step, 1)
                    dve.wait_ge(lsum_step, at.count(3, 2))
                    wait(dve, lp_ready, at.count(1, 0))
                    nc.vector.tensor_scalar(lat_w[:], lat_inv[:], lat_rows[:, 0:1], None, ALU.mult).then_inc(lsum_step, 1)

            x_stats(At(0, 0))
            dve.wait_ge(ln_step, 1)
            norm_moments(ln_step)
            x_scale(At(0, 0))
            step(At(0, 0))
            step(At(0, 1))
            with dve.Fori(0, NPAIR // 2 - 2) as i:
                step(At(i, 2))
                step(At(i, 3))
            step(At(0, NPAIR - 2))
            step(At(0, NPAIR - 1))
            step(At(0, NPAIR))

        @block.gpsimd
        def _(pool):
            def x_pair(at):
                return x_sb[:, bass.ds(at.i * 4 + 2 * at.off, 2), :]

            def one_over_deviation(at, step, with_eps, scaled):
                pool.wait_ge(step, at.count(2, 2))
                nc.gpsimd.tensor_tensor(var_eps[:], moments[:, :, 1], eps[:], ALU.add).then_inc(with_eps, 1)
                pool.wait_ge(with_eps, at.count(1, 1))
                nc.gpsimd.tensor_tensor(rstd[:], var_eps[:], minus_half[:], ALU.pow).then_inc(scaled, 1)

            def step(at):
                has, prev = at.off < NPAIR or not isinstance(at.i, int), at.back()
                had = at.off > 0
                if has:
                    parts = [(qk_rest[:, 0:2, :], [p[:, 0:2, :] for p in qk_part]),
                             (qk_rest[:, 2:4, :], [p[:, 2:4, :] for p in qk_part])]
                    if local:
                        parts.append((lat_rest[:], [p[:] for p in lat_part]))
                    for n, (rest, part) in enumerate(parts):
                        pool.wait_ge(part_m, at.count(nparts, n + 1))
                        nc.gpsimd.tensor_tensor(part[2], rest, part[1], ALU.subtract).then_inc(part_l, 1)
                if not local and has:
                    wait(pool, av_filled, at.count(GROUPS, -GROUPS))
                    for tt in range(2):
                        pool.wait_ge(v_ready, at.count(2, tt + 1))
                        pool.sem_inc(pool_turn, 1)
                        nc.gpsimd.tensor_scalar(v_heads[at.par][:, tt, :, 0:HD],
                                                v_raw[:, tt, :].rearrange("p (h n) -> p h n", n=HD), 0.0, None,
                                                ALU.max).then_inc(v_relu, 1)
                if local and had:
                    pool.wait_ge(remote_ready, prev.count(1, 1))
                    nc.gpsimd.tensor_tensor(remote_g[:].rearrange("p t (h n) -> p (t h) n", n=HD),
                                            remote[:].rearrange("p t (h n) -> p (t h) n", n=HD),
                                            gate_r[:].unsqueeze(1).to_broadcast([128, 2 * H, HD]),
                                            ALU.mult).then_inc(remote_gated, 1)
                    wait(pool, x_done, prev.count(1, 0))
                    nc.gpsimd.tensor_tensor(x_bias[:], x_pair(prev), b_out[:].unsqueeze(1).to_broadcast([128, 2, D]),
                                            ALU.add).then_inc(xb_ready, 1)
                if has and not (isinstance(at.i, int) and at.off == NPAIR - 1):
                    one_over_deviation(At(at.i, at.off + 1), ln_step, ln_eps, ln_scaled)
                if had:
                    for g in range(GROUPS):
                        pool.wait_ge(exp_done, prev.count(GROUPS, g + 1))
                        pool.sem_inc(pool_turn, 1)
                        pt = probs_t[g % 4]
                        nc.gpsimd.affine_select(out=pt[:], in_=pt[:], pattern=[[0, 4], [1, 128]], compare_op=ALU.is_ge,
                                                fill=0.0, base=-1 if local else 0,
                                                channel_multiplier=-1).then_inc(masked, 1)
                    pool.wait_ge(attn_ready, prev.count(2, 2))
                    if local:
                        def heads(x):
                            return x[:].rearrange("p t (h n) -> p (t h) n", n=HD)

                        wait(pool, z_ready, prev.count(1, 0))
                        nc.gpsimd.tensor_tensor(heads(tmp[0]), heads(attn),
                                                gate_l[:].unsqueeze(1).to_broadcast([128, 2 * H, HD]),
                                                ALU.mult).then_inc(mix_step, 1)
                        pool.wait_ge(mix_step, prev.count(3, 1))
                        pool.wait_ge(remote_gated, prev.count(1, 1))
                        nc.gpsimd.tensor_tensor(tmp[1][:], tmp[0][:], remote_g[:], ALU.add).then_inc(z_in, 1)
                        nc.gpsimd.tensor_tensor(tmp[2][:], attn[:], remote[:], ALU.subtract).then_inc(mix_step, 1)
                        pool.wait_ge(mix_step, prev.count(3, 2))
                        pool.wait_ge(gate_ready, prev.count(1, 1))
                        pool.wait_ge(z_in, prev.count(1, 1))
                        nc.gpsimd.tensor_tensor(heads(tmp[0]), heads(tmp[2]),
                                                gate[:].rearrange("p t h -> p (t h)").unsqueeze(2)
                                                .to_broadcast([128, 2 * H, HD]), ALU.mult).then_inc(mix_step, 1)
                        pool.wait_ge(mix_step, prev.count(3, 3))
                        wait(pool, mixT_filled, prev.count(1, 0))
                        nc.gpsimd.tensor_tensor(tmp[3][:], tmp[0][:], remote[:], ALU.add).then_inc(mixed, 1)
                    else:
                        pool.wait_ge(qT_ready, prev.count(1, 1))
                        wait(pool, norm_ready, prev.count(1, 0))
                        nc.gpsimd.tensor_tensor(tmp[0][:], attn[:], q_tok[prev.par][:], ALU.add).then_inc(sum_ready, 1)
                        one_over_deviation(prev, norm_step, norm_eps, norm_scaled)
                        pool.wait_ge(norm_ready, prev.count(1, 1))
                        nc.gpsimd.tensor_tensor(tmp[2][:], tmp[1][:], gamma[:].unsqueeze(1).to_broadcast([128, 2, D]),
                                                ALU.mult).then_inc(mix_step, 1)
                        pool.wait_ge(mix_step, prev.count(2, 1))
                        nc.gpsimd.tensor_tensor(tmp[3][:], tmp[2][:], beta[:].unsqueeze(1).to_broadcast([128, 2, D]),
                                                ALU.add).then_inc(mix_step, 1)
                        pool.wait_ge(mix_step, prev.count(2, 2))
                        nc.gpsimd.tensor_tensor(x_pair(prev), x_pair(prev), tmp[3][:], ALU.add).then_inc(x_done, 1)
                if local and has:
                    pool.wait_ge(lsum_step, at.count(3, 3))
                    wait(pool, lpT_filled, at.count(2, 0))
                    nc.gpsimd.tensor_tensor(
                        lat_pd[:].rearrange("p t h l r -> p (t h) l r"),
                        lat_p[:].rearrange("p t h l -> p (t h) l").unsqueeze(3).to_broadcast([128, 2 * LH, LAT, 2]),
                        lat_w[:].rearrange("p t h -> p (t h)").unsqueeze(2).unsqueeze(3)
                        .to_broadcast([128, 2 * LH, LAT, 2]), ALU.mult).then_inc(lp_ready, 1)

            one_over_deviation(At(0, 0), ln_step, ln_eps, ln_scaled)
            step(At(0, 0))
            step(At(0, 1))
            with pool.Fori(0, NPAIR // 2 - 2) as i:
                step(At(i, 2))
                step(At(i, 3))
            for k in range(NPAIR - 2, NPAIR + 1):
                step(At(0, k))


def slots(nc, scope, sem, a, out, bank, x_sb, ident):
    def sb(name, shape, dt=F32):
        return scope.enter_context(nc.sbuf_tensor(name, shape, dt))

    G = 3 * D
    PS = 2 * SLOTS
    NOT_CHOSEN = -3e38
    w1 = sb("w1", [128, 2 * C, 128])
    b1 = sb("b1", [128, 1])
    w2 = sb("w2", [128, SLOTS])
    b2 = sb("b2", [128, SLOTS])
    tau = sb("tau", [128, 1])
    tau_abs = sb("tau_abs", [128, 1])
    inv_tau = sb("inv_tau", [128, 1])
    w_ih = sb("w_ih", [128, C, G])
    w_hh = sb("w_hh", [128, C, G])
    b_ih = sb("b_ih", [128, G])
    b_hh = sb("b_hh", [128, G])
    wv = sb("wv", [128, C, D])
    wo = sb("wo", [128, C, D])
    bv = sb("bv", [128, C])
    bv_cols = sb("bv_cols", [128, C, 128])
    b_o = sb("b_o", [128, D])
    slot_init = sb("slot_init", [128, D])
    slot_scale = sb("slot_scale", [128, 1])
    slot0 = sb("slot0", [128, D])
    slot0_t = sb("slot0_t", [128, C, PS])
    mean_w = sb("mean_w", [SLOTS, 1])
    slot_mean = sb("slot_mean", [128, C])
    b1_all = sb("b1_all", [128, 1])
    h_gates = sb("h_gates", [128, G])
    rz_const = sb("rz_const", [128, 2 * D])
    half_hn = sb("half_hn", [128, D])
    n_const = sb("n_const", [128, D])
    w_vo = sb("w_vo", [128, C, D])
    b_vo = sb("b_vo", [128, D])

    stats = sb("f_stats", [128, 2, 6])
    moments = sb("f_moments", [128, 2, 2])
    var_eps = sb("f_var_eps", [128, 2])
    rstd = sb("f_rstd", [128, 2])
    minus_half = sb("f_minus_half", [128, 2])
    eps = sb("f_eps", [128, 2])
    XW = D + 1
    xn = [sb(f"f_xn{i}", [128, 2, XW]) for i in range(2)]
    xn_t = sb("f_xn_t", [128, C, PT])
    h_t = sb("h_t", [128, PT])
    logits = sb("logits", [128, 2, SLOTS])
    top = sb("top", [128, 2, TOPK])
    rest = sb("rest", [128, 2, SLOTS])
    neg_top = sb("neg_top", [128, 2])
    expd = sb("expd", [128, 2, SLOTS])
    chosen = sb("chosen", [128, 2, SLOTS])
    chosen_sum = sb("chosen_sum", [128, 2])
    chosen_inv = sb("chosen_inv", [128, 2])
    alpha = [sb(f"alpha{i}", [128, 2, PS]) for i in range(2)]
    alpha_t = [sb(f"alpha_t{i}", [128, 2, 128]) for i in range(2)]
    w_sum = sb("w_sum", [128, 1])
    w_inv = sb("w_inv", [128, 1])
    gi = sb("gi", [128, D])
    gi_t = sb("gi_t", [128, C, PS])
    rz = sb("rz", [128, 2 * D])
    rz_t = sb("rz_t", [128, 2 * D])
    r_hn = sb("r_hn", [128, D])
    r_hn_c = sb("r_hn_c", [128, D])
    n_in = sb("n_in", [128, D])
    n_out = sb("n_out", [128, D])
    h_n = sb("h_n", [128, D])
    z_hn = sb("z_hn", [128, D])
    slot_new = sb("slot_new", [128, D])
    slot_new_t = sb("slot_new_t", [128, C, PS])
    slot_val = sb("slot_val", [128, D])
    x_bias = sb("f_x_bias", [128, 2, D])
    y = [sb(f"y{i}", [128, 2, D]) for i in range(2)]

    loaded = sem("f_weights_loaded")
    prep_v, prep_p = sem("f_prep_dve"), sem("f_prep_pe")

    with nc.Block() as block:
        loads = [(w1, a["ffn_w1"]), (b1, a["ffn_b1"]), (w2, a["ffn_w2"]), (w_ih, a["ffn_w_ih"]), (w_hh, a["ffn_w_hh"]),
                 (wv, a["ffn_wv"]), (wo, a["ffn_wo"]), (bv, a["ffn_bv"])]
        rows = [(b2, a["ffn_b2"]), (tau, a["ffn_tau"]), (b_ih, a["ffn_b_ih"]), (b_hh, a["ffn_b_hh"]), (b_o, a["ffn_bo"])]

        @block.sync
        def _(sp):
            for tile, src in loads:
                sp.dma_start(tile[:], src).then_inc(loaded, 16)
            for tile, src in rows:
                sp.dma_start(tile[:], src.partition_broadcast(128)).then_inc(loaded, 16)
            for k in range(2):
                half = slice(SLOTS * k, SLOTS * k + SLOTS)
                sp.dma_start(slot_init[half, :], a["ffn_slot_init"]).then_inc(loaded, 16)
                sp.dma_start(slot_scale[half, :], a["ffn_slot_scale"]).then_inc(loaded, 16)
            sp.wait_ge(loaded, 16 * (len(loads) + len(rows) + 4))

        @block.vector
        def _(dve):
            nc.vector.memset(minus_half[:], -0.5)
            nc.vector.memset(eps[:], LN_EPS)
            nc.vector.memset(mean_w[:], 1.0 / SLOTS).then_inc(prep_v, 1)
            for k in range(2):
                nc.vector.memset(alpha[k][:], 0.0).then_inc(prep_v, 1)
                nc.vector.memset(xn[k][:, :, D:XW], 1.0).then_inc(prep_v, 1)
            dve.wait_ge(loaded, 16 * (len(loads) + len(rows) + 4))
            nc.vector.tensor_scalar(slot0[:], slot_init[:], slot_scale[:, 0:1], None, ALU.mult).then_inc(prep_v, 1)
            nc.vector.tensor_copy(bv_cols[:], bv[:].unsqueeze(2).to_broadcast([128, C, 128])).then_inc(prep_v, 1)
            nc.vector.scalar_tensor_tensor(tau_abs[:], tau[:], -1.0, tau[:], ALU.mult, ALU.max).then_inc(prep_v, 1)
            dve.wait_ge(prep_v, 8)
            nc.vector.tensor_scalar(tau_abs[:], tau_abs[:], 0.1, None, ALU.add).then_inc(prep_v, 1)
            dve.wait_ge(prep_v, 9)
            nc.vector.reciprocal(inv_tau[:], tau_abs[:]).then_inc(prep_v, 1)
            dve.wait_ge(prep_v, 10)
            nc.vector.tensor_scalar(b2[:], b2[:], inv_tau[:, 0:1], None, ALU.mult).then_inc(prep_v, 1)
            dve.wait_ge(prep_p, 1)
            nc.vector.tensor_copy(slot0_t[:].rearrange("p c n -> p (c n)"), bank[0][:, 0:C * PS]).then_inc(prep_v, 1)
            dve.wait_ge(prep_p, 2)
            nc.vector.tensor_copy(slot_mean[:], bank[1][:, 0:C]).then_inc(prep_v, 1)
            dve.wait_ge(prep_p, 3)
            nc.vector.tensor_tensor(b1_all[:], bank[2][:, 0:1], b1[:], ALU.add).then_inc(prep_v, 1)
            dve.wait_ge(prep_p, 4)
            nc.vector.tensor_tensor(h_gates[:, 0:512], bank[3][:], b_hh[:, 0:512], ALU.add).then_inc(prep_v, 1)
            nc.vector.tensor_tensor(h_gates[:, 512:G], bank[4][:, 0:G - 512], b_hh[:, 512:G], ALU.add).then_inc(prep_v, 1)
            dve.wait_ge(prep_v, 16)
            nc.vector.tensor_tensor(rz_const[:], h_gates[:, 0:2 * D], b_ih[:, 0:2 * D], ALU.add).then_inc(prep_v, 1)
            nc.vector.tensor_scalar(half_hn[:], h_gates[:, 2 * D:G], 0.5, None, ALU.mult).then_inc(prep_v, 1)
            dve.wait_ge(prep_v, 18)
            nc.vector.tensor_tensor(n_const[:], half_hn[:], b_ih[:, 2 * D:G], ALU.add).then_inc(prep_v, 1)
            dve.wait_ge(prep_p, 5)
            nc.vector.tensor_copy(w_vo[:].rearrange("p c n -> p (c n)"), bank[5][:, 0:C * D]).then_inc(prep_v, 1)
            nc.vector.tensor_copy(b_vo[:], bank[6][:, 0:D]).then_inc(prep_v, 1)
            dve.wait_ge(prep_v, 21)

        @block.tensor
        def _(pe):
            pe.wait_ge(prep_v, 6)
            for c in range(C):
                mm = pe.transpose(bank[0][:, PS * c:PS * c + PS], slot0[:, 128 * c:128 * c + 128], ident[:])
            mm.then_inc(prep_p, 1)
            for c in range(C):
                mm = pe.matmul(bank[1][:, c:c + 1], slot0[0:SLOTS, 128 * c:128 * c + 128], mean_w[:],
                               start=True, stop=True, skip_group_check=True)
            mm.then_inc(prep_p, 1)
            pe.wait_ge(prep_v, 13)
            for c in range(C):
                mm = pe.matmul(bank[2][:, 0:1], w1[:, C + c, :], slot_mean[:, c:c + 1], start=(c == 0), stop=(c == C - 1))
            mm.then_inc(prep_p, 1)
            for lo, hi, b in ((0, 512, 3), (512, G, 4)):
                for c in range(C):
                    mm = pe.matmul(bank[b][:, 0:hi - lo], slot0_t[:, c, :], w_hh[:, c, lo:hi], start=(c == 0), stop=(c == C - 1))
            mm.then_inc(prep_p, 1)
            for d in range(C):
                for c in range(C):
                    pe.matmul(bank[5][:, D * d:D * d + D], wv[:, c, 128 * d:128 * d + 128], wo[:, c, :],
                              start=(c == 0), stop=(c == C - 1), skip_group_check=True)
            for c in range(C):
                mm = pe.matmul(bank[6][:, 0:D], bv_cols[:, c, :], wo[:, c, :], start=(c == 0), stop=(c == C - 1))
            mm.then_inc(prep_p, 1)

    tr_bank, hid_bank, logit_bank, in_bank, gate_bank, new_bank, out_bank = (
        bank[0], bank[1], bank[2], bank[3], bank[4:6], bank[6], bank[7])

    def s(name):
        return sem(f"f_{name}")

    ln_eps, ln_scaled = s("ln_eps"), s("ln_scaled")
    ln_step, xn_ready, xnT_filled, xnT_ready = s("ln_step"), s("xn_ready"), s("xnT_filled"), s("xnT_ready")
    hid_filled, hid_ready, logit_filled, logit_ready = s("hid_filled"), s("hid_ready"), s("logit_filled"), s("logit_ready")
    top_ready, negtop_ready, exp_ready = s("top_ready"), s("negtop_ready"), s("exp_ready")
    pick_step, alpha_ready, alphaT_filled, alphaT_ready = s("pick_step"), s("alpha_ready"), s("alphaT_filled"), s("alphaT_ready")
    in_filled, in_step, giT_filled, giT_ready = s("in_filled"), s("in_step"), s("giT_filled"), s("giT_ready")
    gate_filled, rz_ready, rz_tanh, rhn_step, rhn_ready = s("gate_filled"), s("rz_ready"), s("rz_tanh"), s("rhn_step"), s("rhn_ready")
    n_in_ready, n_ready, hn_ready, zhn_ready, slot_ready = s("n_in_ready"), s("n_ready"), s("hn_ready"), s("zhn_ready"), s("slot_ready")
    newT_filled, newT_ready, val_filled, val_ready = s("newT_filled"), s("newT_ready"), s("val_filled"), s("val_ready")
    out_filled, xb_ready, y_ready = s("out_filled"), s("xb_ready"), s("y_ready")
    stored = [s(f"stored{i}") for i in range(2)]

    dest = out.rearrange("s p d -> p s d")
    LAST = 2

    def stages(at):
        drains = isinstance(at.i, int) and at.off >= NPAIR
        route = None if drains else at
        feed = at.back() if at.off >= 1 and not (drains and at.off > NPAIR) else None
        give = at.back(2) if at.off >= 2 else None
        return route, feed, give

    with nc.Block() as block:

        @block.sync
        def _(sp):
            def step(at):
                route, feed, give = stages(at)
                if give:
                    sp.wait_ge(y_ready, give.count(1, 1))
                    sp.dma_start(dest[:, bass.ds(give.i * 4 + 2 * give.off, 2), :],
                                 y[give.par][:]).then_inc(stored[give.par], 16)

            pairs(sp, step, LAST)
            for k in range(2):
                sp.wait_ge(stored[k], 16 * (NPAIR // 2))

        @block.tensor
        def _(pe):
            def step(at):
                route, feed, give = stages(at)
                if route:
                    pe.wait_ge(xn_ready, route.count(1, 1))
                    wait(pe, xnT_ready, route.count(1, 0))
                    for tt in range(2):
                        for c in range(C):
                            mm = pe.transpose(tr_bank[:, c * PT + tt * S:c * PT + tt * S + S],
                                              xn[route.par][:, tt, 128 * c:128 * c + 128], ident[:])
                    mm.then_inc(xnT_filled, 1)
                if feed:
                    pe.wait_ge(alpha_ready, feed.count(2, 2))
                    wait(pe, giT_ready, feed.count(1, 0))
                    for tt in range(2):
                        half = slice(SLOTS * tt, SLOTS * tt + SLOTS)
                        mm = pe.matmul(in_bank[half, 0:XW], alpha[feed.par][:, tt, half], xn[feed.par][:, tt, :],
                                       start=True, stop=True, skip_group_check=True)
                    mm.then_inc(in_filled, 1)
                if give:
                    pe.wait_ge(slot_ready, give.count(1, 1))
                    wait(pe, val_ready, give.count(1, 0))
                    for c in range(C):
                        mm = pe.transpose(new_bank[:, PS * c:PS * c + PS], slot_new[:, 128 * c:128 * c + 128], ident[:])
                    mm.then_inc(newT_filled, 1)
                if route:
                    pe.wait_ge(xnT_ready, route.count(1, 1))
                    wait(pe, hid_ready, route.count(1, 0))
                    for c in range(C):
                        mm = pe.matmul(hid_bank[:, 0:PT], w1[:, c, :], xn_t[:, c, :], start=(c == 0), stop=(c == C - 1))
                    mm.then_inc(hid_filled, 1)
                if feed:
                    wait(pe, y_ready, feed.count(1, -1))
                    for tt in range(2):
                        mm = pe.transpose(out_bank[:, 128 * tt:128 * tt + 128], alpha[feed.par][:, tt, :], ident[:])
                    mm.then_inc(alphaT_filled, 1)
                    pe.wait_ge(in_step, feed.count(3, 3))
                    for c in range(C):
                        mm = pe.transpose(in_bank[:, PS * c:PS * c + PS], gi[:, 128 * c:128 * c + 128], ident[:])
                    mm.then_inc(giT_filled, 1)
                if give:
                    pe.wait_ge(newT_ready, give.count(1, 1))
                    for c in range(C):
                        mm = pe.matmul(new_bank[:, 0:D], slot_new_t[:, c, :], w_vo[:, c, :], start=(c == 0), stop=(c == C - 1))
                    mm.then_inc(val_filled, 1)
                if route:
                    pe.wait_ge(hid_ready, route.count(1, 1))
                    wait(pe, logit_ready, route.count(1, 0))
                    for tt in range(2):
                        mm = pe.matmul(logit_bank[:, SLOTS * tt:SLOTS * tt + SLOTS], h_t[:, S * tt:S * tt + S], w2[:],
                                       start=True, stop=True, skip_group_check=True)
                    mm.then_inc(logit_filled, 1)
                if feed:
                    pe.wait_ge(giT_ready, feed.count(1, 1))
                    wait(pe, n_in_ready, feed.count(1, 0))
                    for lo, hi, b in ((0, 2 * D, 0), (2 * D, G, 1)):
                        for c in range(C):
                            mm = pe.matmul(gate_bank[b][:, 0:hi - lo], gi_t[:, c, :], w_ih[:, c, lo:hi],
                                           start=(c == 0), stop=(c == C - 1))
                    mm.then_inc(gate_filled, 1)
                if give:
                    pe.wait_ge(val_ready, give.count(1, 1))
                    last = 2 if feed else 1
                    pe.wait_ge(alphaT_ready, give.count(1, last))
                    for tt in range(2):
                        mm = pe.matmul(out_bank[:, D * tt:D * tt + D], alpha_t[give.par][:, tt, :], slot_val[:],
                                       start=True, stop=True, skip_group_check=True)
                    mm.then_inc(out_filled, 1)

            pairs(pe, step, LAST)

        @block.scalar
        def _(act):
            def step(at):
                route, feed, give = stages(at)
                if route:
                    act.wait_ge(xnT_filled, route.count(1, 1))
                    wait(act, hid_filled, route.count(1, 0))
                    nc.scalar.activation(xn_t[:].rearrange("p c t -> p (c t)"), tr_bank[:], ACT.Copy).then_inc(xnT_ready, 1)
                if give:
                    act.wait_ge(newT_filled, give.count(1, 1))
                    wait(act, val_filled, give.count(1, 0))
                    nc.scalar.activation(slot_new_t[:].rearrange("p c n -> p (c n)"), new_bank[:, 0:C * PS],
                                         ACT.Copy).then_inc(newT_ready, 1)
                if route:
                    act.wait_ge(hid_filled, route.count(1, 1))
                    wait(act, logit_filled, route.count(1, 0))
                    nc.scalar.activation(h_t[:], hid_bank[:, 0:PT], ACT.Gelu, bias=b1_all[:, 0:1]).then_inc(hid_ready, 1)
                if feed:
                    act.wait_ge(alphaT_filled, feed.count(1, 1))
                    wait(act, out_filled, feed.count(1, -1))
                    nc.scalar.activation(alpha_t[feed.par][:].rearrange("p t n -> p (t n)"), out_bank[:, 0:256],
                                         ACT.Copy).then_inc(alphaT_ready, 1)
                    act.wait_ge(giT_filled, feed.count(1, 1))
                    wait(act, gate_filled, feed.count(1, 0))
                    nc.scalar.activation(gi_t[:].rearrange("p c n -> p (c n)"), in_bank[:, 0:C * PS],
                                         ACT.Copy).then_inc(giT_ready, 1)
                if route:
                    act.wait_ge(negtop_ready, route.count(1, 1))
                    wait(act, alpha_ready, route.count(2, 0))
                    for tt in range(2):
                        ins = nc.scalar.activation(expd[:, tt, :], logits[:, tt, :], ACT.Exp, bias=neg_top[:, tt:tt + 1])
                    ins.then_inc(exp_ready, 1)
                if feed:
                    act.wait_ge(rz_ready, feed.count(1, 1))
                    wait(act, slot_ready, feed.count(1, 0))
                    nc.scalar.activation(rz_t[:], rz[:], ACT.Tanh, scale=0.5).then_inc(rz_tanh, 1)
                    act.wait_ge(n_in_ready, feed.count(1, 1))
                    wait(act, slot_ready, feed.count(1, 0))
                    nc.scalar.activation(n_out[:], n_in[:], ACT.Tanh).then_inc(n_ready, 1)

            pairs(act, step, LAST)

        @block.vector
        def _(dve):
            def x_rows(at, tt):
                return x_sb[:, bass.ds(at.i * 4 + 2 * at.off + tt, 1), :].rearrange("p s d -> p (s d)")

            def norm_stats(at):
                for tt in range(2):
                    ins = nc.vector.bn_stats(stats[:, tt, :], x_rows(at, tt))
                ins.then_inc(ln_step, 1)

            def norm_moments():
                for tt in range(2):
                    ins = nc.vector.bn_aggr(moments[:, tt, :], stats[:, tt, :])
                ins.then_inc(ln_step, 1)

            def norm_scale(at):
                dve.wait_ge(ln_scaled, at.count(1, 1))
                wait(dve, in_filled, at.count(1, -1))
                for tt in range(2):
                    ins = nc.vector.tensor_scalar(xn[at.par][:, tt, 0:D], x_rows(at, tt), moments[:, tt, 0:1],
                                                  rstd[:, tt:tt + 1], ALU.subtract, ALU.mult)
                ins.then_inc(xn_ready, 1)

            def step(at):
                route, feed, give = stages(at)
                if feed:
                    dve.wait_ge(in_filled, feed.count(1, 1))
                    nc.vector.tensor_scalar(w_sum[:], in_bank[:, D:XW], 1e-8, None, ALU.add).then_inc(in_step, 1)
                    dve.wait_ge(in_step, feed.count(3, 1))
                    nc.vector.reciprocal(w_inv[:], w_sum[:]).then_inc(in_step, 1)
                    dve.wait_ge(in_step, feed.count(3, 2))
                    wait(dve, giT_filled, feed.count(1, 0))
                    nc.vector.tensor_scalar(gi[:], in_bank[:, 0:D], w_inv[:, 0:1], None, ALU.mult).then_inc(in_step, 1)
                if give:
                    dve.wait_ge(val_filled, give.count(1, 1))
                    wait(dve, out_filled, give.count(1, 0))
                    nc.vector.tensor_tensor(slot_val[:], new_bank[:, 0:D], b_vo[:], ALU.add).then_inc(val_ready, 1)
                after = None
                if route and not (isinstance(at.i, int) and at.off == NPAIR - 1):
                    after = At(at.i, at.off + 1)
                    norm_stats(after)
                    dve.wait_ge(ln_step, after.count(2, 1))
                if route:
                    dve.wait_ge(logit_filled, route.count(1, 1))
                    wait(dve, exp_ready, route.count(1, 0))
                    nc.vector.scalar_tensor_tensor(logits[:], logit_bank[:, 0:2 * SLOTS].rearrange("p (t n) -> p t n", t=2),
                                                   inv_tau[:, 0:1], b2[:].unsqueeze(1).to_broadcast([128, 2, SLOTS]),
                                                   ALU.mult, ALU.add).then_inc(logit_ready, 1)
                    if after:
                        norm_moments()
                    dve.wait_ge(logit_ready, route.count(1, 1))
                    if after:
                        norm_scale(after)
                    for tt in range(2):
                        ins = nc.vector.max(top[:, tt, :], logits[:, tt, :])
                    ins.then_inc(top_ready, 1)
                    dve.wait_ge(top_ready, route.count(1, 1))
                    nc.vector.tensor_scalar(neg_top[:], top[:, :, 0], -1.0, None, ALU.mult).then_inc(negtop_ready, 1)
                    for tt in range(2):
                        ins = nc.vector.match_replace(rest[:, tt, :], top[:, tt, :], logits[:, tt, :], NOT_CHOSEN)
                    ins.then_inc(pick_step, 1)
                    dve.wait_ge(pick_step, route.count(4, 1))
                    dve.wait_ge(exp_ready, route.count(1, 1))
                    for tt in range(2):
                        ins = nc.vector.scalar_tensor_tensor(chosen[:, tt, :], rest[:, tt, :], NOT_CHOSEN, expd[:, tt, :],
                                                             ALU.is_le, ALU.mult)
                    ins.then_inc(pick_step, 1)
                    dve.wait_ge(pick_step, route.count(4, 2))
                    nc.vector.tensor_reduce(chosen_sum[:], chosen[:], AX.X, ALU.add).then_inc(pick_step, 1)
                    dve.wait_ge(pick_step, route.count(4, 3))
                    nc.vector.reciprocal(chosen_inv[:], chosen_sum[:]).then_inc(pick_step, 1)
                    dve.wait_ge(pick_step, route.count(4, 4))
                    wait(dve, alphaT_filled, route.count(1, -1))
                    for tt in range(2):
                        nc.vector.tensor_scalar(alpha[route.par][:, tt, SLOTS * tt:SLOTS * tt + SLOTS], chosen[:, tt, :],
                                                chosen_inv[:, tt:tt + 1], None, ALU.mult).then_inc(alpha_ready, 1)
                if feed:
                    dve.wait_ge(gate_filled, feed.count(1, 1))
                    wait(dve, rz_tanh, feed.count(1, 0))
                    nc.vector.tensor_tensor(rz[:], gate_bank[0][:], rz_const[:], ALU.add).then_inc(rz_ready, 1)
                if give:
                    dve.wait_ge(out_filled, give.count(1, 1))
                    dve.wait_ge(xb_ready, give.count(1, 1))
                    wait(dve, stored[give.par], give.turn(16, 0))
                    nc.vector.tensor_tensor(y[give.par][:], out_bank[:].rearrange("p (t d) -> p t d", t=2), x_bias[:],
                                            ALU.add).then_inc(y_ready, 1)
                if feed:
                    dve.wait_ge(rhn_ready, feed.count(1, 1))
                    wait(dve, n_ready, feed.count(1, 0))
                    nc.vector.tensor_tensor(n_in[:], gate_bank[1][:, 0:D], r_hn_c[:], ALU.add).then_inc(n_in_ready, 1)
                    dve.wait_ge(hn_ready, feed.count(1, 1))
                    nc.vector.scalar_tensor_tensor(z_hn[:], rz_t[:, D:2 * D], 1.0, h_n[:], ALU.add,
                                                   ALU.mult).then_inc(zhn_ready, 1)
                    dve.wait_ge(zhn_ready, feed.count(1, 1))
                    wait(dve, newT_filled, feed.count(1, 0))
                    nc.vector.scalar_tensor_tensor(slot_new[:], z_hn[:], 0.5, n_out[:], ALU.mult,
                                                   ALU.add).then_inc(slot_ready, 1)

            norm_stats(At(0, 0))
            dve.wait_ge(ln_step, 1)
            norm_moments()
            norm_scale(At(0, 0))
            step(At(0, 0))
            step(At(0, 1))
            with dve.Fori(0, NPAIR // 2 - 2) as i:
                step(At(i, 2))
                step(At(i, 3))
            for k in range(NPAIR - 2, NPAIR + LAST):
                step(At(0, k))

        @block.gpsimd
        def _(pool):
            def one_over_deviation(at, step, with_eps, scaled):
                pool.wait_ge(step, at.count(2, 2))
                nc.gpsimd.tensor_tensor(var_eps[:], moments[:, :, 1], eps[:], ALU.add).then_inc(with_eps, 1)
                pool.wait_ge(with_eps, at.count(1, 1))
                nc.gpsimd.tensor_tensor(rstd[:], var_eps[:], minus_half[:], ALU.pow).then_inc(scaled, 1)

            def step(at):
                route, feed, give = stages(at)
                if give:
                    wait(pool, y_ready, give.count(1, 0))
                    nc.gpsimd.tensor_tensor(x_bias[:], x_sb[:, bass.ds(give.i * 4 + 2 * give.off, 2), :],
                                            b_o[:].unsqueeze(1).to_broadcast([128, 2, D]), ALU.add).then_inc(xb_ready, 1)
                if route and not (isinstance(at.i, int) and at.off == NPAIR - 1):
                    one_over_deviation(At(at.i, at.off + 1), ln_step, ln_eps, ln_scaled)
                if feed:
                    pool.wait_ge(rz_tanh, feed.count(1, 1))
                    nc.gpsimd.tensor_tensor(r_hn[:], rz_t[:, 0:D], half_hn[:], ALU.mult).then_inc(rhn_step, 1)
                    pool.wait_ge(rhn_step, feed.count(1, 1))
                    wait(pool, n_in_ready, feed.count(1, 0))
                    nc.gpsimd.tensor_tensor(r_hn_c[:], r_hn[:], n_const[:], ALU.add).then_inc(rhn_ready, 1)
                    pool.wait_ge(n_ready, feed.count(1, 1))
                    wait(pool, zhn_ready, feed.count(1, 0))
                    nc.gpsimd.tensor_tensor(h_n[:], slot0[:], n_out[:], ALU.subtract).then_inc(hn_ready, 1)

            one_over_deviation(At(0, 0), ln_step, ln_eps, ln_scaled)
            step(At(0, 0))
            step(At(0, 1))
            with pool.Fori(0, NPAIR // 2 - 2) as i:
                step(At(i, 2))
                step(At(i, 3))
            for k in range(NPAIR - 2, NPAIR + LAST):
                step(At(0, k))


def kernel(**inputs):
    import numpy as np
    import concourse.bacc as bacc
    from concourse import mybir as mb
    from concourse.bass_utils import run_bass_kernel_spmd

    given = {k: np.asarray(v) for k, v in inputs.items()}

    def attn(name):
        return given["L0_attn_" + name]

    def xattn(name):
        return given["L0_xattn_" + name]

    def ffn(name):
        return given["L0_ffn_" + name]

    def by_heads(w):
        return w.reshape(*w.shape[:-1], H // 2, 2, HD).swapaxes(-3, -2).swapaxes(-2, -1)

    def by_latent_heads(w):
        return w.reshape(*w.shape[:-1], LH, HD).swapaxes(-2, -1).reshape(*w.shape)

    def chunks(w):
        return w.reshape(w.shape[0] // 128, 128, -1).swapaxes(0, 1)

    def qk_weight(wq, wk):
        w = np.stack([by_heads(wq), by_heads(wk)], axis=1)
        return chunks(w.reshape(D, -1)).reshape(128, C, 4, 128)

    def qk_bias(bq, bk):
        return np.stack([by_heads(bq), by_heads(bk)]).reshape(4, 128).T

    w, bias, lat = attn("qkv_w"), attn("qkv_b"), LH * HD
    laid = {
        "x": given["x"], "ctx": given["ctx_1024"],
        "attn_qk_w": qk_weight(w[:, 0:D], w[:, D:2 * D]),
        "attn_qk_b": qk_bias(bias[0:D], bias[D:2 * D]),
        "attn_v_w": chunks(np.concatenate([w[:, 2 * D:], attn("rkv_w")[:, lat:]], axis=1)),
        "attn_v_b": np.concatenate([bias[2 * D:], attn("rkv_b")[lat:]]),
        "lat_w": chunks(np.concatenate([by_latent_heads(attn("rq_w")), by_latent_heads(attn("rkv_w")[:, :lat])], axis=1)),
        "lat_b": np.concatenate([by_latent_heads(attn("rq_b")), by_latent_heads(attn("rkv_b")[:lat])]).reshape(128, 1),
        "attn_rout_w": attn("rout_w"), "attn_rout_b": attn("rout_b"),
        "attn_out_w": chunks(attn("out_w")), "attn_out_b": attn("out_b"),
        "attn_gl_w": attn("gl_w").reshape(-1), "attn_gr_w": attn("gr_w").reshape(-1),
        "xattn_qk_w": qk_weight(xattn("Wq"), xattn("Wk")),
        "xattn_qk_b": qk_bias(xattn("bq"), xattn("bk")),
        "xattn_v_w": chunks(xattn("Wv")), "xattn_v_b": xattn("bv"),
        "xattn_gamma": xattn("gamma"), "xattn_beta": xattn("beta"),
        "ffn_slot_init": ffn("slot_init"), "ffn_slot_scale": ffn("slot_scale"),
        "ffn_w1": chunks(ffn("w1").T), "ffn_b1": ffn("b1").reshape(128, 1),
        "ffn_w2": ffn("w2").T, "ffn_b2": ffn("b2"), "ffn_tau": ffn("tau"),
        "ffn_w_ih": chunks(ffn("gru_wih").T), "ffn_w_hh": chunks(ffn("gru_whh").T),
        "ffn_b_ih": ffn("gru_bih"), "ffn_b_hh": ffn("gru_bhh"),
        "ffn_wv": chunks(ffn("wv")), "ffn_wo": chunks(ffn("wo").T),
        "ffn_bv": ffn("bv").reshape(C, 128).T, "ffn_bo": ffn("bo"),
    }
    nc = bacc.Bacc("TRN2", target_bir_lowering=False, num_devices=1)
    arrays, args = {}, {}
    for name, value in laid.items():
        value = np.ascontiguousarray(value)
        arrays[f"in_{name}"] = value
        args[name] = nc.dram_tensor(f"in_{name}", value.shape, mb.dt.from_np(value.dtype), kind="ExternalInput").ap()
    out = nc.dram_tensor("out", (B, S, D), mb.dt.float32, kind="ExternalOutput").ap()
    decoder(nc, args, out)
    return run_bass_kernel_spmd(nc, [arrays], core_ids=[0]).results[0]["out"]
```

```python
from contextlib import ExitStack

import concourse.bass as bass
from concourse import mybir

F32 = mybir.dt.float32
BF16 = mybir.dt.bfloat16
ALU = mybir.AluOpType
ACT = mybir.ActivationFunctionType
AX = mybir.AxisListType

B, S, D = 64, 128, 256
C = D // 128
H, HD = 16, 16
LH, LAT = 4, S // 2
HW = 32
NPAIR = B // 2
PT = 2 * S
GROUPS = 8
NPROD = 6
SPLIT = NPROD * HD
STACK = SPLIT + 2
SLOTS, TOPK = 64, 8
LN_EPS = 1e-5
NEG = -1e30
MADE = 12
SCALE = float(HD) ** -0.5

Q_PART = (0, 0, 1, 1, 0, 2)
K_PART = (0, 1, 0, 1, 2, 0)


class At:

    def __init__(self, i, off):
        self.i, self.off = i, off

    @property
    def pair(self):
        return self.i * 2 + self.off

    @property
    def par(self):
        return self.off % 2

    def back(self, k=1):
        return At(self.i, self.off - k)

    @property
    def real(self):
        return not isinstance(self.i, int) or 0 <= self.off < NPAIR

    @property
    def last(self):
        return isinstance(self.i, int) and self.off == NPAIR - 1

    def count(self, per, k):
        return self.i * (2 * per) + (self.off * per + k)

    def turn(self, per, k):
        return self.i * per + (self.off // 2 * per + k)


def wait(eng, sem, value):
    if isinstance(value, int) and value <= 0:
        return
    eng.wait_ge(sem, value)


PEELED = 4


def pairs(eng, step, last, ahead=0):
    for k in range(PEELED):
        step(At(0, k))
    with eng.Fori(0, (NPAIR - PEELED - 2 * ahead) // 2) as i:
        step(At(i, PEELED))
        step(At(i, PEELED + 1))
    for k in range(NPAIR - 2 * ahead, NPAIR + last):
        step(At(0, k))


def decoder(nc, a, out):
    with ExitStack() as ctx:
        def sem(name):
            return ctx.enter_context(nc.semaphore(name))

        def sb(name, shape, dt=F32):
            return ctx.enter_context(nc.sbuf_tensor(name, shape, dt))

        bank = [ctx.enter_context(nc.psum_tensor(f"bank{b}", [128, 512], F32)) for b in range(8)]
        x_sb = sb("x_sb", [128, B, D])
        ident = sb("ident", [128, 128])
        ident_bf = sb("ident_bf", [128, 128], BF16)
        with ExitStack() as scope:
            attentions(nc, scope, sem, a, bank, x_sb, ident, ident_bf)
        with ExitStack() as scope:
            slots(nc, scope, sem, a, out, bank, x_sb, ident)


def attentions(nc, scope, sem, a, bank, x_sb, ident, ident_bf):
    def sb(name, shape, dt=F32):
        return scope.enter_context(nc.sbuf_tensor(name, shape, dt))

    w_qk = [sb(f"w_qk_{p}", [128, C, 4, 128]) for p in "ab"]
    b_qk = [sb(f"b_qk_{p}", [128, 4]) for p in "ab"]
    w_v = [sb("w_v_a", [128, C, D + LH * HD]), sb("w_v_b", [128, C, D])]
    b_v = [sb("b_v_a", [128, D + LH * HD]), sb("b_v_b", [128, D])]
    w_lat = sb("w_lat", [128, C, 128])
    b_lat = sb("b_lat", [128, 1])
    w_rout = sb("w_rout", [128, D])
    b_rout = sb("b_rout", [128, D])
    w_out = sb("w_out", [128, C, D])
    b_out = sb("b_out", [128, D])
    gate_l = sb("gate_l", [128, HD])
    gate_r = sb("gate_r", [128, HD])
    gamma = sb("gamma", [128, D])
    beta = sb("beta", [128, D])
    ones_sq = sb("ones_sq", [128, 128])
    mask = [sb(f"mask_{p}", [128, 4, 128], BF16) for p in "ab"]
    mask_lat = sb("mask_lat", [128, LH, LAT], BF16)
    lat_rows = sb("lat_rows", [128, 1])

    stats = sb("stats", [128, 2, 6])
    moments = sb("moments", [128, 2, 2])
    var_eps = sb("var_eps", [128, 2])
    rstd = sb("rstd", [128, 2])
    minus_half = sb("minus_half", [128, 2])
    eps = sb("eps", [128, 2])
    xn = sb("xn", [128, 2, D])
    xn_t = sb("xn_t", [128, C, PT])
    qk_f = sb("qk_f", [128, 4, PT])
    qk_rest = sb("qk_rest", [128, 4, PT])
    qk_part = [sb(f"qk_part{i}", [128, 4, PT], BF16) for i in range(3)]
    lat_f = sb("lat_f", [128, PT])
    lat_raw = sb("lat_raw", [128, PT])
    lat_rest = sb("lat_rest", [128, PT])
    lat_part = [sb(f"lat_part{i}", [128, PT], BF16) for i in range(3)]
    q_stack = [sb(f"q_stack{i}", [128, H, PT], BF16) for i in range(2)]
    k_stack = [sb(f"k_stack{i}", [128, H, PT], BF16) for i in range(2)]
    rq_stack = [sb(f"rq_stack{i}", [128, LH, PT], BF16) for i in range(2)]
    rk_stack = [sb(f"rk_stack{i}", [128, LH, 2 * LAT], BF16) for i in range(2)]
    v_heads = [sb(f"v_heads{i}", [128, 2, H, HW]) for i in range(2)]
    rv_heads = [sb(f"rv_heads{i}", [128, 2, LH, HW]) for i in range(2)]
    neg_max = sb("neg_max", [128, 2, H])
    max_part = sb("max_part", [128, 2, 2, H], BF16)
    max_t = sb("max_t", [2 * H, PT], BF16)
    probs_t = [sb(f"probs_t{i}", [128, 4, 128]) for i in range(4)]
    av_t = [sb(f"av_t{i}", [128, 4, 128]) for i in range(2)]
    sums = sb("sums", [128, 2, H])
    inv = sb("inv", [128, 2, H])
    attn = sb("attn", [128, 2, D])
    lat_max = sb("lat_max", [128, 2, LH])
    lat_s = sb("lat_s", [128, 2, LH, LAT])
    lat_p = sb("lat_p", [128, 2, LH, LAT])
    lat_sum = sb("lat_sum", [128, 2, LH])
    lat_inv = sb("lat_inv", [128, 2, LH])
    lat_w = sb("lat_w", [128, 2, LH])
    lat_pd = sb("lat_pd", [128, 2, LH, LAT, 2])
    lat_pt = [sb(f"lat_pt{i}", [128, LH, 128]) for i in range(2)]
    lat_out = sb("lat_out", [128, PT])
    remote = sb("remote", [128, 2, D])
    remote_g = sb("remote_g", [128, 2, D])
    tmp = [sb(f"tmp{i}", [128, 2, D]) for i in range(4)]
    gate_z = sb("gate_z", [128, 2, H])
    gate_t = sb("gate_t", [128, 2, H])
    gate = sb("gate", [128, 2, H])
    mix_t = sb("mix_t", [128, 2, C, 128])
    x_bias = sb("x_bias", [128, 2, D])
    ctx_in = [x[:].rearrange("p t h l -> p t (h l)") for x in (lat_s, lat_p)]
    ctx_t, v_raw = remote_g[:], remote[:]
    q_tok = [x[:].rearrange("p (t a) n -> p t (a n)", t=2) for x in lat_pt]

    pool_turn, sp_turn = sem("pool_turn"), sem("sp_turn")
    loaded, made, made_v = sem("weights_loaded"), sem("consts_made_pool"), sem("consts_made_dve")

    with nc.Block() as block:
        loads = [
            (w_qk[0], a["attn_qk_w"]), (w_qk[1], a["xattn_qk_w"]),
            (b_qk[0], a["attn_qk_b"]), (b_qk[1], a["xattn_qk_b"]),
            (w_v[0], a["attn_v_w"]), (w_v[1], a["xattn_v_w"]),
            (w_lat, a["lat_w"]), (b_lat, a["lat_b"]), (w_out, a["attn_out_w"]),
        ]
        rows = [(b_v[0], a["attn_v_b"]), (b_v[1], a["xattn_v_b"]), (b_rout, a["attn_rout_b"]),
                (b_out, a["attn_out_b"]), (gate_l, a["attn_gl_w"]), (gate_r, a["attn_gr_w"]),
                (gamma, a["xattn_gamma"]), (beta, a["xattn_beta"])]

        @block.sync
        def _(sp):
            for tile, src in loads:
                sp.dma_start(tile[:], src).then_inc(loaded, 16)
            for tile, src in rows:
                sp.dma_start(tile[:], src.partition_broadcast(128)).then_inc(loaded, 16)
            sp.wait_ge(made_v, 1)
            for h in range(LH):
                sp.dma_start(w_rout[HW * h:HW * h + HD, :], a["attn_rout_w"][HD * h:HD * h + HD, :]).then_inc(loaded, 16)
            sp.wait_ge(loaded, 16 * (len(loads) + len(rows) + LH))

        @block.vector
        def _(dve):
            nc.vector.memset(w_rout[:], 0.0).then_inc(made_v, 1)
            for t in range(2):
                nc.vector.memset(v_heads[t][:], 0.0).then_inc(made_v, 1)
                nc.vector.memset(rv_heads[t][:], 0.0).then_inc(made_v, 1)
            nc.vector.memset(lat_rows[:], 0.5).then_inc(made_v, 1)
            nc.vector.memset(lat_f[:], 0.0).then_inc(made_v, 1)
            dve.wait_ge(made_v, 7)
            for t in range(2):
                nc.vector.memset(k_stack[t][SPLIT:STACK, :, :], 1.0).then_inc(made_v, 1)
                nc.vector.memset(v_heads[t][:, :, :, HD:HD + 1], 1.0).then_inc(made_v, 1)
            nc.vector.memset(lat_rows[0:2, :], 0.0).then_inc(made_v, 1)
            dve.wait_ge(made_v, 12)

        @block.gpsimd
        def _(pool):
            nc.gpsimd.memset(minus_half[:], -0.5)
            nc.gpsimd.memset(ones_sq[:], 1.0).then_inc(made, 1)
            nc.gpsimd.memset(mask[0][:], 0.0).then_inc(made, 1)
            nc.gpsimd.memset(mask[1][:], 0.0).then_inc(made, 1)
            nc.gpsimd.memset(mask_lat[:], 0.0).then_inc(made, 1)
            nc.gpsimd.memset(eps[:], LN_EPS).then_inc(made, 1)
            pool.wait_ge(made, 5)
            nc.gpsimd.affine_select(out=ident[:], in_=ones_sq[:], pattern=[[-1, 128]], compare_op=ALU.is_equal,
                                    fill=0.0, base=0, channel_multiplier=1).then_inc(made, 1)
            nc.gpsimd.affine_select(out=mask[0][:], in_=mask[0][:], pattern=[[0, 4], [-1, 128]], compare_op=ALU.is_ge,
                                    fill=NEG, base=-1, channel_multiplier=1).then_inc(made, 1)
            nc.gpsimd.affine_select(out=mask[1][:], in_=mask[1][:], pattern=[[0, 4], [-1, 128]], compare_op=ALU.is_ge,
                                    fill=NEG, base=0, channel_multiplier=1).then_inc(made, 1)
            nc.gpsimd.affine_select(out=mask_lat[:], in_=mask_lat[:], pattern=[[0, LH], [-2, LAT]], compare_op=ALU.is_ge,
                                    fill=NEG, base=-2, channel_multiplier=1).then_inc(made, 1)
            pool.wait_ge(made, 9)
            nc.gpsimd.memset(mask[0][0:1, :, 0:1], 0.0).then_inc(made, 1)
            nc.gpsimd.memset(mask_lat[0:2, :, 0:1], 0.0).then_inc(made, 1)
            nc.gpsimd.tensor_copy(ident_bf[:], ident[:]).then_inc(made, 1)
            pool.wait_ge(made, MADE)

    attn_phase(nc, sem, locals(), local=True)
    attn_phase(nc, sem, locals(), local=False)


def attn_phase(nc, sem, t, local):
    ph = 0 if local else 1
    P = "ab"[ph]
    a, bank, x_sb, ident, ident_bf = t["a"], t["bank"], t["x_sb"], t["ident"], t["ident_bf"]
    var_eps, minus_half, eps, pool_turn, sp_turn = (
        t[k] for k in ("var_eps", "minus_half", "eps", "pool_turn", "sp_turn"))
    (ctx_in, stats, moments, rstd, xn, xn_t, ctx_t, qk_f, qk_rest, qk_part, lat_f, lat_raw, lat_rest, lat_part) = (
        t[k] for k in ("ctx_in", "stats", "moments", "rstd", "xn", "xn_t", "ctx_t", "qk_f", "qk_rest", "qk_part",
                       "lat_f", "lat_raw", "lat_rest", "lat_part"))
    (q_stack, k_stack, rq_stack, rk_stack, v_heads, rv_heads, v_raw, neg_max, max_part, max_t, probs_t, av_t) = (
        t[k] for k in ("q_stack", "k_stack", "rq_stack", "rk_stack", "v_heads", "rv_heads", "v_raw", "neg_max",
                       "max_part", "max_t", "probs_t", "av_t"))
    (sums, inv, attn, lat_max, lat_s, lat_p, lat_sum, lat_inv, lat_w, lat_pd, lat_pt, lat_out, remote, remote_g) = (
        t[k] for k in ("sums", "inv", "attn", "lat_max", "lat_s", "lat_p", "lat_sum", "lat_inv", "lat_w", "lat_pd",
                       "lat_pt", "lat_out", "remote", "remote_g"))
    (tmp, gate_z, gate_t, gate, mix_t, x_bias, q_tok, gate_l, gate_r, lat_rows) = (
        t[k] for k in ("tmp", "gate_z", "gate_t", "gate", "mix_t", "x_bias", "q_tok", "gate_l", "gate_r", "lat_rows"))
    w_qk, b_qk, w_v, b_v, mask = (t[k][ph] for k in ("w_qk", "b_qk", "w_v", "b_v", "mask"))
    w_lat, b_lat, w_rout, b_rout, w_out, b_out, gamma, beta, mask_lat = (
        t[k] for k in ("w_lat", "b_lat", "w_rout", "b_rout", "w_out", "b_out", "gamma", "beta", "mask_lat"))

    tr_bank, proj_bank, score_bank, av_bank, back_bank, out_bank = (
        bank[0], bank[1:3], bank[3:5], bank[5], bank[6], bank[7])

    only_local = """lat_filled lat_evac lat_ready ls_filled lmax_done lsub_done lexp_done lsum_step lp_ready
        lpT_filled lpT_ready lo_filled lo_ready remote_filled remote_ready remote_gated z_in z_ready tanh_ready
        gate_ready mixed mixT_filled mixT_ready out_filled xb_ready""".split()
    only_context = "ctxT_filled ctxT_ready v_relu qT_filled qT_ready sum_ready norm_ready norm_step norm_eps norm_scaled".split()

    def s(name):
        return None if name in (only_context if local else only_local) else sem(f"{P}_{name}")

    x_loaded = [s(f"x_loaded{i}") for i in range(2)]
    ln_step, xn_ready = s("ln_step"), s("xn_ready")
    ln_eps, ln_scaled = s("ln_eps"), s("ln_scaled")
    norm_eps, norm_scaled = s("norm_eps"), s("norm_scaled")
    xnT_filled, xnT_ready = s("xnT_filled"), s("xnT_ready")
    ctxT_filled, ctxT_ready = s("ctxT_filled"), s("ctxT_ready")
    q_filled, k_filled, q_ready, k_ready = s("q_filled"), s("k_filled"), s("q_ready"), s("k_ready")
    lat_filled, lat_evac, lat_ready = s("lat_filled"), s("lat_evac"), s("lat_ready")
    v_filled, v_ready, v_relu = s("v_filled"), s("v_ready"), s("v_relu")
    part_step = s("part_step")
    stacked = [s(f"stacked{i}") for i in range(2)]
    lat_stacked = [s(f"lat_stacked{i}") if local else None for i in range(2)]
    max_stacked = [s(f"max_stacked{i}") for i in range(2)]
    sc_filled, max_done = s("sc_filled"), s("max_done")
    max_step = s("max_step")
    maxT_filled, maxT_ready = s("maxT_filled"), s("maxT_ready")
    sct_filled, exp_done, masked = s("sct_filled"), s("exp_done"), s("masked")
    av_filled, av_ready = s("av_filled"), s("av_ready")
    back_filled, sum_step, attn_ready = s("back_filled"), s("sum_step"), s("attn_ready")
    ls_filled, lmax_done, lsub_done, lexp_done = s("ls_filled"), s("lmax_done"), s("lsub_done"), s("lexp_done")
    lsum_step, lp_ready = s("lsum_step"), s("lp_ready")
    lpT_filled, lpT_ready, lo_filled, lo_ready = s("lpT_filled"), s("lpT_ready"), s("lo_filled"), s("lo_ready")
    remote_filled, remote_ready, remote_gated = s("remote_filled"), s("remote_ready"), s("remote_gated")
    mix_step, z_in, z_ready, tanh_ready, gate_ready = (
        s("mix_step"), s("z_in"), s("z_ready"), s("tanh_ready"), s("gate_ready"))
    mixed, mixT_filled, mixT_ready = s("mixed"), s("mixT_filled"), s("mixT_ready")
    out_filled, xb_ready, x_done = s("out_filled"), s("xb_ready"), s("x_done")
    qT_filled, qT_ready = s("qT_filled"), s("qT_ready")
    sum_ready, norm_ready, norm_step = s("sum_ready"), s("norm_ready"), s("norm_step")

    STEPS = 3 * 2 + (4 if local else 0)
    STACKED = 16 * NPROD * 2

    source = (a["x"] if local else a["ctx"]).rearrange("s p d -> p s d")

    with nc.Block() as block:

        @block.sync
        def _(sp):
            def load(at):
                if local:
                    dst = x_sb[:, bass.ds(at.i * 4 + 2 * at.off, 2), :]
                else:
                    wait(sp, ctxT_filled, at.count(1, -1))
                    dst = ctx_in[at.par]
                wait(sp, x_loaded[at.par], at.turn(16, 0))
                sp.dma_start(dst, source[:, bass.ds(at.i * 4 + 2 * at.off, 2), :]).then_inc(x_loaded[at.par], 16)

            def stack_max(at):
                wait(sp, maxT_ready, at.count(1, 1))
                sp.dma_start(q_stack[at.par][SPLIT:STACK, :, :], max_t[:]).then_inc(max_stacked[at.par], 16)

            def step(at):
                p = at.par
                if at.off > 0:
                    stack_max(at.back())
                wait(sp, av_filled, at.count(GROUPS, -GROUPS))
                if at.off >= 2:
                    sp.sem_inc(sp_turn, 1)
                order = [("q", 0), ("q", 1), ("k", 0), ("k", 1), ("q", 2), ("k", 2)]
                if local:
                    order += [("lat", 0), ("lat", 1), ("lat", 2)]
                for what, part in order:
                    if what != "lat" and part == 0:
                        wait(sp, q_ready if what == "q" else k_ready, at.count(1, 1))
                    else:
                        n = {"q": (0, 2, 3), "k": (0, 5, 6), "lat": (7, 9, 10)}[what][part]
                        wait(sp, part_step, at.count(STEPS, n))
                    for j in range(NPROD):
                        rows = slice(HD * j, HD * j + HD)
                        if what == "q" and Q_PART[j] == part:
                            sp.dma_start(q_stack[p][rows, :, :], qk_part[part][:, 0:2, :]).then_inc(stacked[p], 16)
                        if what == "k" and K_PART[j] == part:
                            sp.dma_start(k_stack[p][rows, :, :], qk_part[part][:, 2:4, :]).then_inc(stacked[p], 16)
                        if what == "lat" and Q_PART[j] == part:
                            sp.dma_start(rq_stack[p][rows, :, :], lat_part[part][0:64, :]).then_inc(lat_stacked[p], 16)
                        if what == "lat" and K_PART[j] == part:
                            sp.dma_start(rk_stack[p][rows, :, :],
                                         lat_part[part][64:128, 0:2 * LAT]).then_inc(lat_stacked[p], 16)

            load(At(0, 0))
            load(At(0, 1))

            for k in range(PEELED):
                load(At(0, k + 2))
                step(At(0, k))
            with sp.Fori(0, (NPAIR - PEELED - 2) // 2) as i:
                for k in range(2):
                    load(At(i, PEELED + k + 2))
                    step(At(i, PEELED + k))
            step(At(0, NPAIR - 2))
            step(At(0, NPAIR - 1))
            stack_max(At(0, NPAIR - 1))
            for p in range(2):
                sp.wait_ge(max_stacked[p], 16 * (NPAIR // 2))

        @block.tensor
        def _(pe):
            def transpose_x(at):
                pe.wait_ge(xn_ready, at.count(1, 1))
                wait(pe, xnT_ready, at.count(1, 0))
                for tt in range(2):
                    for c in range(C):
                        mm = pe.transpose(tr_bank[:, c * PT + tt * S:c * PT + tt * S + S],
                                          xn[:, tt, 128 * c:128 * c + 128], ident[:])
                mm.then_inc(xnT_filled, 1)

            def transpose_ctx(at):
                pe.wait_ge(x_loaded[at.par], at.turn(16, 16))
                wait(pe, ctxT_ready, at.count(1, 0))
                for tt in range(2):
                    for c in range(C):
                        mm = pe.transpose(out_bank[:, c * PT + tt * S:c * PT + tt * S + S],
                                          ctx_in[at.par][:, tt, 128 * c:128 * c + 128], ident[:])
                mm.then_inc(ctxT_filled, 1)

            def project(dst, w, src, filled):
                for c in range(C):
                    mm = pe.matmul(dst, w(c), src[:, c, :], start=(c == 0), stop=(c == C - 1))
                return mm

            def project_q(at):
                pe.wait_ge(xnT_ready, at.count(1, 1))
                wait(pe, v_ready, at.count(2, 0))
                for g in range(2):
                    mm = project(proj_bank[0][:, g * PT:g * PT + PT], lambda c: w_qk[:, c, g, :], xn_t, None)
                mm.then_inc(q_filled, 1)

            def project_k(at):
                if not local:
                    pe.wait_ge(ctxT_ready, at.count(1, 1))
                wait(pe, v_ready, at.count(2, -1))
                for g in range(2):
                    mm = project(proj_bank[1][:, g * PT:g * PT + PT], lambda c: w_qk[:, c, 2 + g, :],
                                 xn_t if local else ctx_t, None)
                mm.then_inc(k_filled, 1)

            def project_lat(at):
                pe.wait_ge(q_ready, at.count(1, 1))
                project(proj_bank[0][:, 0:PT], lambda c: w_lat[:, c, :], xn_t, None).then_inc(lat_filled, 1)

            def project_v(at, tt):
                if tt == 0:
                    pe.wait_ge(k_ready, at.count(1, 1))
                elif local:
                    pe.wait_ge(lat_evac, at.count(1, 1))
                else:
                    pe.wait_ge(q_ready, at.count(1, 1))
                n = w_v.shape[2]
                src = xn_t if local else ctx_t
                for c in range(C):
                    mm = pe.matmul(proj_bank[1 - tt][:, 0:n], src[:, c, S * tt:S * tt + S], w_v[:, c, :],
                                   start=(c == 0), stop=(c == C - 1))
                mm.then_inc(v_filled, 1)

            def transpose_q(at):
                pe.wait_ge(q_ready, at.count(1, 1))
                wait(pe, attn_ready, at.count(2, -2))
                for tt in range(2):
                    for g in range(2):
                        mm = pe.transpose(back_bank[:, 256 * tt + 128 * g:256 * tt + 128 * g + 128],
                                          qk_f[:, g, S * tt:S * tt + S], ident[:])
                mm.then_inc(qT_filled, 1)

            def scores(at, g):
                tt, h0, dst = g // 4, 4 * (g % 4), score_bank[g % 2]
                if g >= 2:
                    pe.wait_ge(max_done, at.count(GROUPS, g - 1))
                else:
                    wait(pe, exp_done, at.count(GROUPS, 0))
                if g == 0:
                    pe.wait_ge(stacked[at.par], at.turn(STACKED, STACKED))
                pe.matmul(dst[:], ident_bf[:], mask[:].rearrange("p j k -> p (j k)"), start=True, stop=False, skip_group_check=True)
                for j in range(4):
                    mm = pe.matmul(dst[:, 128 * j:128 * j + 128], q_stack[at.par][0:SPLIT, h0 + j, S * tt:S * tt + S],
                                   k_stack[at.par][0:SPLIT, h0 + j, S * tt:S * tt + S],
                                   start=False, stop=(j == 3), skip_group_check=True)
                mm.then_inc(sc_filled, 1)

            def max_transpose(at):
                pe.wait_ge(max_step, at.count(2, 2))
                wait(pe, av_ready, at.count(2, 0))
                dst = av_bank[:].bitcast(BF16)
                for tt in range(2):
                    mm = pe.transpose(dst[0:2 * H, S * tt:S * tt + S],
                                      max_part[:, tt, :, :].rearrange("p a h -> p (a h)"), ident_bf[:])
                mm.then_inc(maxT_filled, 1)

            def lat_scores(at, tt):
                dst = back_bank[:, LH * LAT * tt:LH * LAT * tt + LH * LAT]
                if tt == 0:
                    wait(pe, attn_ready, at.count(2, 0))
                    pe.wait_ge(lat_stacked[at.par], at.turn(STACKED, STACKED))
                pe.matmul(dst, ident_bf[:], mask_lat[:].rearrange("p h l -> p (h l)"), start=True, stop=False, skip_group_check=True)
                for h in range(LH):
                    mm = pe.matmul(dst[:, LAT * h:LAT * h + LAT], rq_stack[at.par][0:SPLIT, h, S * tt:S * tt + S],
                                   rk_stack[at.par][0:SPLIT, h, LAT * tt:LAT * tt + LAT],
                                   start=False, stop=(h == LH - 1), skip_group_check=True)
                if tt == 1:
                    mm.then_inc(ls_filled, 1)

            def lat_transpose(at, tt):
                if tt == 0:
                    pe.wait_ge(lp_ready, at.count(1, 1))
                    wait(pe, x_done, at.count(1, 0))
                else:
                    pe.wait_ge(lpT_ready, at.count(2, 1))
                for h in range(LH):
                    mm = pe.transpose(out_bank[:, 128 * h:128 * h + 128],
                                      lat_pd_view(tt, h), ident[:])
                mm.then_inc(lpT_filled, 1)

            def lat_pd_view(tt, h):
                return lat_pd[:, tt, h, :, :].rearrange("p l r -> p (l r)")

            def lat_values(at):
                pe.wait_ge(lpT_ready, at.count(2, 2))
                pe.wait_ge(v_ready, at.count(2, 2))
                for tt in range(2):
                    for h in range(LH):
                        mm = pe.matmul(out_bank[HW * h:HW * h + HW, S * tt:S * tt + S],
                                       rv_heads[at.par][:, tt, h, :], lat_pt[tt][:, h, :], start=True, stop=True,
                                       skip_group_check=True)
                mm.then_inc(lo_filled, 1)

            def remote_out(at):
                pe.wait_ge(lo_ready, at.count(1, 1))
                for tt in range(2):
                    mm = pe.matmul(out_bank[:, D * tt:D * tt + D], lat_out[:, S * tt:S * tt + S], w_rout[:],
                                   start=True, stop=True, skip_group_check=True)
                mm.then_inc(remote_filled, 1)

            def scores_t(at, g):
                tt, h0, dst = g // 4, 4 * (g % 4), score_bank[g % 2]
                if g >= 2:
                    pe.wait_ge(exp_done, at.count(GROUPS, g - 1))
                else:
                    pe.wait_ge(max_done, at.count(GROUPS, 7 + g))
                if g == 0:
                    pe.wait_ge(max_stacked[at.par], at.turn(16, 16))
                for j in range(4):
                    mm = pe.matmul(dst[:, 128 * j:128 * j + 128], k_stack[at.par][0:STACK, h0 + j, S * tt:S * tt + S],
                                   q_stack[at.par][0:STACK, h0 + j, S * tt:S * tt + S],
                                   start=True, stop=True, skip_group_check=True)
                mm.then_inc(sct_filled, 1)

            def values(at, g):
                tt, h0 = g // 4, 4 * (g % 4)
                pe.wait_ge(masked, at.count(GROUPS, g + 1))
                if g == 0:
                    pe.wait_ge(v_ready if local else v_relu, at.count(2, 2))
                if g == 4:
                    pe.wait_ge(av_ready, at.count(2, 1))
                for j in range(4):
                    mm = pe.matmul(av_bank[HW * j:HW * j + HW, 128 * (g % 4):128 * (g % 4) + 128],
                                   v_heads[at.par][:, tt, h0 + j, :], probs_t[g % 4][:, j, :],
                                   start=True, stop=True, skip_group_check=True)
                mm.then_inc(av_filled, 1)

            def back(at, tt):
                pe.wait_ge(av_ready, at.count(2, tt + 1))
                if tt == 1:
                    pe.wait_ge(attn_ready, at.count(2, 1))
                elif local:
                    wait(pe, mixT_ready, at.count(1, 0))
                else:
                    qT = 2 if at.off + 1 < NPAIR or not isinstance(at.i, int) else 1
                    pe.wait_ge(qT_ready, at.count(1, qT))
                for g in range(4):
                    mm = pe.transpose(back_bank[:, 128 * g:128 * g + 128], av_t[tt][:, g, :], ident[:])
                mm.then_inc(back_filled, 1)

            def mix_transpose(at):
                pe.wait_ge(mixed, at.count(1, 1))
                if at.back(-1).real:
                    pe.wait_ge(lsub_done, at.count(1, 2))
                for tt in range(2):
                    for c in range(C):
                        mm = pe.transpose(back_bank[:, 256 * tt + 128 * c:256 * tt + 128 * c + 128],
                                          tmp[3][:, tt, 128 * c:128 * c + 128], ident[:])
                mm.then_inc(mixT_filled, 1)

            def project_out(at):
                pe.wait_ge(mixT_ready, at.count(1, 1))
                pe.wait_ge(remote_ready, at.count(1, 1))
                for tt in range(2):
                    for c in range(C):
                        mm = pe.matmul(out_bank[:, D * tt:D * tt + D], mix_t[:, tt, c, :], w_out[:, c, :],
                                       start=(c == 0), stop=(c == C - 1), skip_group_check=True)
                mm.then_inc(out_filled, 1)

            def step(at):
                prev, old = at.back(), at.back(2)
                after = {1: [(old, lambda n: back(n, 1)), (at, transpose_x)], 3: [(at, project_q)], 7: [(at, project_k)]}
                before = {0: [(at, lambda n: project_v(n, 0))]}
                if local:
                    after[5], after[6] = [(prev, lambda n: lat_scores(n, 0))], [(prev, lambda n: lat_scores(n, 1))]
                    before.update({
                        0: [(at, project_lat), (old, mix_transpose), (at, lambda n: project_v(n, 0))],
                        2: [(old, project_out)], 3: [(at, lambda n: project_v(n, 1))],
                        5: [(prev, lambda n: lat_transpose(n, 0))], 6: [(prev, lambda n: lat_transpose(n, 1))],
                        7: [(prev, lat_values)], 8: [(prev, remote_out)]})
                else:
                    after[2] = [(at, transpose_ctx)]
                    before.update({1: [(at, lambda n: project_v(n, 1))], 3: [(at, transpose_q)]})

                def run(steps):
                    for pair, what in steps:
                        if pair.real:
                            what(pair)

                for g in range(GROUPS):
                    if prev.real:
                        scores(prev, g)
                    run(after.get(g, []))
                if prev.real:
                    max_transpose(prev)
                for g in range(GROUPS + 2):
                    run(before.get(g, []))
                    if prev.real:
                        if g < GROUPS:
                            scores_t(prev, g)
                        if g >= 2:
                            values(prev, g - 2)
                        if g == 7:
                            back(prev, 0)

            pairs(pe, step, 2)

        @block.scalar
        def _(act):
            def step(at):
                prev, old = at.back(), at.back(2)

                def copy_lat_t(tt):
                    act.wait_ge(lpT_filled, prev.count(2, tt + 1))
                    wait(act, lo_filled, prev.count(1, 0))
                    nc.scalar.activation(lat_pt[tt][:].rearrange("p h t -> p (h t)"), out_bank[:],
                                         ACT.Copy).then_inc(lpT_ready, 1)

                def evac_qk(filled, ready, g0, reread):
                    act.wait_ge(filled, at.count(1, 1))
                    reread()
                    wait(act, stacked[1 - at.par], at.back().turn(STACKED, STACKED))
                    src = proj_bank[g0 // 2]
                    for dst in (qk_part[0], qk_f):
                        for g in range(2):
                            ins = nc.scalar.activation(dst[:, g0 + g, :], src[:, g * PT:g * PT + PT],
                                                       ACT.Identity if local else ACT.Relu,
                                                       bias=b_qk[:, g0 + g:g0 + g + 1])
                    ins.then_inc(ready, 1)

                def copy_xn():
                    act.wait_ge(xnT_filled, at.count(1, 1))
                    wait(act, v_filled if local else q_filled, at.count(2 if local else 1, 0))
                    nc.scalar.activation(xn_t[:].rearrange("p c t -> p (c t)"), tr_bank[:],
                                         ACT.Copy).then_inc(xnT_ready, 1)

                def copy_ctx():
                    act.wait_ge(ctxT_filled, at.count(1, 1))
                    wait(act, v_filled, at.count(2, 0))
                    nc.scalar.activation(ctx_t.rearrange("p c t -> p (c t)"), out_bank[:],
                                         ACT.Copy).then_inc(ctxT_ready, 1)

                def evac_q():
                    def reread():
                        wait(act, part_step, at.count(STEPS, -STEPS + 1))
                        if not local:
                            wait(act, qT_filled, at.count(1, 0))
                    evac_qk(q_filled, q_ready, 0, reread)

                def evac_k():
                    evac_qk(k_filled, k_ready, 2, lambda: wait(act, part_step, at.count(STEPS, -STEPS + 4)))

                def evac_lat():
                    act.wait_ge(lat_filled, at.count(1, 1))
                    wait(act, part_step, at.count(STEPS, -2))
                    nc.scalar.activation(lat_f[0:64, :], proj_bank[0][0:64, 0:PT], ACT.Identity, bias=b_lat[0:64, :])
                    nc.scalar.activation(lat_raw[64:128, :], proj_bank[0][64:128, 0:PT], ACT.Identity,
                                         bias=b_lat[64:128, :]).then_inc(lat_evac, 1)

                def relu_v(tt):
                    act.wait_ge(v_ready, at.count(2, tt + 1))
                    wait(act, av_filled, at.count(GROUPS, -GROUPS))
                    nc.scalar.activation(v_heads[at.par][:, tt, :, 0:HD],
                                         v_raw[:, tt, :].rearrange("p (h n) -> p h n", n=HD),
                                         ACT.Relu).then_inc(v_relu, 1)

                def copy_lat_out():
                    act.wait_ge(lo_filled, prev.count(1, 1))
                    wait(act, remote_filled, prev.count(1, 0))
                    nc.scalar.activation(lat_out[:], out_bank[:, 0:PT], ACT.Copy).then_inc(lo_ready, 1)

                def copy_mix():
                    act.wait_ge(mixT_filled, old.count(1, 1))
                    wait(act, out_filled, old.count(1, 0))
                    nc.scalar.activation(mix_t[:].rearrange("p t c n -> p (t c n)"), back_bank[:],
                                         ACT.Copy).then_inc(mixT_ready, 1)

                def copy_q_tok():
                    act.wait_ge(qT_filled, at.count(1, 1))
                    wait(act, sum_ready, at.count(1, -1))
                    for tt in range(2):
                        ins = nc.scalar.activation(
                            q_tok[at.par][:, tt, :].rearrange("p (hh g r) -> p g r hh", g=2, r=HD),
                            back_bank[:, 256 * tt:256 * tt + 256].rearrange("p (g r hh) -> p g r hh", g=2, r=HD),
                            ACT.Copy)
                    ins.then_inc(qT_ready, 1)

                def exp(g):
                    act.wait_ge(sct_filled, prev.count(GROUPS, g + 1))
                    wait(act, av_filled, prev.count(GROUPS, g - 3))
                    nc.scalar.activation(probs_t[g % 4][:].rearrange("p j t -> p (j t)"), score_bank[g % 2][:],
                                         ACT.Exp, scale=SCALE).then_inc(exp_done, 1)

                def evac_av(at, tt):
                    act.wait_ge(av_filled, at.count(GROUPS, 4 * tt + 4))
                    wait(act, back_filled, at.count(2, tt - 1))
                    nc.scalar.activation(av_t[tt][:].rearrange("p g t -> p (g t)"), av_bank[:],
                                         ACT.Copy).then_inc(av_ready, 1)

                def copy_max():
                    act.wait_ge(maxT_filled, prev.count(1, 1))
                    wait(act, max_stacked[1 - prev.par], prev.back().turn(16, 16))
                    nc.scalar.activation(max_t[:], av_bank[:].bitcast(BF16)[0:2 * H, 0:PT],
                                         ACT.Copy).then_inc(maxT_ready, 1)

                def gate_tanh(at):
                    act.wait_ge(z_ready, at.count(1, 1))
                    wait(act, gate_ready, at.count(1, 0))
                    nc.scalar.activation(gate_t[:], gate_z[:], ACT.Tanh, scale=0.5).then_inc(tanh_ready, 1)

                def exp_lat():
                    act.wait_ge(lsub_done, prev.count(1, 1))
                    wait(act, lp_ready, prev.count(1, 0))
                    nc.scalar.activation(lat_p[:].rearrange("p t h l -> p (t h l)"),
                                         lat_s[:].rearrange("p t h l -> p (t h l)"),
                                         ACT.Exp, scale=0.5 * SCALE).then_inc(lexp_done, 1)

                if old.real:
                    evac_av(old, 1)
                if at.real:
                    copy_xn()
                    if not local:
                        copy_ctx()
                    evac_q()
                if local and old.real:
                    gate_tanh(old)
                if prev.real:
                    copy_max()
                if at.real:
                    evac_k()
                if local and old.real:
                    copy_mix()
                if local and prev.real:
                    exp_lat()
                if prev.real:
                    exp(0)
                    exp(1)
                if local and at.real:
                    evac_lat()
                if prev.real:
                    exp(2)
                if not local and at.real:
                    relu_v(0)
                if prev.real:
                    exp(3)
                if not local and at.real:
                    relu_v(1)
                if prev.real:
                    exp(4)
                if not local and at.real:
                    copy_q_tok()
                if prev.real:
                    if local:
                        copy_lat_t(0)
                    exp(5)
                    evac_av(prev, 0)
                    if local:
                        copy_lat_t(1)
                    exp(6)
                    if local:
                        copy_lat_out()
                    exp(7)

            pairs(act, step, 2)

        @block.vector
        def _(dve):
            def x_rows(at, tt):
                return x_sb[:, bass.ds(at.i * 4 + 2 * at.off + tt, 1), :].rearrange("p s d -> p (s d)")

            def x_pair(at):
                return x_sb[:, bass.ds(at.i * 4 + 2 * at.off, 2), :]

            def norm_stats(src, step):
                for tt in range(2):
                    ins = nc.vector.bn_stats(stats[:, tt, :], src(tt))
                ins.then_inc(step, 1)

            def norm_moments(step):
                for tt in range(2):
                    ins = nc.vector.bn_aggr(moments[:, tt, :], stats[:, tt, :])
                ins.then_inc(step, 1)

            def norm_scale(src, dst, done):
                for tt in range(2):
                    ins = nc.vector.tensor_scalar(dst[:, tt, :], src(tt), moments[:, tt, 0:1], rstd[:, tt:tt + 1],
                                                  ALU.subtract, ALU.mult)
                ins.then_inc(done, 1)

            def x_stats(at):
                if local:
                    dve.wait_ge(x_loaded[at.par], at.turn(16, 16))
                norm_stats(lambda tt: x_rows(at, tt), ln_step)

            def x_scale(at):
                dve.wait_ge(ln_scaled, at.count(1, 1))
                wait(dve, xnT_filled, at.count(1, 0))
                norm_scale(lambda tt: x_rows(at, tt), xn, xn_ready)

            def split(at, n, src, rest, part):
                first = 3 * n + (n == 2)
                if n == 2:
                    nc.vector.tensor_copy(part[0], src).then_inc(part_step, 1)
                    dve.wait_ge(part_step, at.count(STEPS, first))
                wait(dve, part_step, at.count(STEPS, first + 3 - STEPS))
                nc.vector.tensor_tensor(rest, src, part[0], ALU.subtract).then_inc(part_step, 1)
                dve.wait_ge(part_step, at.count(STEPS, first + 1))
                nc.vector.tensor_copy(part[1], rest).then_inc(part_step, 1)
                dve.wait_ge(part_step, at.count(STEPS, first + 2))
                nc.vector.tensor_tensor(part[2], rest, part[1], ALU.subtract).then_inc(part_step, 1)

            def normalise(at, tt):
                dve.wait_ge(back_filled, at.count(2, tt + 1))
                src = back_bank[:].rearrange("p (h n) -> p h n", n=HW)
                nc.vector.tensor_scalar(sums[:, tt, :], src[:, :, HD], 1e-30, None, ALU.max).then_inc(sum_step, 1)
                dve.wait_ge(sum_step, at.count(4, 2 * tt + 1))
                nc.vector.reciprocal(inv[:, tt, :], sums[:, tt, :]).then_inc(sum_step, 1)
                dve.wait_ge(sum_step, at.count(4, 2 * tt + 2))
                if local:
                    wait(dve, mixed, at.count(1, 0))
                else:
                    wait(dve, sum_ready, at.count(1, 0))
                nc.vector.tensor_tensor(attn[:, tt, :].rearrange("p (h n) -> p h n", n=HD), src[:, :, 0:HD],
                                        inv[:, tt, :].unsqueeze(2).to_broadcast([128, H, HD]),
                                        ALU.mult).then_inc(attn_ready, 1)

            def row_max(at, g):
                tt, h0 = g // 4, 4 * (g % 4)
                dve.wait_ge(sc_filled, at.count(GROUPS, g + 1))
                nc.vector.tensor_reduce(neg_max[:, tt, h0:h0 + 4],
                                        score_bank[g % 2][:].rearrange("p (j k) -> p j k", k=128), AX.X, ALU.max,
                                        negate=True).then_inc(max_done, 1)

            def max_parts(at):
                dve.wait_ge(max_done, at.count(GROUPS, GROUPS))
                wait(dve, maxT_filled, at.count(1, 0))
                nc.vector.tensor_copy(max_part[:, :, 0, :], neg_max[:]).then_inc(max_step, 1)
                dve.wait_ge(max_step, at.count(2, 1))
                nc.vector.tensor_tensor(max_part[:, :, 1, :], neg_max[:], max_part[:, :, 0, :],
                                        ALU.subtract).then_inc(max_step, 1)

            def remote_bias(at):
                dve.wait_ge(remote_filled, at.count(1, 1))
                wait(dve, mixed, at.count(1, 0))
                nc.vector.tensor_tensor(remote[:], out_bank[:].rearrange("p (t d) -> p t d", t=2),
                                        b_rout[:].unsqueeze(1).to_broadcast([128, 2, D]),
                                        ALU.add).then_inc(remote_ready, 1)

            def add_to_x(at):
                dve.wait_ge(out_filled, at.count(1, 1))
                dve.wait_ge(xb_ready, at.count(1, 1))
                nc.vector.tensor_tensor(x_pair(at), out_bank[:].rearrange("p (t d) -> p t d", t=2), x_bias[:],
                                        ALU.add).then_inc(x_done, 1)

            def split_lat(at):
                dve.wait_ge(lat_evac, at.count(1, 1))
                wait(dve, lat_stacked[1 - at.par], at.back().turn(STACKED, STACKED))
                two = lat_raw[64:128, :].rearrange("p (l r) -> p l r", r=2)
                nc.vector.tensor_tensor(lat_f[64:128, 0:2 * LAT], two[:, :, 0], two[:, :, 1],
                                        ALU.add).then_inc(lat_ready, 1)
                dve.wait_ge(lat_ready, at.count(1, 1))
                split(at, 2, lat_f[:], lat_rest[:], [p[:] for p in lat_part])

            def bias_v(at, tt):
                src = proj_bank[1 - tt]
                dve.wait_ge(v_filled, at.count(2, tt + 1))
                if local:
                    nc.vector.tensor_tensor(v_heads[at.par][:, tt, :, 0:HD],
                                            src[:, 0:D].rearrange("p (h n) -> p h n", n=HD),
                                            b_v[:, 0:D].rearrange("p (h n) -> p h n", n=HD), ALU.add)
                    nc.vector.tensor_tensor(rv_heads[at.par][:, tt, :, 0:HD],
                                            src[:, D:].rearrange("p (h n) -> p h n", n=HD)[:, 0:LH, :],
                                            b_v[:, D:].rearrange("p (h n) -> p h n", n=HD),
                                            ALU.add).then_inc(v_ready, 1)
                else:
                    nc.vector.tensor_tensor(v_raw[:, tt, :], src[:, 0:D], b_v[:], ALU.add).then_inc(v_ready, 1)

            def gate_logits(at):
                dve.wait_ge(z_in, at.count(1, 1))
                wait(dve, tanh_ready, at.count(1, 0))
                nc.vector.tensor_reduce(gate_z[:].rearrange("p t h -> p (t h)"),
                                        tmp[1][:].rearrange("p t (h n) -> p (t h) n", n=HD), AX.X,
                                        ALU.add).then_inc(z_ready, 1)

            def gate_value(at):
                dve.wait_ge(tanh_ready, at.count(1, 1))
                wait(dve, mixed, at.count(1, 0))
                nc.vector.tensor_scalar(gate[:], gate_t[:], 0.5, 0.5, ALU.mult, ALU.add).then_inc(gate_ready, 1)

            def lat_center(at):
                src = back_bank[:].rearrange("p (h l) -> p h l", l=LAT)
                dve.wait_ge(ls_filled, at.count(1, 1))
                nc.vector.tensor_reduce(lat_max[:].rearrange("p t h -> p (t h)"), src, AX.X,
                                        ALU.max).then_inc(lmax_done, 1)
                dve.wait_ge(lmax_done, at.count(1, 1))
                wait(dve, lexp_done, at.count(1, 0))
                nc.vector.tensor_tensor(lat_s[:].rearrange("p t h l -> p (t h) l"), src,
                                        lat_max[:].rearrange("p t h -> p (t h)").unsqueeze(2)
                                        .to_broadcast([128, 2 * LH, LAT]), ALU.subtract).then_inc(lsub_done, 1)

            def lat_norm(at):
                dve.wait_ge(lexp_done, at.count(1, 1))
                nc.vector.tensor_reduce(lat_sum[:].rearrange("p t h -> p (t h)"),
                                        lat_p[:].rearrange("p t h l -> p (t h) l"), AX.X,
                                        ALU.add).then_inc(lsum_step, 1)
                dve.wait_ge(lsum_step, at.count(3, 1))
                nc.vector.reciprocal(lat_inv[:], lat_sum[:]).then_inc(lsum_step, 1)
                dve.wait_ge(lsum_step, at.count(3, 2))
                wait(dve, lp_ready, at.count(1, 0))
                nc.vector.tensor_scalar(lat_w[:], lat_inv[:], lat_rows[:, 0:1], None, ALU.mult).then_inc(lsum_step, 1)

            def step(at):
                prev, old = at.back(), at.back(2)
                following = At(at.i, at.off + 1)
                norms = at.real and not at.last
                for g in range(GROUPS):
                    if old.real and not local and g == 5:
                        dve.wait_ge(norm_step, old.count(2, 1))
                    if prev.real:
                        row_max(prev, g)
                    if old.real and g == 1:
                        normalise(old, 1)
                    if old.real and not local and g == 4:
                        dve.wait_ge(sum_ready, old.count(1, 1))
                        norm_stats(lambda tt: tmp[0][:, tt, :], norm_step)
                    if old.real and not local and g == 5:
                        norm_moments(norm_step)
                    if old.real and local and g == 5:
                        gate_logits(old)
                    if old.real and local and g == 6:
                        gate_value(old)
                if prev.real:
                    max_parts(prev)
                    if local:
                        lat_center(prev)
                if at.real:
                    wait(dve, stacked[1 - at.par], at.back().turn(STACKED, STACKED))
                    dve.wait_ge(q_ready, at.count(1, 1))
                    split(at, 0, qk_f[:, 0:2, :], qk_rest[:, 0:2, :], [p[:, 0:2, :] for p in qk_part])
                if local and prev.real:
                    lat_norm(prev)
                if not local and old.real:
                    dve.wait_ge(norm_scaled, old.count(1, 1))
                    wait(dve, x_done, old.count(1, 0))
                    norm_scale(lambda tt: tmp[0][:, tt, :], tmp[1], norm_ready)
                if norms:
                    x_stats(following)
                    dve.wait_ge(ln_step, following.count(2, 1))
                if at.real:
                    dve.wait_ge(k_ready, at.count(1, 1))
                    split(at, 1, qk_f[:, 2:4, :], qk_rest[:, 2:4, :], [p[:, 2:4, :] for p in qk_part])
                if norms:
                    norm_moments(ln_step)
                if local and at.real:
                    split_lat(at)
                if local and old.real:
                    add_to_x(old)
                if at.real:
                    wait(dve, av_filled if local else v_relu, at.count(GROUPS, -GROUPS) if local else at.count(2, 0))
                    bias_v(at, 0)
                    bias_v(at, 1)
                if norms:
                    x_scale(following)
                if prev.real:
                    normalise(prev, 0)
                    if local:
                        remote_bias(prev)

            x_stats(At(0, 0))
            dve.wait_ge(ln_step, 1)
            norm_moments(ln_step)
            x_scale(At(0, 0))
            pairs(dve, step, 2, ahead=1)

        @block.gpsimd
        def _(pool):
            def x_pair(at):
                return x_sb[:, bass.ds(at.i * 4 + 2 * at.off, 2), :]

            def one_over_deviation(at, step, with_eps, scaled):
                pool.wait_ge(step, at.count(2, 2))
                nc.gpsimd.tensor_tensor(var_eps[:], moments[:, :, 1], eps[:], ALU.add).then_inc(with_eps, 1)
                pool.wait_ge(with_eps, at.count(1, 1))
                nc.gpsimd.tensor_tensor(rstd[:], var_eps[:], minus_half[:], ALU.pow).then_inc(scaled, 1)

            def mask_weights(at, g):
                pool.wait_ge(exp_done, at.count(GROUPS, g + 1))
                pool.sem_inc(pool_turn, 1)
                pt = probs_t[g % 4]
                nc.gpsimd.affine_select(out=pt[:], in_=pt[:], pattern=[[0, 4], [1, 128]], compare_op=ALU.is_ge,
                                        fill=0.0, base=-1 if local else 0, channel_multiplier=-1).then_inc(masked, 1)

            def heads(x):
                return x[:].rearrange("p t (h n) -> p (t h) n", n=HD)

            def bias_x(at):
                wait(pool, x_done, at.count(1, 0))
                nc.gpsimd.tensor_tensor(x_bias[:], x_pair(at), b_out[:].unsqueeze(1).to_broadcast([128, 2, D]),
                                        ALU.add).then_inc(xb_ready, 1)

            def remote_terms(at):
                pool.wait_ge(remote_ready, at.count(1, 1))
                nc.gpsimd.tensor_tensor(heads(remote_g), heads(remote),
                                        gate_r[:].unsqueeze(1).to_broadcast([128, 2 * H, HD]),
                                        ALU.mult).then_inc(remote_gated, 1)

            def gate_terms(at):
                pool.wait_ge(attn_ready, at.count(2, 2))
                wait(pool, z_ready, at.count(1, 0))
                nc.gpsimd.tensor_tensor(heads(tmp[0]), heads(attn),
                                        gate_l[:].unsqueeze(1).to_broadcast([128, 2 * H, HD]),
                                        ALU.mult).then_inc(mix_step, 1)
                pool.wait_ge(mix_step, at.count(3, 1))
                pool.wait_ge(remote_gated, at.count(1, 1))
                nc.gpsimd.tensor_tensor(tmp[1][:], tmp[0][:], remote_g[:], ALU.add).then_inc(z_in, 1)
                nc.gpsimd.tensor_tensor(tmp[2][:], attn[:], remote[:], ALU.subtract).then_inc(mix_step, 1)

            def mix(at):
                pool.wait_ge(mix_step, at.count(3, 2))
                pool.wait_ge(gate_ready, at.count(1, 1))
                pool.wait_ge(z_in, at.count(1, 1))
                nc.gpsimd.tensor_tensor(heads(tmp[0]), heads(tmp[2]),
                                        gate[:].rearrange("p t h -> p (t h)").unsqueeze(2)
                                        .to_broadcast([128, 2 * H, HD]), ALU.mult).then_inc(mix_step, 1)
                pool.wait_ge(mix_step, at.count(3, 3))
                wait(pool, mixT_filled, at.count(1, 0))
                nc.gpsimd.tensor_tensor(tmp[3][:], tmp[0][:], remote[:], ALU.add).then_inc(mixed, 1)

            def add_normed(at):
                pool.wait_ge(attn_ready, at.count(2, 2))
                pool.wait_ge(qT_ready, at.count(1, 1))
                wait(pool, norm_ready, at.count(1, 0))
                nc.gpsimd.tensor_tensor(tmp[0][:], attn[:], q_tok[at.par][:], ALU.add).then_inc(sum_ready, 1)
                one_over_deviation(at, norm_step, norm_eps, norm_scaled)

            def scale_normed(at):
                pool.wait_ge(norm_ready, at.count(1, 1))
                nc.gpsimd.tensor_tensor(tmp[2][:], tmp[1][:], gamma[:].unsqueeze(1).to_broadcast([128, 2, D]),
                                        ALU.mult).then_inc(mix_step, 1)
                pool.wait_ge(mix_step, at.count(2, 1))
                nc.gpsimd.tensor_tensor(tmp[3][:], tmp[2][:], beta[:].unsqueeze(1).to_broadcast([128, 2, D]),
                                        ALU.add).then_inc(mix_step, 1)
                pool.wait_ge(mix_step, at.count(2, 2))
                nc.gpsimd.tensor_tensor(x_pair(at), x_pair(at), tmp[3][:], ALU.add).then_inc(x_done, 1)

            def lat_weights(at):
                pool.wait_ge(lsum_step, at.count(3, 3))
                wait(pool, lpT_filled, at.count(2, 0))
                nc.gpsimd.tensor_tensor(
                    lat_pd[:].rearrange("p t h l r -> p (t h) l r"),
                    lat_p[:].rearrange("p t h l -> p (t h) l").unsqueeze(3).to_broadcast([128, 2 * LH, LAT, 2]),
                    lat_w[:].rearrange("p t h -> p (t h)").unsqueeze(2).unsqueeze(3)
                    .to_broadcast([128, 2 * LH, LAT, 2]), ALU.mult).then_inc(lp_ready, 1)

            def step(at):
                prev, old = at.back(), at.back(2)
                if old.real:
                    if local:
                        remote_terms(old)
                        bias_x(old)
                        gate_terms(old)
                        mix(old)
                    else:
                        add_normed(old)
                if not local and old.real:
                    scale_normed(old)
                between = {}
                if at.real and not at.last:
                    between[3] = lambda: one_over_deviation(At(at.i, at.off + 1), ln_step, ln_eps, ln_scaled)
                if local and prev.real:
                    between[2] = lambda: lat_weights(prev)
                for g in range(GROUPS):
                    if g in between:
                        between[g]()
                    if prev.real:
                        mask_weights(prev, g)

            one_over_deviation(At(0, 0), ln_step, ln_eps, ln_scaled)
            pairs(pool, step, 2, ahead=1)


def slots(nc, scope, sem, a, out, bank, x_sb, ident):
    def sb(name, shape, dt=F32):
        return scope.enter_context(nc.sbuf_tensor(name, shape, dt))

    G = 3 * D
    PS = 2 * SLOTS
    NOT_CHOSEN = -3e38
    w1 = sb("w1", [128, 2 * C, 128])
    b1 = sb("b1", [128, 1])
    w2 = sb("w2", [128, SLOTS])
    b2 = sb("b2", [128, SLOTS])
    tau = sb("tau", [128, 1])
    tau_abs = sb("tau_abs", [128, 1])
    inv_tau = sb("inv_tau", [128, 1])
    w_ih = sb("w_ih", [128, C, G])
    w_hh = sb("w_hh", [128, C, G])
    b_ih = sb("b_ih", [128, G])
    b_hh = sb("b_hh", [128, G])
    wv = sb("wv", [128, C, D])
    wo = sb("wo", [128, C, D])
    bv = sb("bv", [128, C])
    bv_cols = sb("bv_cols", [128, C, 128])
    b_o = sb("b_o", [128, D])
    slot_init = sb("slot_init", [128, D])
    slot_scale = sb("slot_scale", [128, 1])
    slot0 = sb("slot0", [128, D])
    slot0_t = sb("slot0_t", [128, C, PS])
    mean_w = sb("mean_w", [SLOTS, 1])
    slot_mean = sb("slot_mean", [128, C])
    b1_all = sb("b1_all", [128, 1])
    h_gates = sb("h_gates", [128, G])
    rz_const = sb("rz_const", [128, 2 * D])
    half_hn = sb("half_hn", [128, D])
    n_const = sb("n_const", [128, D])
    w_vo = sb("w_vo", [128, C, D])
    b_vo = sb("b_vo", [128, D])

    stats = sb("f_stats", [128, 2, 6])
    moments = sb("f_moments", [128, 2, 2])
    var_eps = sb("f_var_eps", [128, 2])
    rstd = sb("f_rstd", [128, 2])
    minus_half = sb("f_minus_half", [128, 2])
    eps = sb("f_eps", [128, 2])
    XW = D + 1
    xn = [sb(f"f_xn{i}", [128, 2, XW]) for i in range(2)]
    xn_t = sb("f_xn_t", [128, C, PT])
    h_t = sb("h_t", [128, PT])
    logits = sb("logits", [128, 2, SLOTS])
    top = sb("top", [128, 2, TOPK])
    rest = sb("rest", [128, 2, SLOTS])
    neg_top = sb("neg_top", [128, 2])
    expd = sb("expd", [128, 2, SLOTS])
    chosen = sb("chosen", [128, 2, SLOTS])
    chosen_sum = sb("chosen_sum", [128, 2])
    chosen_inv = sb("chosen_inv", [128, 2])
    alpha = [sb(f"alpha{i}", [128, 2, PS]) for i in range(2)]
    alpha_t = [sb(f"alpha_t{i}", [128, 2, 128]) for i in range(2)]
    w_sum = sb("w_sum", [128, 1])
    w_inv = sb("w_inv", [128, 1])
    gi = sb("gi", [128, D])
    gi_t = sb("gi_t", [128, C, PS])
    rz = sb("rz", [128, 2 * D])
    rz_t = sb("rz_t", [128, 2 * D])
    r_hn = sb("r_hn", [128, D])
    r_hn_c = sb("r_hn_c", [128, D])
    n_in = sb("n_in", [128, D])
    n_out = sb("n_out", [128, D])
    h_n = sb("h_n", [128, D])
    z_hn = sb("z_hn", [128, D])
    slot_new = sb("slot_new", [128, D])
    slot_new_t = sb("slot_new_t", [128, C, PS])
    slot_val = sb("slot_val", [128, D])
    x_bias = sb("f_x_bias", [128, 2, D])
    y = [sb(f"y{i}", [128, 2, D]) for i in range(2)]

    loaded = sem("f_weights_loaded")
    prep_v, prep_p = sem("f_prep_dve"), sem("f_prep_pe")

    with nc.Block() as block:
        loads = [(w1, a["ffn_w1"]), (b1, a["ffn_b1"]), (w2, a["ffn_w2"]), (w_ih, a["ffn_w_ih"]), (w_hh, a["ffn_w_hh"]),
                 (wv, a["ffn_wv"]), (wo, a["ffn_wo"]), (bv, a["ffn_bv"])]
        rows = [(b2, a["ffn_b2"]), (tau, a["ffn_tau"]), (b_ih, a["ffn_b_ih"]), (b_hh, a["ffn_b_hh"]), (b_o, a["ffn_bo"])]

        @block.sync
        def _(sp):
            for tile, src in loads:
                sp.dma_start(tile[:], src).then_inc(loaded, 16)
            for tile, src in rows:
                sp.dma_start(tile[:], src.partition_broadcast(128)).then_inc(loaded, 16)
            for k in range(2):
                half = slice(SLOTS * k, SLOTS * k + SLOTS)
                sp.dma_start(slot_init[half, :], a["ffn_slot_init"]).then_inc(loaded, 16)
                sp.dma_start(slot_scale[half, :], a["ffn_slot_scale"]).then_inc(loaded, 16)
            sp.wait_ge(loaded, 16 * (len(loads) + len(rows) + 4))

        @block.vector
        def _(dve):
            nc.vector.memset(minus_half[:], -0.5)
            nc.vector.memset(eps[:], LN_EPS)
            nc.vector.memset(mean_w[:], 1.0 / SLOTS).then_inc(prep_v, 1)
            for k in range(2):
                nc.vector.memset(alpha[k][:], 0.0).then_inc(prep_v, 1)
                nc.vector.memset(xn[k][:, :, D:XW], 1.0).then_inc(prep_v, 1)
            dve.wait_ge(loaded, 16 * (len(loads) + len(rows) + 4))
            nc.vector.tensor_scalar(slot0[:], slot_init[:], slot_scale[:, 0:1], None, ALU.mult).then_inc(prep_v, 1)
            nc.vector.tensor_copy(bv_cols[:], bv[:].unsqueeze(2).to_broadcast([128, C, 128])).then_inc(prep_v, 1)
            nc.vector.scalar_tensor_tensor(tau_abs[:], tau[:], -1.0, tau[:], ALU.mult, ALU.max).then_inc(prep_v, 1)
            dve.wait_ge(prep_v, 8)
            nc.vector.tensor_scalar(tau_abs[:], tau_abs[:], 0.1, None, ALU.add).then_inc(prep_v, 1)
            dve.wait_ge(prep_v, 9)
            nc.vector.reciprocal(inv_tau[:], tau_abs[:]).then_inc(prep_v, 1)
            dve.wait_ge(prep_v, 10)
            nc.vector.tensor_scalar(b2[:], b2[:], inv_tau[:, 0:1], None, ALU.mult).then_inc(prep_v, 1)
            dve.wait_ge(prep_p, 1)
            nc.vector.tensor_copy(slot0_t[:].rearrange("p c n -> p (c n)"), bank[0][:, 0:C * PS]).then_inc(prep_v, 1)
            dve.wait_ge(prep_p, 2)
            nc.vector.tensor_copy(slot_mean[:], bank[1][:, 0:C]).then_inc(prep_v, 1)
            dve.wait_ge(prep_p, 3)
            nc.vector.tensor_tensor(b1_all[:], bank[2][:, 0:1], b1[:], ALU.add).then_inc(prep_v, 1)
            dve.wait_ge(prep_p, 4)
            nc.vector.tensor_tensor(h_gates[:, 0:512], bank[3][:], b_hh[:, 0:512], ALU.add).then_inc(prep_v, 1)
            nc.vector.tensor_tensor(h_gates[:, 512:G], bank[4][:, 0:G - 512], b_hh[:, 512:G], ALU.add).then_inc(prep_v, 1)
            dve.wait_ge(prep_v, 16)
            nc.vector.tensor_tensor(rz_const[:], h_gates[:, 0:2 * D], b_ih[:, 0:2 * D], ALU.add).then_inc(prep_v, 1)
            nc.vector.tensor_scalar(half_hn[:], h_gates[:, 2 * D:G], 0.5, None, ALU.mult).then_inc(prep_v, 1)
            dve.wait_ge(prep_v, 18)
            nc.vector.tensor_tensor(n_const[:], half_hn[:], b_ih[:, 2 * D:G], ALU.add).then_inc(prep_v, 1)
            dve.wait_ge(prep_p, 5)
            nc.vector.tensor_copy(w_vo[:].rearrange("p c n -> p (c n)"), bank[5][:, 0:C * D]).then_inc(prep_v, 1)
            nc.vector.tensor_copy(b_vo[:], bank[6][:, 0:D]).then_inc(prep_v, 1)
            dve.wait_ge(prep_v, 21)

        @block.tensor
        def _(pe):
            pe.wait_ge(prep_v, 6)
            for c in range(C):
                mm = pe.transpose(bank[0][:, PS * c:PS * c + PS], slot0[:, 128 * c:128 * c + 128], ident[:])
            mm.then_inc(prep_p, 1)
            for c in range(C):
                mm = pe.matmul(bank[1][:, c:c + 1], slot0[0:SLOTS, 128 * c:128 * c + 128], mean_w[:],
                               start=True, stop=True, skip_group_check=True)
            mm.then_inc(prep_p, 1)
            pe.wait_ge(prep_v, 13)
            for c in range(C):
                mm = pe.matmul(bank[2][:, 0:1], w1[:, C + c, :], slot_mean[:, c:c + 1], start=(c == 0), stop=(c == C - 1))
            mm.then_inc(prep_p, 1)
            for lo, hi, b in ((0, 512, 3), (512, G, 4)):
                for c in range(C):
                    mm = pe.matmul(bank[b][:, 0:hi - lo], slot0_t[:, c, :], w_hh[:, c, lo:hi], start=(c == 0), stop=(c == C - 1))
            mm.then_inc(prep_p, 1)
            for d in range(C):
                for c in range(C):
                    pe.matmul(bank[5][:, D * d:D * d + D], wv[:, c, 128 * d:128 * d + 128], wo[:, c, :],
                              start=(c == 0), stop=(c == C - 1), skip_group_check=True)
            for c in range(C):
                mm = pe.matmul(bank[6][:, 0:D], bv_cols[:, c, :], wo[:, c, :], start=(c == 0), stop=(c == C - 1))
            mm.then_inc(prep_p, 1)

    tr_bank, hid_bank, logit_bank, in_bank, gate_bank, new_bank, out_bank = (
        bank[0], bank[1], bank[2], bank[3], bank[4:6], bank[6], bank[7])

    def s(name):
        return sem(f"f_{name}")

    ln_eps, ln_scaled = s("ln_eps"), s("ln_scaled")
    ln_step, xn_ready, xnT_filled, xnT_ready = s("ln_step"), s("xn_ready"), s("xnT_filled"), s("xnT_ready")
    hid_filled, hid_ready, logit_filled, logit_ready = s("hid_filled"), s("hid_ready"), s("logit_filled"), s("logit_ready")
    top_ready, negtop_ready, exp_ready = s("top_ready"), s("negtop_ready"), s("exp_ready")
    pick_step, alpha_ready, alphaT_filled, alphaT_ready = s("pick_step"), s("alpha_ready"), s("alphaT_filled"), s("alphaT_ready")
    in_filled, in_step, giT_filled, giT_ready = s("in_filled"), s("in_step"), s("giT_filled"), s("giT_ready")
    gate_filled, rz_ready, rz_tanh, rhn_step, rhn_ready = s("gate_filled"), s("rz_ready"), s("rz_tanh"), s("rhn_step"), s("rhn_ready")
    n_in_ready, n_ready, hn_ready, zhn_ready, slot_ready = s("n_in_ready"), s("n_ready"), s("hn_ready"), s("zhn_ready"), s("slot_ready")
    newT_filled, newT_ready, val_filled, val_ready = s("newT_filled"), s("newT_ready"), s("val_filled"), s("val_ready")
    out_filled, xb_ready, y_ready = s("out_filled"), s("xb_ready"), s("y_ready")
    stored = [s(f"stored{i}") for i in range(2)]

    dest = out.rearrange("s p d -> p s d")
    LAST = 2

    def stages(at):
        drains = isinstance(at.i, int) and at.off >= NPAIR
        route = None if drains else at
        feed = at.back() if at.off >= 1 and not (drains and at.off > NPAIR) else None
        give = at.back(2) if at.off >= 2 else None
        return route, feed, give

    with nc.Block() as block:

        @block.sync
        def _(sp):
            def step(at):
                route, feed, give = stages(at)
                if give:
                    sp.wait_ge(y_ready, give.count(1, 1))
                    sp.dma_start(dest[:, bass.ds(give.i * 4 + 2 * give.off, 2), :],
                                 y[give.par][:]).then_inc(stored[give.par], 16)

            pairs(sp, step, LAST)
            for k in range(2):
                sp.wait_ge(stored[k], 16 * (NPAIR // 2))

        @block.tensor
        def _(pe):
            def step(at):
                route, feed, give = stages(at)
                if route:
                    pe.wait_ge(xn_ready, route.count(1, 1))
                    wait(pe, xnT_ready, route.count(1, 0))
                    for tt in range(2):
                        for c in range(C):
                            mm = pe.transpose(tr_bank[:, c * PT + tt * S:c * PT + tt * S + S],
                                              xn[route.par][:, tt, 128 * c:128 * c + 128], ident[:])
                    mm.then_inc(xnT_filled, 1)
                if feed:
                    pe.wait_ge(alpha_ready, feed.count(2, 2))
                    wait(pe, giT_ready, feed.count(1, 0))
                    for tt in range(2):
                        half = slice(SLOTS * tt, SLOTS * tt + SLOTS)
                        mm = pe.matmul(in_bank[half, 0:XW], alpha[feed.par][:, tt, half], xn[feed.par][:, tt, :],
                                       start=True, stop=True, skip_group_check=True)
                    mm.then_inc(in_filled, 1)
                if give:
                    pe.wait_ge(slot_ready, give.count(1, 1))
                    wait(pe, val_ready, give.count(1, 0))
                    for c in range(C):
                        mm = pe.transpose(new_bank[:, PS * c:PS * c + PS], slot_new[:, 128 * c:128 * c + 128], ident[:])
                    mm.then_inc(newT_filled, 1)
                if route:
                    pe.wait_ge(xnT_ready, route.count(1, 1))
                    wait(pe, hid_ready, route.count(1, 0))
                    for c in range(C):
                        mm = pe.matmul(hid_bank[:, 0:PT], w1[:, c, :], xn_t[:, c, :], start=(c == 0), stop=(c == C - 1))
                    mm.then_inc(hid_filled, 1)
                if feed:
                    wait(pe, y_ready, feed.count(1, -1))
                    for tt in range(2):
                        mm = pe.transpose(out_bank[:, 128 * tt:128 * tt + 128], alpha[feed.par][:, tt, :], ident[:])
                    mm.then_inc(alphaT_filled, 1)
                    pe.wait_ge(in_step, feed.count(3, 3))
                    for c in range(C):
                        mm = pe.transpose(in_bank[:, PS * c:PS * c + PS], gi[:, 128 * c:128 * c + 128], ident[:])
                    mm.then_inc(giT_filled, 1)
                if give:
                    pe.wait_ge(newT_ready, give.count(1, 1))
                    for c in range(C):
                        mm = pe.matmul(new_bank[:, 0:D], slot_new_t[:, c, :], w_vo[:, c, :], start=(c == 0), stop=(c == C - 1))
                    mm.then_inc(val_filled, 1)
                if route:
                    pe.wait_ge(hid_ready, route.count(1, 1))
                    wait(pe, logit_ready, route.count(1, 0))
                    for tt in range(2):
                        mm = pe.matmul(logit_bank[:, SLOTS * tt:SLOTS * tt + SLOTS], h_t[:, S * tt:S * tt + S], w2[:],
                                       start=True, stop=True, skip_group_check=True)
                    mm.then_inc(logit_filled, 1)
                if feed:
                    pe.wait_ge(giT_ready, feed.count(1, 1))
                    wait(pe, n_in_ready, feed.count(1, 0))
                    for lo, hi, b in ((0, 2 * D, 0), (2 * D, G, 1)):
                        for c in range(C):
                            mm = pe.matmul(gate_bank[b][:, 0:hi - lo], gi_t[:, c, :], w_ih[:, c, lo:hi],
                                           start=(c == 0), stop=(c == C - 1))
                    mm.then_inc(gate_filled, 1)
                if give:
                    pe.wait_ge(val_ready, give.count(1, 1))
                    last = 2 if feed else 1
                    pe.wait_ge(alphaT_ready, give.count(1, last))
                    for tt in range(2):
                        mm = pe.matmul(out_bank[:, D * tt:D * tt + D], alpha_t[give.par][:, tt, :], slot_val[:],
                                       start=True, stop=True, skip_group_check=True)
                    mm.then_inc(out_filled, 1)

            pairs(pe, step, LAST)

        @block.scalar
        def _(act):
            def step(at):
                route, feed, give = stages(at)
                if route:
                    act.wait_ge(xnT_filled, route.count(1, 1))
                    wait(act, hid_filled, route.count(1, 0))
                    nc.scalar.activation(xn_t[:].rearrange("p c t -> p (c t)"), tr_bank[:], ACT.Copy).then_inc(xnT_ready, 1)
                if give:
                    act.wait_ge(newT_filled, give.count(1, 1))
                    wait(act, val_filled, give.count(1, 0))
                    nc.scalar.activation(slot_new_t[:].rearrange("p c n -> p (c n)"), new_bank[:, 0:C * PS],
                                         ACT.Copy).then_inc(newT_ready, 1)
                if route:
                    act.wait_ge(hid_filled, route.count(1, 1))
                    wait(act, logit_filled, route.count(1, 0))
                    nc.scalar.activation(h_t[:], hid_bank[:, 0:PT], ACT.Gelu, bias=b1_all[:, 0:1]).then_inc(hid_ready, 1)
                if feed:
                    act.wait_ge(alphaT_filled, feed.count(1, 1))
                    wait(act, out_filled, feed.count(1, -1))
                    nc.scalar.activation(alpha_t[feed.par][:].rearrange("p t n -> p (t n)"), out_bank[:, 0:256],
                                         ACT.Copy).then_inc(alphaT_ready, 1)
                    act.wait_ge(giT_filled, feed.count(1, 1))
                    wait(act, gate_filled, feed.count(1, 0))
                    nc.scalar.activation(gi_t[:].rearrange("p c n -> p (c n)"), in_bank[:, 0:C * PS],
                                         ACT.Copy).then_inc(giT_ready, 1)
                if route:
                    act.wait_ge(negtop_ready, route.count(1, 1))
                    wait(act, alpha_ready, route.count(2, 0))
                    for tt in range(2):
                        ins = nc.scalar.activation(expd[:, tt, :], logits[:, tt, :], ACT.Exp, bias=neg_top[:, tt:tt + 1])
                    ins.then_inc(exp_ready, 1)
                if feed:
                    act.wait_ge(rz_ready, feed.count(1, 1))
                    wait(act, slot_ready, feed.count(1, 0))
                    nc.scalar.activation(rz_t[:], rz[:], ACT.Tanh, scale=0.5).then_inc(rz_tanh, 1)
                    act.wait_ge(n_in_ready, feed.count(1, 1))
                    wait(act, slot_ready, feed.count(1, 0))
                    nc.scalar.activation(n_out[:], n_in[:], ACT.Tanh).then_inc(n_ready, 1)

            pairs(act, step, LAST)

        @block.vector
        def _(dve):
            def x_rows(at, tt):
                return x_sb[:, bass.ds(at.i * 4 + 2 * at.off + tt, 1), :].rearrange("p s d -> p (s d)")

            def norm_stats(at):
                for tt in range(2):
                    ins = nc.vector.bn_stats(stats[:, tt, :], x_rows(at, tt))
                ins.then_inc(ln_step, 1)

            def norm_moments():
                for tt in range(2):
                    ins = nc.vector.bn_aggr(moments[:, tt, :], stats[:, tt, :])
                ins.then_inc(ln_step, 1)

            def norm_scale(at):
                dve.wait_ge(ln_scaled, at.count(1, 1))
                wait(dve, in_filled, at.count(1, -1))
                for tt in range(2):
                    ins = nc.vector.tensor_scalar(xn[at.par][:, tt, 0:D], x_rows(at, tt), moments[:, tt, 0:1],
                                                  rstd[:, tt:tt + 1], ALU.subtract, ALU.mult)
                ins.then_inc(xn_ready, 1)

            def step(at):
                route, feed, give = stages(at)
                if feed:
                    dve.wait_ge(in_filled, feed.count(1, 1))
                    nc.vector.tensor_scalar(w_sum[:], in_bank[:, D:XW], 1e-8, None, ALU.add).then_inc(in_step, 1)
                    dve.wait_ge(in_step, feed.count(3, 1))
                    nc.vector.reciprocal(w_inv[:], w_sum[:]).then_inc(in_step, 1)
                    dve.wait_ge(in_step, feed.count(3, 2))
                    wait(dve, giT_filled, feed.count(1, 0))
                    nc.vector.tensor_scalar(gi[:], in_bank[:, 0:D], w_inv[:, 0:1], None, ALU.mult).then_inc(in_step, 1)
                if give:
                    dve.wait_ge(val_filled, give.count(1, 1))
                    wait(dve, out_filled, give.count(1, 0))
                    nc.vector.tensor_tensor(slot_val[:], new_bank[:, 0:D], b_vo[:], ALU.add).then_inc(val_ready, 1)
                after = None
                if route and not (isinstance(at.i, int) and at.off == NPAIR - 1):
                    after = At(at.i, at.off + 1)
                    norm_stats(after)
                    dve.wait_ge(ln_step, after.count(2, 1))
                if route:
                    dve.wait_ge(logit_filled, route.count(1, 1))
                    wait(dve, exp_ready, route.count(1, 0))
                    nc.vector.scalar_tensor_tensor(logits[:], logit_bank[:, 0:2 * SLOTS].rearrange("p (t n) -> p t n", t=2),
                                                   inv_tau[:, 0:1], b2[:].unsqueeze(1).to_broadcast([128, 2, SLOTS]),
                                                   ALU.mult, ALU.add).then_inc(logit_ready, 1)
                    if after:
                        norm_moments()
                    dve.wait_ge(logit_ready, route.count(1, 1))
                    if after:
                        norm_scale(after)
                    for tt in range(2):
                        ins = nc.vector.max(top[:, tt, :], logits[:, tt, :])
                    ins.then_inc(top_ready, 1)
                    dve.wait_ge(top_ready, route.count(1, 1))
                    nc.vector.tensor_scalar(neg_top[:], top[:, :, 0], -1.0, None, ALU.mult).then_inc(negtop_ready, 1)
                    for tt in range(2):
                        ins = nc.vector.match_replace(rest[:, tt, :], top[:, tt, :], logits[:, tt, :], NOT_CHOSEN)
                    ins.then_inc(pick_step, 1)
                    dve.wait_ge(pick_step, route.count(4, 1))
                    dve.wait_ge(exp_ready, route.count(1, 1))
                    for tt in range(2):
                        ins = nc.vector.scalar_tensor_tensor(chosen[:, tt, :], rest[:, tt, :], NOT_CHOSEN, expd[:, tt, :],
                                                             ALU.is_le, ALU.mult)
                    ins.then_inc(pick_step, 1)
                    dve.wait_ge(pick_step, route.count(4, 2))
                    nc.vector.tensor_reduce(chosen_sum[:], chosen[:], AX.X, ALU.add).then_inc(pick_step, 1)
                    dve.wait_ge(pick_step, route.count(4, 3))
                    nc.vector.reciprocal(chosen_inv[:], chosen_sum[:]).then_inc(pick_step, 1)
                    dve.wait_ge(pick_step, route.count(4, 4))
                    wait(dve, alphaT_filled, route.count(1, -1))
                    for tt in range(2):
                        nc.vector.tensor_scalar(alpha[route.par][:, tt, SLOTS * tt:SLOTS * tt + SLOTS], chosen[:, tt, :],
                                                chosen_inv[:, tt:tt + 1], None, ALU.mult).then_inc(alpha_ready, 1)
                if feed:
                    dve.wait_ge(gate_filled, feed.count(1, 1))
                    wait(dve, rz_tanh, feed.count(1, 0))
                    nc.vector.tensor_tensor(rz[:], gate_bank[0][:], rz_const[:], ALU.add).then_inc(rz_ready, 1)
                if give:
                    dve.wait_ge(out_filled, give.count(1, 1))
                    dve.wait_ge(xb_ready, give.count(1, 1))
                    wait(dve, stored[give.par], give.turn(16, 0))
                    nc.vector.tensor_tensor(y[give.par][:], out_bank[:].rearrange("p (t d) -> p t d", t=2), x_bias[:],
                                            ALU.add).then_inc(y_ready, 1)
                if feed:
                    dve.wait_ge(rhn_ready, feed.count(1, 1))
                    wait(dve, n_ready, feed.count(1, 0))
                    nc.vector.tensor_tensor(n_in[:], gate_bank[1][:, 0:D], r_hn_c[:], ALU.add).then_inc(n_in_ready, 1)
                    dve.wait_ge(hn_ready, feed.count(1, 1))
                    nc.vector.scalar_tensor_tensor(z_hn[:], rz_t[:, D:2 * D], 1.0, h_n[:], ALU.add,
                                                   ALU.mult).then_inc(zhn_ready, 1)
                    dve.wait_ge(zhn_ready, feed.count(1, 1))
                    wait(dve, newT_filled, feed.count(1, 0))
                    nc.vector.scalar_tensor_tensor(slot_new[:], z_hn[:], 0.5, n_out[:], ALU.mult,
                                                   ALU.add).then_inc(slot_ready, 1)

            norm_stats(At(0, 0))
            dve.wait_ge(ln_step, 1)
            norm_moments()
            norm_scale(At(0, 0))
            pairs(dve, step, LAST, ahead=1)

        @block.gpsimd
        def _(pool):
            def one_over_deviation(at, step, with_eps, scaled):
                pool.wait_ge(step, at.count(2, 2))
                nc.gpsimd.tensor_tensor(var_eps[:], moments[:, :, 1], eps[:], ALU.add).then_inc(with_eps, 1)
                pool.wait_ge(with_eps, at.count(1, 1))
                nc.gpsimd.tensor_tensor(rstd[:], var_eps[:], minus_half[:], ALU.pow).then_inc(scaled, 1)

            def step(at):
                route, feed, give = stages(at)
                if give:
                    wait(pool, y_ready, give.count(1, 0))
                    nc.gpsimd.tensor_tensor(x_bias[:], x_sb[:, bass.ds(give.i * 4 + 2 * give.off, 2), :],
                                            b_o[:].unsqueeze(1).to_broadcast([128, 2, D]), ALU.add).then_inc(xb_ready, 1)
                if route and not (isinstance(at.i, int) and at.off == NPAIR - 1):
                    one_over_deviation(At(at.i, at.off + 1), ln_step, ln_eps, ln_scaled)
                if feed:
                    pool.wait_ge(rz_tanh, feed.count(1, 1))
                    nc.gpsimd.tensor_tensor(r_hn[:], rz_t[:, 0:D], half_hn[:], ALU.mult).then_inc(rhn_step, 1)
                    pool.wait_ge(rhn_step, feed.count(1, 1))
                    wait(pool, n_in_ready, feed.count(1, 0))
                    nc.gpsimd.tensor_tensor(r_hn_c[:], r_hn[:], n_const[:], ALU.add).then_inc(rhn_ready, 1)
                    pool.wait_ge(n_ready, feed.count(1, 1))
                    wait(pool, zhn_ready, feed.count(1, 0))
                    nc.gpsimd.tensor_tensor(h_n[:], slot0[:], n_out[:], ALU.subtract).then_inc(hn_ready, 1)

            one_over_deviation(At(0, 0), ln_step, ln_eps, ln_scaled)
            pairs(pool, step, LAST, ahead=1)


def kernel(**inputs):
    import numpy as np
    import concourse.bacc as bacc
    from concourse import mybir as mb
    from concourse.bass_utils import run_bass_kernel_spmd

    given = {k: np.asarray(v) for k, v in inputs.items()}

    def attn(name):
        return given["L0_attn_" + name]

    def xattn(name):
        return given["L0_xattn_" + name]

    def ffn(name):
        return given["L0_ffn_" + name]

    def by_heads(w):
        return w.reshape(*w.shape[:-1], H // 2, 2, HD).swapaxes(-3, -2).swapaxes(-2, -1)

    def by_latent_heads(w):
        return w.reshape(*w.shape[:-1], LH, HD).swapaxes(-2, -1).reshape(*w.shape)

    def chunks(w):
        return w.reshape(w.shape[0] // 128, 128, -1).swapaxes(0, 1)

    def qk_weight(wq, wk):
        w = np.stack([by_heads(wq), by_heads(wk)], axis=1)
        return chunks(w.reshape(D, -1)).reshape(128, C, 4, 128)

    def qk_bias(bq, bk):
        return np.stack([by_heads(bq), by_heads(bk)]).reshape(4, 128).T

    w, bias, lat = attn("qkv_w"), attn("qkv_b"), LH * HD
    laid = {
        "x": given["x"], "ctx": given["ctx_1024"],
        "attn_qk_w": qk_weight(w[:, 0:D], w[:, D:2 * D]),
        "attn_qk_b": qk_bias(bias[0:D], bias[D:2 * D]),
        "attn_v_w": chunks(np.concatenate([w[:, 2 * D:], attn("rkv_w")[:, lat:]], axis=1)),
        "attn_v_b": np.concatenate([bias[2 * D:], attn("rkv_b")[lat:]]),
        "lat_w": chunks(np.concatenate([by_latent_heads(attn("rq_w")), by_latent_heads(attn("rkv_w")[:, :lat])], axis=1)),
        "lat_b": np.concatenate([by_latent_heads(attn("rq_b")), by_latent_heads(attn("rkv_b")[:lat])]).reshape(128, 1),
        "attn_rout_w": attn("rout_w"), "attn_rout_b": attn("rout_b"),
        "attn_out_w": chunks(attn("out_w")), "attn_out_b": attn("out_b"),
        "attn_gl_w": attn("gl_w").reshape(-1), "attn_gr_w": attn("gr_w").reshape(-1),
        "xattn_qk_w": qk_weight(xattn("Wq"), xattn("Wk")),
        "xattn_qk_b": qk_bias(xattn("bq"), xattn("bk")),
        "xattn_v_w": chunks(xattn("Wv")), "xattn_v_b": xattn("bv"),
        "xattn_gamma": xattn("gamma"), "xattn_beta": xattn("beta"),
        "ffn_slot_init": ffn("slot_init"), "ffn_slot_scale": ffn("slot_scale"),
        "ffn_w1": chunks(ffn("w1").T), "ffn_b1": ffn("b1").reshape(128, 1),
        "ffn_w2": ffn("w2").T, "ffn_b2": ffn("b2"), "ffn_tau": ffn("tau"),
        "ffn_w_ih": chunks(ffn("gru_wih").T), "ffn_w_hh": chunks(ffn("gru_whh").T),
        "ffn_b_ih": ffn("gru_bih"), "ffn_b_hh": ffn("gru_bhh"),
        "ffn_wv": chunks(ffn("wv")), "ffn_wo": chunks(ffn("wo").T),
        "ffn_bv": ffn("bv").reshape(C, 128).T, "ffn_bo": ffn("bo"),
    }
    nc = bacc.Bacc("TRN2", target_bir_lowering=False, num_devices=1)
    arrays, args = {}, {}
    for name, value in laid.items():
        value = np.ascontiguousarray(value)
        arrays[f"in_{name}"] = value
        args[name] = nc.dram_tensor(f"in_{name}", value.shape, mb.dt.from_np(value.dtype), kind="ExternalInput").ap()
    out = nc.dram_tensor("out", (B, S, D), mb.dt.float32, kind="ExternalOutput").ap()
    decoder(nc, args, out)
    return run_bass_kernel_spmd(nc, [arrays], core_ids=[0]).results[0]["out"]
```

```python
from contextlib import ExitStack

import concourse.bass as bass
from concourse import mybir

F32 = mybir.dt.float32
BF16 = mybir.dt.bfloat16
ALU = mybir.AluOpType
ACT = mybir.ActivationFunctionType
AX = mybir.AxisListType

B, S, D = 64, 128, 256
C = D // 128
H, HD = 16, 16
LH, LAT = 4, S // 2
HW = 32
ONE = HD + 1
VW = H * (HD + 1)
NPAIR = B // 2
PT = 2 * S
GROUPS = 8
NPROD = 6
SPLIT = NPROD * HD
STACK = SPLIT + 2
SLOTS, TOPK = 64, 8
LN_EPS = 1e-5
NEG = -1e30
MADE = 13
SCALE = float(HD) ** -0.5

Q_PART = (0, 0, 1, 1, 0, 2)
K_PART = (0, 1, 0, 1, 2, 0)


class At:

    def __init__(self, i, off, by=2):
        self.i, self.off, self.by = i, off, by

    @property
    def row(self):
        return self.i * (2 * self.by) + 2 * self.off

    @property
    def par(self):
        return self.off % 2

    def back(self, k=1):
        return At(self.i, self.off - k, self.by)

    @property
    def real(self):
        return not isinstance(self.i, int) or 0 <= self.off < NPAIR

    @property
    def last(self):
        return isinstance(self.i, int) and self.off == NPAIR - 1

    def count(self, per, k):
        return self.i * (self.by * per) + (self.off * per + k)

    def turn(self, per, k):
        return self.i * (self.by // 2 * per) + (self.off // 2 * per + k)


def wait(eng, sem, value):
    if isinstance(value, int) and value <= 0:
        return
    eng.wait_ge(sem, value)


def pairs(eng, step, last, ahead=0, by=2):
    for k in range(2 * by):
        step(At(0, k))
    with eng.Fori(0, (NPAIR - 2 * by - ahead * by) // by) as i:
        for k in range(by):
            step(At(i, 2 * by + k, by))
    for k in range(NPAIR - ahead * by, NPAIR + last):
        step(At(0, k))


def decoder(nc, a, out):
    with ExitStack() as ctx:
        def sem(name):
            return ctx.enter_context(nc.semaphore(name))

        def sb(name, shape, dt=F32):
            return ctx.enter_context(nc.sbuf_tensor(name, shape, dt))

        bank = [ctx.enter_context(nc.psum_tensor(f"bank{b}", [128, 512], F32)) for b in range(8)]
        x_sb = sb("x_sb", [128, B, D])
        ident = sb("ident", [128, 128])
        ident_bf = sb("ident_bf", [128, 128], BF16)
        with ExitStack() as scope:
            attentions(nc, scope, sem, a, bank, x_sb, ident, ident_bf)
        with ExitStack() as scope:
            slots(nc, scope, sem, a, out, bank, x_sb, ident)


def attentions(nc, scope, sem, a, bank, x_sb, ident, ident_bf):
    def sb(name, shape, dt=F32):
        return scope.enter_context(nc.sbuf_tensor(name, shape, dt))

    w_qk = [sb(f"w_qk_{p}", [128, C, 4, 128]) for p in "ab"]
    b_qk = [sb(f"b_qk_{p}", [128, 4]) for p in "ab"]
    w_v = [sb("w_v_a", [128, C, VW + LH * HD]), sb("w_v_b", [128, C, D])]
    b_v = [sb("b_v_a", [128, VW + LH * HD]), sb("b_v_b", [128, D])]
    w_lat = sb("w_lat", [128, C, 128])
    b_lat = sb("b_lat", [128, 1])
    w_rout = sb("w_rout", [128, D + H])
    w_out = sb("w_out", [128, C, D])
    b_out = sb("b_out", [128, D])
    gate_l = sb("gate_l", [128, HD])
    gate_r = sb("gate_r", [128, HD])
    gamma = sb("gamma", [128, D])
    beta = sb("beta", [128, D])
    ones_sq = sb("ones_sq", [128, 128])
    mask = [sb(f"mask_{p}", [128, 4, 128], BF16) for p in "ab"]
    mask_lat = sb("mask_lat", [128, LH, LAT], BF16)
    lat_rows = sb("lat_rows", [128, 1])

    stats = sb("stats", [128, 2, 6])
    moments = sb("moments", [128, 2, 2])
    var_eps = sb("var_eps", [128, 2])
    out_stats = sb("out_stats", [128, 2, 6])
    out_moments = sb("out_moments", [128, 2, 2])
    out_var_eps = sb("out_var_eps", [128, 2])
    out_rstd = sb("out_rstd", [128, 2])
    rstd = sb("rstd", [128, 2])
    minus_half = sb("minus_half", [128, 2])
    eps = sb("eps", [128, 2])
    xn = sb("xn", [128, 2, D])
    xn_t = sb("xn_t", [128, C, PT])
    qk_f = sb("qk_f", [128, 4, PT])
    qk_rest = sb("qk_rest", [128, 4, PT])
    qk_part = [sb(f"qk_part{i}", [128, 4, PT], BF16) for i in range(3)]
    lat_f = sb("lat_f", [128, PT])
    lat_raw = sb("lat_raw", [128, PT])
    lat_rest = sb("lat_rest", [128, PT])
    lat_part = [sb(f"lat_part{i}", [128, PT], BF16) for i in range(3)]
    q_stack = [sb(f"q_stack{i}", [128, H, PT], BF16) for i in range(2)]
    k_stack = [sb(f"k_stack{i}", [128, H, PT], BF16) for i in range(2)]
    rq_stack = [sb(f"rq_stack{i}", [128, LH, PT], BF16) for i in range(2)]
    rk_stack = [sb(f"rk_stack{i}", [128, LH, 2 * LAT], BF16) for i in range(2)]
    v_heads = [sb(f"v_heads{i}", [128, 2, H, HW]) for i in range(2)]
    rv_heads = [sb(f"rv_heads{i}", [128, 2, LH, HW]) for i in range(2)]
    neg_max = sb("neg_max", [128, 2, H])
    max_part = sb("max_part", [128, 2, 2, H], BF16)
    max_t = sb("max_t", [2 * H, PT], BF16)
    probs_t = [sb(f"probs_t{i}", [128, 4, 128]) for i in range(4)]
    av_t = [sb(f"av_t{i}", [128, 4, 128]) for i in range(2)]
    sums = sb("sums", [128, 2, H])
    inv = sb("inv", [128, 2, H])
    attn = sb("attn", [128, 2, D])
    lat_max = sb("lat_max", [128, 2, LH])
    lat_s = sb("lat_s", [128, 2, LH, LAT])
    lat_p = sb("lat_p", [128, 2, LH, LAT])
    lat_sum = sb("lat_sum", [128, 2, LH])
    lat_inv = sb("lat_inv", [128, 2, LH])
    lat_w = sb("lat_w", [128, 2, LH])
    lat_pd = sb("lat_pd", [128, 2, LH, LAT, 2])
    lat_pt = [sb(f"lat_pt{i}", [128, LH, 128]) for i in range(2)]
    lat_out = sb("lat_out", [128, PT])
    remote = sb("remote", [128, 2, D])
    remote_g = sb("remote_g", [128, 2, D])
    tmp = [sb(f"tmp{i}", [128, 2, D]) for i in range(4)]
    z_local = sb("z_local", [128, 2, H])
    z_remote = sb("z_remote", [128, 2, H])
    gate_z = sb("gate_z", [128, 2, H])
    gate_t = sb("gate_t", [128, 2, H])
    gate = sb("gate", [128, 2, H])
    mix_t = sb("mix_t", [128, 2, C, 128])
    x_bias = sb("x_bias", [128, 2, D])
    ctx_in = [x[:].rearrange("p t h l -> p t (h l)") for x in (lat_s, lat_p)]
    ctx_t, v_raw = remote_g[:], remote[:]
    q_tok = [x[:].rearrange("p (t a) n -> p t (a n)", t=2) for x in lat_pt]

    pool_turn, sp_turn = sem("pool_turn"), sem("sp_turn")
    loaded, gate_loaded = sem("weights_loaded"), sem("gate_weights_loaded")
    made, made_v = sem("consts_made_pool"), sem("consts_made_dve")

    def by_head(x):
        return x.rearrange("p (h n) -> p h n", n=HD + 1)

    with nc.Block() as block:
        loads = [
            (w_qk[0], a["attn_qk_w"]), (w_qk[1], a["xattn_qk_w"]),
            (b_qk[0], a["attn_qk_b"]), (b_qk[1], a["xattn_qk_b"]),
            (w_v[0][:, :, VW:], a["attn_v_w"][:, :, D:]), (w_v[1], a["xattn_v_w"]),
            (w_lat, a["lat_w"]), (b_lat, a["lat_b"]), (w_out, a["attn_out_w"]),
        ]
        rows = [(b_v[0][:, VW:], a["attn_v_b"][D:]), (b_v[1], a["xattn_v_b"]), (b_out, a["attn_out_b"]),
                (gamma, a["xattn_gamma"]), (beta, a["xattn_beta"])]
        gate_loads = [(by_head(w_v[0][:, c, 0:VW])[:, :, 0:HD],
                       a["attn_v_w"][:, c, 0:D].rearrange("p (h n) -> p h n", n=HD)) for c in range(C)]
        gate_loads += [(by_head(b_v[0][:, 0:VW])[:, :, 0:HD],
                        a["attn_v_b"][0:D].partition_broadcast(128).rearrange("p (h n) -> p h n", n=HD)),
                       (gate_l, a["attn_gl_w"].partition_broadcast(128)),
                       (gate_r, a["attn_gr_w"].partition_broadcast(128)),
                       (w_rout[HD:HD + 1, 0:D], a["attn_rout_b"].unsqueeze(0))]
        gate_loads += [(w_rout[HW * h:HW * h + HD, 0:D], a["attn_rout_w"][HD * h:HD * h + HD, :]) for h in range(LH)]

        @block.sync
        def _(sp):
            sp.dma_start(x_sb[:, 0:4, :], a["x"].rearrange("s p d -> p s d")[:, 0:4, :]).then_inc(loaded, 16)
            sp.wait_ge(made_v, 1)
            for tile, src in gate_loads:
                sp.dma_start(tile[:], src).then_inc(gate_loaded, 16)
            for tile, src in loads:
                sp.dma_start(tile[:], src).then_inc(loaded, 16)
            for tile, src in rows:
                sp.dma_start(tile[:], src.partition_broadcast(128)).then_inc(loaded, 16)
            sp.wait_ge(gate_loaded, 16 * len(gate_loads))
            sp.wait_ge(loaded, 16 * (1 + len(loads) + len(rows)))

        @block.vector
        def _(dve):
            nc.vector.memset(w_rout[:], 0.0).then_inc(made_v, 1)
            for t in range(2):
                nc.vector.memset(v_heads[t][:], 0.0).then_inc(made_v, 1)
                nc.vector.memset(rv_heads[t][:], 0.0).then_inc(made_v, 1)
            nc.vector.memset(lat_rows[:], 0.5).then_inc(made_v, 1)
            nc.vector.memset(lat_f[:], 0.0).then_inc(made_v, 1)
            dve.wait_ge(made_v, 7)
            nc.vector.memset(k_stack[0][SPLIT:STACK, :, :], 1.0).then_inc(made_v, 1)
            for t in range(2):
                nc.vector.memset(v_heads[t][:, :, :, ONE:ONE + 1], 1.0).then_inc(made_v, 1)
            nc.vector.memset(lat_rows[0:2, :], 0.0).then_inc(made_v, 1)
            dve.wait_ge(gate_loaded, 16 * len(gate_loads))
            terms = [(w_v[0][:, :, 0:VW].rearrange("p c (h n) -> p c h n", n=HD + 1), gate_l, tmp[0][:]),
                     (by_head(b_v[0][:, 0:VW]).unsqueeze(1), gate_l, tmp[1][:, 0:1, :])]
            for w, g, products in terms:
                n = w.shape[1]
                nc.vector.tensor_tensor(products.rearrange("p c (h n) -> p c h n", n=HD), w[:, :, :, 0:HD],
                                        g[:].unsqueeze(1).unsqueeze(1).to_broadcast([128, n, H, HD]),
                                        ALU.mult).then_inc(made_v, 1)
            nc.vector.tensor_tensor(tmp[1][:, 1, :].rearrange("p (h n) -> p h n", n=HD),
                                    w_rout[:, 0:D].rearrange("p (h n) -> p h n", n=HD),
                                    gate_r[:].unsqueeze(1).to_broadcast([128, H, HD]), ALU.mult).then_inc(made_v, 1)
            dve.wait_ge(made_v, 14)
            for w, g, products in terms:
                nc.vector.tensor_reduce(w[:, :, :, HD], products.rearrange("p c (h n) -> p c h n", n=HD), AX.X,
                                        ALU.add).then_inc(made_v, 1)
            nc.vector.tensor_reduce(w_rout[:, D:], tmp[1][:, 1, :].rearrange("p (h n) -> p h n", n=HD), AX.X,
                                    ALU.add).then_inc(made_v, 1)
            dve.wait_ge(made_v, 17)

        @block.gpsimd
        def _(pool):
            nc.gpsimd.memset(minus_half[:], -0.5)
            nc.gpsimd.memset(ones_sq[:], 1.0).then_inc(made, 1)
            nc.gpsimd.memset(mask[0][:], 0.0).then_inc(made, 1)
            nc.gpsimd.memset(mask[1][:], 0.0).then_inc(made, 1)
            nc.gpsimd.memset(mask_lat[:], 0.0).then_inc(made, 1)
            nc.gpsimd.memset(eps[:], LN_EPS).then_inc(made, 1)
            pool.wait_ge(made, 5)
            nc.gpsimd.affine_select(out=ident[:], in_=ones_sq[:], pattern=[[-1, 128]], compare_op=ALU.is_equal,
                                    fill=0.0, base=0, channel_multiplier=1).then_inc(made, 1)
            nc.gpsimd.affine_select(out=mask[0][:], in_=mask[0][:], pattern=[[0, 4], [-1, 128]], compare_op=ALU.is_ge,
                                    fill=NEG, base=-1, channel_multiplier=1).then_inc(made, 1)
            nc.gpsimd.affine_select(out=mask[1][:], in_=mask[1][:], pattern=[[0, 4], [-1, 128]], compare_op=ALU.is_ge,
                                    fill=NEG, base=0, channel_multiplier=1).then_inc(made, 1)
            nc.gpsimd.affine_select(out=mask_lat[:], in_=mask_lat[:], pattern=[[0, LH], [-2, LAT]], compare_op=ALU.is_ge,
                                    fill=NEG, base=-2, channel_multiplier=1).then_inc(made, 1)
            pool.wait_ge(made, 9)
            nc.gpsimd.memset(mask[0][0:1, :, 0:1], 0.0).then_inc(made, 1)
            nc.gpsimd.memset(mask_lat[0:2, :, 0:1], 0.0).then_inc(made, 1)
            nc.gpsimd.tensor_copy(ident_bf[:], ident[:]).then_inc(made, 1)
            pool.wait_ge(made, MADE - 1)
            nc.gpsimd.memset(k_stack[1][SPLIT:STACK, :, :], 1.0).then_inc(made, 1)
            pool.wait_ge(made, MADE)

    attn_phase(nc, sem, locals(), local=True)
    attn_phase(nc, sem, locals(), local=False)


def attn_phase(nc, sem, t, local):
    ph = 0 if local else 1
    P = "ab"[ph]
    a, bank, x_sb, ident, ident_bf = t["a"], t["bank"], t["x_sb"], t["ident"], t["ident_bf"]
    var_eps, minus_half, eps, pool_turn, sp_turn = (
        t[k] for k in ("var_eps", "minus_half", "eps", "pool_turn", "sp_turn"))
    out_stats, out_moments, out_var_eps, out_rstd = (
        t[k] for k in ("out_stats", "out_moments", "out_var_eps", "out_rstd"))
    (ctx_in, stats, moments, rstd, xn, xn_t, ctx_t, qk_f, qk_rest, qk_part, lat_f, lat_raw, lat_rest, lat_part) = (
        t[k] for k in ("ctx_in", "stats", "moments", "rstd", "xn", "xn_t", "ctx_t", "qk_f", "qk_rest", "qk_part",
                       "lat_f", "lat_raw", "lat_rest", "lat_part"))
    (q_stack, k_stack, rq_stack, rk_stack, v_heads, rv_heads, v_raw, neg_max, max_part, max_t, probs_t, av_t) = (
        t[k] for k in ("q_stack", "k_stack", "rq_stack", "rk_stack", "v_heads", "rv_heads", "v_raw", "neg_max",
                       "max_part", "max_t", "probs_t", "av_t"))
    (sums, inv, attn, lat_max, lat_s, lat_p, lat_sum, lat_inv, lat_w, lat_pd, lat_pt, lat_out, remote, remote_g) = (
        t[k] for k in ("sums", "inv", "attn", "lat_max", "lat_s", "lat_p", "lat_sum", "lat_inv", "lat_w", "lat_pd",
                       "lat_pt", "lat_out", "remote", "remote_g"))
    (tmp, z_local, z_remote, gate_z, gate_t, gate, mix_t, x_bias, q_tok, lat_rows) = (
        t[k] for k in ("tmp", "z_local", "z_remote", "gate_z", "gate_t", "gate", "mix_t", "x_bias", "q_tok", "lat_rows"))
    w_qk, b_qk, w_v, b_v, mask = (t[k][ph] for k in ("w_qk", "b_qk", "w_v", "b_v", "mask"))
    w_lat, b_lat, w_rout, w_out, b_out, gamma, beta, mask_lat = (
        t[k] for k in ("w_lat", "b_lat", "w_rout", "w_out", "b_out", "gamma", "beta", "mask_lat"))

    tr_bank, proj_bank, score_bank, av_bank, back_bank, out_bank = (
        bank[0], bank[1:3], bank[3:5], bank[5], bank[6], bank[7])

    v_bank = (tr_bank, proj_bank[0]) if local else (out_bank, tr_bank)

    only_local = """lat_filled lat_evac lat_ready ls_filled lmax_done lsub_done lexp_done lsum_step lp_ready
        lpT_filled lpT_ready lo_filled lo_ready remote_filled remote_ready z_in z_ready tanh_ready
        gate_ready mixed mixT_filled mixT_ready out_filled xb_ready""".split()
    only_context = "ctxT_filled ctxT_ready v_relu qT_filled qT_ready sum_ready norm_ready norm_step norm_eps norm_scaled".split()

    def s(name):
        return None if name in (only_context if local else only_local) else sem(f"{P}_{name}")

    x_loaded = [s(f"x_loaded{i}") for i in range(2)]
    ln_step, xn_ready = s("ln_step"), s("xn_ready")
    ln_eps, ln_scaled = s("ln_eps"), s("ln_scaled")
    norm_eps, norm_scaled = s("norm_eps"), s("norm_scaled")
    xnT_filled, xnT_ready = s("xnT_filled"), s("xnT_ready")
    ctxT_filled, ctxT_ready = s("ctxT_filled"), s("ctxT_ready")
    q_filled, k_filled, q_ready, k_ready = s("q_filled"), s("k_filled"), s("q_ready"), s("k_ready")
    lat_filled, lat_evac, lat_ready = s("lat_filled"), s("lat_evac"), s("lat_ready")
    v_filled, v_ready, v_relu = s("v_filled"), s("v_ready"), s("v_relu")
    part_step = s("part_step")
    stacked = [s(f"stacked{i}") for i in range(2)]
    lat_stacked = [s(f"lat_stacked{i}") if local else None for i in range(2)]
    max_stacked = [s(f"max_stacked{i}") for i in range(2)]
    sc_filled, max_done = s("sc_filled"), s("max_done")
    max_step = s("max_step")
    maxT_filled, maxT_ready = s("maxT_filled"), s("maxT_ready")
    sct_filled, exp_done, masked = s("sct_filled"), s("exp_done"), s("masked")
    av_filled, av_ready = s("av_filled"), s("av_ready")
    back_filled, sum_step, attn_ready = s("back_filled"), s("sum_step"), s("attn_ready")
    ls_filled, lmax_done, lsub_done, lexp_done = s("ls_filled"), s("lmax_done"), s("lsub_done"), s("lexp_done")
    lsum_step, lp_ready = s("lsum_step"), s("lp_ready")
    lpT_filled, lpT_ready, lo_filled, lo_ready = s("lpT_filled"), s("lpT_ready"), s("lo_filled"), s("lo_ready")
    remote_filled, remote_ready = s("remote_filled"), s("remote_ready")
    mix_step, z_in, z_ready, tanh_ready, gate_ready = (
        s("mix_step"), s("z_in"), s("z_ready"), s("tanh_ready"), s("gate_ready"))
    mixed, mixT_filled, mixT_ready = s("mixed"), s("mixT_filled"), s("mixT_ready")
    out_filled, xb_ready, x_done = s("out_filled"), s("xb_ready"), s("x_done")
    qT_filled, qT_ready = s("qT_filled"), s("qT_ready")
    sum_ready, norm_ready, norm_step = s("sum_ready"), s("norm_ready"), s("norm_step")

    STEPS = 3 * 2 + (4 if local else 0)
    STACKED = 16 * NPROD * 2

    source = (a["x"] if local else a["ctx"]).rearrange("s p d -> p s d")

    CAME = 16 if local else 0
    EARLY = 2
    LAG = 2 if local else 3

    with nc.Block() as block:

        @block.sync
        def _(sp):
            def load(at):
                if local:
                    dst = x_sb[:, bass.ds(at.row, 2), :]
                else:
                    wait(sp, ctxT_filled, at.count(1, -1))
                    dst = ctx_in[at.par]
                wait(sp, x_loaded[at.par], at.turn(16, -CAME))
                sp.dma_start(dst, source[:, bass.ds(at.row, 2), :]).then_inc(x_loaded[at.par], 16)

            def stack_max(at):
                wait(sp, maxT_ready, at.count(1, 1))
                sp.dma_start(q_stack[at.par][SPLIT:STACK, :, :], max_t[:]).then_inc(max_stacked[at.par], 16)

            def step(at):
                p = at.par
                wait(sp, av_filled, at.count(GROUPS, -GROUPS))
                if at.off >= 2:
                    sp.sem_inc(sp_turn, 1)
                copies = 0
                order = [("q", 0), ("q", 1), ("k", 0), ("k", 1), ("q", 2), ("k", 2)]
                if local:
                    order += [("lat", 0), ("lat", 1), ("lat", 2)]
                for what, part in order:
                    if what != "lat" and part == 0:
                        wait(sp, q_ready if what == "q" else k_ready, at.count(1, 1))
                    else:
                        n = {"q": (0, 2, 3), "k": (0, 5, 6), "lat": (7, 9, 10)}[what][part]
                        wait(sp, part_step, at.count(STEPS, n))
                    for j in range(NPROD):
                        rows = slice(HD * j, HD * j + HD)
                        if copies == EARLY and at.off > 0:
                            stack_max(at.back())
                            copies += 1
                        copies += (Q_PART if what in "q lat" else K_PART)[j] == part
                        if what == "q" and Q_PART[j] == part:
                            sp.dma_start(q_stack[p][rows, :, :], qk_part[part][:, 0:2, :]).then_inc(stacked[p], 16)
                        if what == "k" and K_PART[j] == part:
                            sp.dma_start(k_stack[p][rows, :, :], qk_part[part][:, 2:4, :]).then_inc(stacked[p], 16)
                        if what == "lat" and Q_PART[j] == part:
                            sp.dma_start(rq_stack[p][rows, :, :], lat_part[part][0:64, :]).then_inc(lat_stacked[p], 16)
                        if what == "lat" and K_PART[j] == part:
                            sp.dma_start(rk_stack[p][rows, :, :],
                                         lat_part[part][64:128, 0:2 * LAT]).then_inc(lat_stacked[p], 16)

            if not local:
                load(At(0, 0))
                load(At(0, 1))

            def load_and_step(at):
                if at.back(-2).real:
                    load(at.back(-2))
                if at.real:
                    step(at)
                else:
                    stack_max(at.back())

            pairs(sp, load_and_step, 1, ahead=1)
            for p in range(2):
                sp.wait_ge(max_stacked[p], 16 * (NPAIR // 2))

        @block.tensor
        def _(pe):
            def transpose_x(at):
                pe.wait_ge(xn_ready, at.count(1, 1))
                wait(pe, xnT_ready, at.count(1, 0))
                wait(pe, v_ready, at.count(2, -1 if local else 0))
                if local:
                    wait(pe, remote_ready, at.count(1, -1))
                for tt in range(2):
                    for c in range(C):
                        mm = pe.transpose(tr_bank[:, c * PT + tt * S:c * PT + tt * S + S],
                                          xn[:, tt, 128 * c:128 * c + 128], ident[:])
                mm.then_inc(xnT_filled, 1)

            def transpose_ctx(at):
                pe.wait_ge(x_loaded[at.par], at.turn(16, 16))
                wait(pe, v_ready, at.count(2, -1))
                for tt in range(2):
                    for c in range(C):
                        mm = pe.transpose(out_bank[:, c * PT + tt * S:c * PT + tt * S + S],
                                          ctx_in[at.par][:, tt, 128 * c:128 * c + 128], ident[:])
                mm.then_inc(ctxT_filled, 1)

            def project(dst, w, src):
                for c in range(C):
                    mm = pe.matmul(dst, w(c), src[:, c, :], start=(c == 0), stop=(c == C - 1))
                return mm

            def project_q(at, g):
                if g == 0:
                    pe.wait_ge(xnT_ready, at.count(1, 1))
                    if local:
                        wait(pe, v_ready, at.count(2, 0))
                    else:
                        wait(pe, q_ready, at.count(1, 0))
                mm = project(proj_bank[0][:, g * PT:g * PT + PT], lambda c: w_qk[:, c, g, :], xn_t)
                if g == 1:
                    mm.then_inc(q_filled, 1)

            def project_k(at, g):
                if g == 0:
                    if not local:
                        pe.wait_ge(ctxT_ready, at.count(1, 1))
                    wait(pe, k_ready, at.count(1, 0))
                mm = project(proj_bank[1][:, g * PT:g * PT + PT], lambda c: w_qk[:, c, 2 + g, :],
                             xn_t if local else ctx_t)
                if g == 1:
                    mm.then_inc(k_filled, 1)

            def project_lat(at):
                pe.wait_ge(q_ready, at.count(1, 1))
                project(proj_bank[0][:, 0:PT], lambda c: w_lat[:, c, :], xn_t).then_inc(lat_filled, 1)

            def project_v(at, tt):
                if local and tt == 1:
                    pe.wait_ge(lat_evac, at.count(1, 1))
                n = w_v.shape[2]
                src = xn_t if local else ctx_t
                for c in range(C):
                    mm = pe.matmul(v_bank[tt][:, 0:n], src[:, c, S * tt:S * tt + S], w_v[:, c, :],
                                   start=(c == 0), stop=(c == C - 1))
                mm.then_inc(v_filled, 1)

            def transpose_q(at):
                pe.wait_ge(q_ready, at.count(1, 1))
                wait(pe, attn_ready, at.count(2, -2))
                for tt in range(2):
                    for g in range(2):
                        mm = pe.transpose(back_bank[:, 256 * tt + 128 * g:256 * tt + 128 * g + 128],
                                          qk_f[:, g, S * tt:S * tt + S], ident[:])
                mm.then_inc(qT_filled, 1)

            def scores(at, g):
                tt, h0, dst = g // 4, 4 * (g % 4), score_bank[g % 2]
                if g >= 2:
                    pe.wait_ge(max_done, at.count(GROUPS, g - 1))
                else:
                    wait(pe, exp_done, at.count(GROUPS, 0))
                if g == 0:
                    pe.wait_ge(stacked[at.par], at.turn(STACKED, STACKED))
                pe.matmul(dst[:], ident_bf[:], mask[:].rearrange("p j k -> p (j k)"), start=True, stop=False,
                          skip_group_check=True)
                for j in range(4):
                    mm = pe.matmul(dst[:, 128 * j:128 * j + 128], q_stack[at.par][0:SPLIT, h0 + j, S * tt:S * tt + S],
                                   k_stack[at.par][0:SPLIT, h0 + j, S * tt:S * tt + S],
                                   start=False, stop=(j == 3), skip_group_check=True)
                mm.then_inc(sc_filled, 1)

            def max_transpose(at):
                pe.wait_ge(max_step, at.count(2, 2))
                wait(pe, av_ready, at.count(2, 0))
                dst = av_bank[:].bitcast(BF16)
                for tt in range(2):
                    mm = pe.transpose(dst[0:2 * H, S * tt:S * tt + S],
                                      max_part[:, tt, :, :].rearrange("p a h -> p (a h)"), ident_bf[:])
                mm.then_inc(maxT_filled, 1)

            def lat_scores(at, tt):
                dst = back_bank[:, LH * LAT * tt:LH * LAT * tt + LH * LAT]
                if tt == 0:
                    wait(pe, attn_ready, at.count(2, 0))
                    pe.wait_ge(lat_stacked[at.par], at.turn(STACKED, STACKED))
                pe.matmul(dst, ident_bf[:], mask_lat[:].rearrange("p h l -> p (h l)"), start=True, stop=False,
                          skip_group_check=True)
                for h in range(LH):
                    mm = pe.matmul(dst[:, LAT * h:LAT * h + LAT], rq_stack[at.par][0:SPLIT, h, S * tt:S * tt + S],
                                   rk_stack[at.par][0:SPLIT, h, LAT * tt:LAT * tt + LAT],
                                   start=False, stop=(h == LH - 1), skip_group_check=True)
                if tt == 1:
                    mm.then_inc(ls_filled, 1)

            def lat_transpose(at, tt):
                if tt == 0:
                    if at.back(-1).real:
                        pe.wait_ge(v_ready, at.count(2, 3))
                    pe.wait_ge(lp_ready, at.count(1, 1))
                else:
                    wait(pe, x_done, at.count(1, 0))
                for h in range(LH):
                    mm = pe.transpose((tr_bank, out_bank)[tt][:, 128 * h:128 * h + 128],
                                      lat_pd_view(tt, h), ident[:])
                mm.then_inc(lpT_filled, 1)

            def lat_pd_view(tt, h):
                return lat_pd[:, tt, h, :, :].rearrange("p l r -> p (l r)")

            def lat_values(at):
                pe.wait_ge(lpT_ready, at.count(2, 2))
                pe.wait_ge(v_ready, at.count(2, 2))
                for tt in range(2):
                    for h in range(LH):
                        mm = pe.matmul(tr_bank[HW * h:HW * h + HW, S * tt:S * tt + S],
                                       rv_heads[at.par][:, tt, h, :], lat_pt[tt][:, h, :], start=True, stop=True,
                                       skip_group_check=True)
                mm.then_inc(lo_filled, 1)

            def remote_out(at):
                pe.wait_ge(lo_ready, at.count(1, 1))
                for tt in range(2):
                    pe.matmul(out_bank[:, D * tt:D * tt + D], lat_out[:, S * tt:S * tt + S], w_rout[:, 0:D],
                              start=True, stop=True, skip_group_check=True)
                for tt in range(2):
                    mm = pe.matmul(tr_bank[:, PT + H * tt:PT + H * tt + H], lat_out[:, S * tt:S * tt + S], w_rout[:, D:],
                                   start=True, stop=True, skip_group_check=True)
                mm.then_inc(remote_filled, 1)

            def scores_t(at, g):
                tt, h0, dst = g // 4, 4 * (g % 4), score_bank[g % 2]
                if g >= 2:
                    pe.wait_ge(exp_done, at.count(GROUPS, g - 1))
                else:
                    pe.wait_ge(max_done, at.count(GROUPS, 7 + g))
                if g == 0:
                    pe.wait_ge(max_stacked[at.par], at.turn(16, 16))
                for j in range(4):
                    mm = pe.matmul(dst[:, 128 * j:128 * j + 128], k_stack[at.par][0:STACK, h0 + j, S * tt:S * tt + S],
                                   q_stack[at.par][0:STACK, h0 + j, S * tt:S * tt + S],
                                   start=True, stop=True, skip_group_check=True)
                mm.then_inc(sct_filled, 1)

            def values(at, g):
                tt, h0 = g // 4, 4 * (g % 4)
                pe.wait_ge(masked, at.count(GROUPS, g + 1))
                if g == 0:
                    pe.wait_ge(v_ready if local else v_relu, at.count(2, 2))
                if g == 4:
                    pe.wait_ge(av_ready, at.count(2, 1))
                for j in range(4):
                    mm = pe.matmul(av_bank[HW * j:HW * j + HW, 128 * (g % 4):128 * (g % 4) + 128],
                                   v_heads[at.par][:, tt, h0 + j, :], probs_t[g % 4][:, j, :],
                                   start=True, stop=True, skip_group_check=True)
                mm.then_inc(av_filled, 1)

            def back(at, tt):
                pe.wait_ge(av_ready, at.count(2, tt + 1))
                if tt == 1:
                    pe.wait_ge(attn_ready, at.count(2, 1))
                elif local:
                    wait(pe, mixT_ready, at.count(1, 0))
                else:
                    qT = 2 if at.off + 1 < NPAIR or not isinstance(at.i, int) else 1
                    pe.wait_ge(qT_ready, at.count(1, qT))
                for g in range(4):
                    mm = pe.transpose(back_bank[:, 128 * g:128 * g + 128], av_t[tt][:, g, :], ident[:])
                mm.then_inc(back_filled, 1)

            def mix_transpose(at):
                pe.wait_ge(mixed, at.count(1, 1))
                if at.back(-1).real:
                    pe.wait_ge(lsub_done, at.count(1, 2))
                for tt in range(2):
                    for c in range(C):
                        mm = pe.transpose(back_bank[:, 256 * tt + 128 * c:256 * tt + 128 * c + 128],
                                          tmp[3][:, tt, 128 * c:128 * c + 128], ident[:])
                mm.then_inc(mixT_filled, 1)

            def project_out(at):
                pe.wait_ge(mixT_ready, at.count(1, 1))
                pe.wait_ge(remote_ready, at.count(1, 1))
                for tt in range(2):
                    for c in range(C):
                        mm = pe.matmul(out_bank[:, D * tt:D * tt + D], mix_t[:, tt, c, :], w_out[:, c, :],
                                       start=(c == 0), stop=(c == C - 1), skip_group_check=True)
                mm.then_inc(out_filled, 1)

            def step(at):
                prev, old, following = at.back(), at.back(2), at.back(-1)
                q, k, v = ([(at, lambda n, f=f, part=part: f(n, part)) for part in range(2)]
                           for f in (project_q, project_k, project_v))
                after = {1: [(old, lambda n: back(n, 1))], 7: [k[0], k[1]]}
                if local:
                    after.update({3: [q[0]], 4: [q[1]], 5: [(prev, lambda n: lat_scores(n, 0))],
                                  6: [(prev, lambda n: lat_scores(n, 1))]})
                else:
                    after.update({3: [q[0]], 5: [q[1]]})
                if local:
                    before = {0: [(at, project_lat), (old, mix_transpose), v[0]], 2: [(old, project_out)], 3: [v[1]],
                              4: [(prev, lambda n: lat_transpose(n, 0))], 5: [(prev, lambda n: lat_transpose(n, 1))],
                              6: [(prev, lat_values)], 8: [(prev, remote_out)]}
                else:
                    before = {0: [v[0], v[1], (at, transpose_q)], 2: [(following, transpose_ctx)]}
                before[GROUPS + 1] = [(following, transpose_x)]

                def run(steps):
                    for pair, what in steps:
                        if pair.real:
                            what(pair)

                for g in range(GROUPS):
                    if prev.real:
                        scores(prev, g)
                    run(after.get(g, []))
                if prev.real:
                    max_transpose(prev)
                for g in range(GROUPS + LAG):
                    run(before.get(g, []))
                    if prev.real:
                        if g < GROUPS:
                            scores_t(prev, g)
                        if g >= LAG:
                            values(prev, g - LAG)
                        if g == GROUPS:
                            back(prev, 0)

            if not local:
                transpose_ctx(At(0, 0))
            transpose_x(At(0, 0))
            pairs(pe, step, 2, ahead=1)

        @block.scalar
        def _(act):
            def copy_xn(at):
                act.wait_ge(xnT_filled, at.count(1, 1))
                wait(act, v_filled if local else q_filled, at.count(2 if local else 1, 0))
                nc.scalar.activation(xn_t[:].rearrange("p c t -> p (c t)"), tr_bank[:],
                                     ACT.Copy).then_inc(xnT_ready, 1)

            def copy_ctx(at):
                act.wait_ge(ctxT_filled, at.count(1, 1))
                wait(act, v_filled, at.count(2, 0))
                nc.scalar.activation(ctx_t.rearrange("p c t -> p (c t)"), out_bank[:],
                                     ACT.Copy).then_inc(ctxT_ready, 1)

            def step(at):
                prev, old, following = at.back(), at.back(2), at.back(-1)

                def copy_lat_t(tt):
                    act.wait_ge(lpT_filled, prev.count(2, tt + 1))
                    wait(act, lo_filled, prev.count(1, 0))
                    nc.scalar.activation(lat_pt[tt][:].rearrange("p h t -> p (h t)"), (tr_bank, out_bank)[tt][:],
                                         ACT.Copy).then_inc(lpT_ready, 1)

                def evac_qk(filled, ready, g0, reread):
                    act.wait_ge(filled, at.count(1, 1))
                    reread()
                    wait(act, stacked[1 - at.par], at.back().turn(STACKED, STACKED))
                    src = proj_bank[g0 // 2]
                    for dst in (qk_part[0], qk_f):
                        for g in range(2):
                            ins = nc.scalar.activation(dst[:, g0 + g, :], src[:, g * PT:g * PT + PT],
                                                       ACT.Identity if local else ACT.Relu,
                                                       bias=b_qk[:, g0 + g:g0 + g + 1])
                    ins.then_inc(ready, 1)

                def evac_q():
                    def reread():
                        wait(act, part_step, at.count(STEPS, -STEPS + 1))
                        if not local:
                            wait(act, qT_filled, at.count(1, 0))
                    evac_qk(q_filled, q_ready, 0, reread)

                def evac_k():
                    evac_qk(k_filled, k_ready, 2, lambda: wait(act, part_step, at.count(STEPS, -STEPS + 4)))

                def evac_lat():
                    act.wait_ge(lat_filled, at.count(1, 1))
                    wait(act, part_step, at.count(STEPS, -2))
                    nc.scalar.activation(lat_f[0:64, :], proj_bank[0][0:64, 0:PT], ACT.Identity, bias=b_lat[0:64, :])
                    nc.scalar.activation(lat_raw[64:128, :], proj_bank[0][64:128, 0:PT], ACT.Identity,
                                         bias=b_lat[64:128, :]).then_inc(lat_evac, 1)

                def relu_v(tt):
                    act.wait_ge(v_ready, prev.count(2, tt + 1))
                    wait(act, av_filled, prev.count(GROUPS, -GROUPS))
                    nc.scalar.activation(v_heads[prev.par][:, tt, :, 0:HD],
                                         v_raw[:, tt, :].rearrange("p (h n) -> p h n", n=HD),
                                         ACT.Relu).then_inc(v_relu, 1)

                def copy_lat_out():
                    act.wait_ge(lo_filled, prev.count(1, 1))
                    wait(act, remote_filled, prev.count(1, 0))
                    nc.scalar.activation(lat_out[:], tr_bank[:, 0:PT], ACT.Identity,
                                         bias=ident[:, HD:HD + 1]).then_inc(lo_ready, 1)

                def copy_remote():
                    act.wait_ge(remote_filled, prev.count(1, 1))
                    wait(act, mixed, prev.count(1, 0))
                    nc.scalar.activation(z_remote[:].rearrange("p t h -> p (t h)"), tr_bank[:, PT:PT + 2 * H], ACT.Copy)
                    nc.scalar.activation(remote[:].rearrange("p t d -> p (t d)"), out_bank[:],
                                         ACT.Copy).then_inc(remote_ready, 1)

                def copy_mix():
                    act.wait_ge(mixT_filled, old.count(1, 1))
                    wait(act, out_filled, old.count(1, 0))
                    nc.scalar.activation(mix_t[:].rearrange("p t c n -> p (t c n)"), back_bank[:],
                                         ACT.Copy).then_inc(mixT_ready, 1)

                def copy_q_tok():
                    act.wait_ge(qT_filled, at.count(1, 1))
                    wait(act, sum_ready, at.count(1, -1))
                    for tt in range(2):
                        ins = nc.scalar.activation(
                            q_tok[at.par][:, tt, :].rearrange("p (hh g r) -> p g r hh", g=2, r=HD),
                            back_bank[:, 256 * tt:256 * tt + 256].rearrange("p (g r hh) -> p g r hh", g=2, r=HD),
                            ACT.Copy)
                    ins.then_inc(qT_ready, 1)

                def exp(g):
                    act.wait_ge(sct_filled, prev.count(GROUPS, g + 1))
                    wait(act, av_filled, prev.count(GROUPS, g - 3))
                    nc.scalar.activation(probs_t[g % 4][:].rearrange("p j t -> p (j t)"), score_bank[g % 2][:],
                                         ACT.Exp, scale=SCALE).then_inc(exp_done, 1)

                def evac_av(at, tt):
                    act.wait_ge(av_filled, at.count(GROUPS, 4 * tt + 4))
                    wait(act, back_filled, at.count(2, tt - 1))
                    nc.scalar.activation(av_t[tt][:].rearrange("p g t -> p (g t)"), av_bank[:],
                                         ACT.Copy).then_inc(av_ready, 1)

                def copy_max():
                    act.wait_ge(maxT_filled, prev.count(1, 1))
                    wait(act, max_stacked[1 - prev.par], prev.back().turn(16, 16))
                    nc.scalar.activation(max_t[:], av_bank[:].bitcast(BF16)[0:2 * H, 0:PT],
                                         ACT.Copy).then_inc(maxT_ready, 1)

                def gate_tanh(at):
                    act.wait_ge(z_ready, at.count(1, 1))
                    wait(act, gate_ready, at.count(1, 0))
                    nc.scalar.activation(gate_t[:], gate_z[:], ACT.Tanh, scale=0.5).then_inc(tanh_ready, 1)

                def exp_lat():
                    act.wait_ge(lsub_done, prev.count(1, 1))
                    wait(act, lp_ready, prev.count(1, 0))
                    nc.scalar.activation(lat_p[:].rearrange("p t h l -> p (t h l)"),
                                         lat_s[:].rearrange("p t h l -> p (t h l)"),
                                         ACT.Exp, scale=0.5 * SCALE).then_inc(lexp_done, 1)

                if old.real:
                    evac_av(old, 1)
                if not local and prev.real:
                    relu_v(0)
                    relu_v(1)
                if local and old.real:
                    gate_tanh(old)
                if at.real:
                    evac_q()
                if prev.real:
                    copy_max()
                if at.real:
                    evac_k()
                    if not local:
                        copy_q_tok()
                if local and old.real:
                    copy_mix()
                if local and prev.real:
                    exp_lat()
                if prev.real:
                    exp(0)
                    exp(1)
                if local and at.real:
                    evac_lat()
                if prev.real:
                    exp(2)
                if prev.real:
                    exp(3)
                    if local:
                        copy_lat_t(0)
                    exp(4)
                if prev.real:
                    if local:
                        copy_lat_t(1)
                    exp(5)
                    evac_av(prev, 0)
                    if local:
                        copy_lat_out()
                    exp(6)
                if prev.real:
                    exp(7)
                    if local:
                        copy_remote()
                if following.real:
                    if not local:
                        copy_ctx(following)
                    copy_xn(following)

            if not local:
                copy_ctx(At(0, 0))
            copy_xn(At(0, 0))
            pairs(act, step, 2, ahead=1)

        @block.vector
        def _(dve):
            def x_rows(at, tt):
                return x_sb[:, bass.ds(at.row + tt, 1), :].rearrange("p s d -> p (s d)")

            def x_pair(at):
                return x_sb[:, bass.ds(at.row, 2), :]

            def norm_stats(src, stats, step):
                for tt in range(2):
                    ins = nc.vector.bn_stats(stats[:, tt, :], src(tt))
                ins.then_inc(step, 1)

            def norm_moments(moments, stats, step):
                for tt in range(2):
                    ins = nc.vector.bn_aggr(moments[:, tt, :], stats[:, tt, :])
                ins.then_inc(step, 1)

            def norm_scale(src, dst, moments, rstd, done):
                for tt in range(2):
                    ins = nc.vector.tensor_scalar(dst[:, tt, :], src(tt), moments[:, tt, 0:1], rstd[:, tt:tt + 1],
                                                  ALU.subtract, ALU.mult)
                ins.then_inc(done, 1)

            def x_stats(at):
                if local:
                    wait(dve, x_loaded[at.par], at.turn(16, 16 - CAME))
                norm_stats(lambda tt: x_rows(at, tt), stats, ln_step)

            def x_scale(at):
                dve.wait_ge(ln_scaled, at.count(1, 1))
                wait(dve, xnT_filled, at.count(1, 0))
                norm_scale(lambda tt: x_rows(at, tt), xn, moments, rstd, xn_ready)

            def split(at, n, src, rest, part):
                first = 3 * n + (n == 2)
                if n == 2:
                    nc.vector.tensor_copy(part[0], src).then_inc(part_step, 1)
                    dve.wait_ge(part_step, at.count(STEPS, first))
                wait(dve, part_step, at.count(STEPS, first + 3 - STEPS))
                nc.vector.tensor_tensor(rest, src, part[0], ALU.subtract).then_inc(part_step, 1)
                dve.wait_ge(part_step, at.count(STEPS, first + 1))
                nc.vector.tensor_copy(part[1], rest).then_inc(part_step, 1)
                dve.wait_ge(part_step, at.count(STEPS, first + 2))
                nc.vector.tensor_tensor(part[2], rest, part[1], ALU.subtract).then_inc(part_step, 1)

            def normalise(at, tt):
                dve.wait_ge(back_filled, at.count(2, tt + 1))
                src = back_bank[:].rearrange("p (h n) -> p h n", n=HW)
                nc.vector.tensor_scalar(sums[:, tt, :], src[:, :, ONE], 1e-30, None, ALU.max).then_inc(sum_step, 1)
                dve.wait_ge(sum_step, at.count(4, 2 * tt + 1))
                nc.vector.reciprocal(inv[:, tt, :], sums[:, tt, :]).then_inc(sum_step, 1)
                dve.wait_ge(sum_step, at.count(4, 2 * tt + 2))
                if local:
                    wait(dve, mixed, at.count(1, 0))
                    nc.vector.tensor_tensor(z_local[:, tt, :], src[:, :, HD], inv[:, tt, :], ALU.mult).then_inc(z_in, 1)
                else:
                    wait(dve, sum_ready, at.count(1, 0))
                nc.vector.tensor_tensor(attn[:, tt, :].rearrange("p (h n) -> p h n", n=HD), src[:, :, 0:HD],
                                        inv[:, tt, :].unsqueeze(2).to_broadcast([128, H, HD]),
                                        ALU.mult).then_inc(attn_ready, 1)

            def row_max(at, g):
                tt, h0 = g // 4, 4 * (g % 4)
                dve.wait_ge(sc_filled, at.count(GROUPS, g + 1))
                nc.vector.tensor_reduce(neg_max[:, tt, h0:h0 + 4],
                                        score_bank[g % 2][:].rearrange("p (j k) -> p j k", k=128), AX.X, ALU.max,
                                        negate=True).then_inc(max_done, 1)

            def max_parts(at):
                dve.wait_ge(max_done, at.count(GROUPS, GROUPS))
                wait(dve, maxT_filled, at.count(1, 0))
                nc.vector.tensor_copy(max_part[:, :, 0, :], neg_max[:]).then_inc(max_step, 1)
                dve.wait_ge(max_step, at.count(2, 1))
                nc.vector.tensor_tensor(max_part[:, :, 1, :], neg_max[:], max_part[:, :, 0, :],
                                        ALU.subtract).then_inc(max_step, 1)

            def add_to_x(at):
                dve.wait_ge(out_filled, at.count(1, 1))
                dve.wait_ge(xb_ready, at.count(1, 1))
                nc.vector.tensor_tensor(x_pair(at), out_bank[:].rearrange("p (t d) -> p t d", t=2), x_bias[:],
                                        ALU.add).then_inc(x_done, 1)

            def split_lat(at):
                dve.wait_ge(lat_evac, at.count(1, 1))
                wait(dve, lat_stacked[1 - at.par], at.back().turn(STACKED, STACKED))
                two = lat_raw[64:128, :].rearrange("p (l r) -> p l r", r=2)
                nc.vector.tensor_tensor(lat_f[64:128, 0:2 * LAT], two[:, :, 0], two[:, :, 1],
                                        ALU.add).then_inc(lat_ready, 1)
                dve.wait_ge(lat_ready, at.count(1, 1))
                split(at, 2, lat_f[:], lat_rest[:], [p[:] for p in lat_part])

            def bias_v(at, tt):
                src = v_bank[tt]
                dve.wait_ge(v_filled, at.count(2, tt + 1))
                if local:
                    nc.vector.tensor_tensor(v_heads[at.par][:, tt, :, 0:HD + 1],
                                            src[:, 0:VW].rearrange("p (h n) -> p h n", n=HD + 1),
                                            b_v[:, 0:VW].rearrange("p (h n) -> p h n", n=HD + 1), ALU.add)
                    nc.vector.tensor_tensor(rv_heads[at.par][:, tt, :, 0:HD],
                                            src[:, VW:VW + LH * HD].rearrange("p (h n) -> p h n", n=HD),
                                            b_v[:, VW:].rearrange("p (h n) -> p h n", n=HD),
                                            ALU.add).then_inc(v_ready, 1)
                else:
                    nc.vector.tensor_tensor(v_raw[:, tt, :], src[:, 0:D], b_v[:], ALU.add).then_inc(v_ready, 1)

            def gate_logits(at):
                dve.wait_ge(z_in, at.count(2, 2))
                dve.wait_ge(remote_ready, at.count(1, 1))
                wait(dve, tanh_ready, at.count(1, 0))
                nc.vector.tensor_tensor(gate_z[:], z_local[:], z_remote[:], ALU.add).then_inc(z_ready, 1)

            def gate_value(at):
                dve.wait_ge(tanh_ready, at.count(1, 1))
                wait(dve, mixed, at.count(1, 0))
                nc.vector.tensor_scalar(gate[:], gate_t[:], 0.5, 0.5, ALU.mult, ALU.add).then_inc(gate_ready, 1)

            def lat_center(at):
                src = back_bank[:].rearrange("p (h l) -> p h l", l=LAT)
                dve.wait_ge(ls_filled, at.count(1, 1))
                nc.vector.tensor_reduce(lat_max[:].rearrange("p t h -> p (t h)"), src, AX.X,
                                        ALU.max).then_inc(lmax_done, 1)
                dve.wait_ge(lmax_done, at.count(1, 1))
                wait(dve, lexp_done, at.count(1, 0))
                nc.vector.tensor_tensor(lat_s[:].rearrange("p t h l -> p (t h) l"), src,
                                        lat_max[:].rearrange("p t h -> p (t h)").unsqueeze(2)
                                        .to_broadcast([128, 2 * LH, LAT]), ALU.subtract).then_inc(lsub_done, 1)

            def lat_norm(at):
                dve.wait_ge(lexp_done, at.count(1, 1))
                nc.vector.tensor_reduce(lat_sum[:].rearrange("p t h -> p (t h)"),
                                        lat_p[:].rearrange("p t h l -> p (t h) l"), AX.X,
                                        ALU.add).then_inc(lsum_step, 1)
                dve.wait_ge(lsum_step, at.count(3, 1))
                nc.vector.reciprocal(lat_inv[:], lat_sum[:]).then_inc(lsum_step, 1)
                dve.wait_ge(lsum_step, at.count(3, 2))
                wait(dve, lp_ready, at.count(1, 0))
                nc.vector.tensor_scalar(lat_w[:], lat_inv[:], lat_rows[:, 0:1], None, ALU.mult).then_inc(lsum_step, 1)

            def step(at):
                prev, old = at.back(), at.back(2)
                following, second = At(at.i, at.off + 1), At(at.i, at.off + 2)
                norms = at.real and following.real
                measures = at.real and second.real
                for g in range(GROUPS):
                    if prev.real:
                        row_max(prev, g)
                    if old.real and g == 1:
                        normalise(old, 1)
                    if old.real and local and g == 2:
                        gate_logits(old)
                    if old.real and local and g == 4:
                        gate_value(old)
                if prev.real:
                    max_parts(prev)
                    if local:
                        lat_center(prev)
                if not local and old.real:
                    dve.wait_ge(sum_ready, old.count(1, 1))
                    norm_stats(lambda tt: tmp[0][:, tt, :], out_stats, norm_step)
                    dve.wait_ge(norm_step, old.count(2, 1))
                    if not at.real:
                        norm_moments(out_moments, out_stats, norm_step)
                if at.real:
                    dve.wait_ge(q_ready, at.count(1, 1))
                    split(at, 0, qk_f[:, 0:2, :], qk_rest[:, 0:2, :], [p[:, 0:2, :] for p in qk_part])
                    if not local and old.real:
                        norm_moments(out_moments, out_stats, norm_step)
                if local and prev.real:
                    lat_norm(prev)
                if at.real and local:
                    wait(dve, av_filled, at.count(GROUPS, -GROUPS))
                    bias_v(at, 0)
                if old.real and local:
                    add_to_x(old)
                if at.real:
                    if not local:
                        wait(dve, v_relu, at.count(2, 0))
                        bias_v(at, 0)
                        bias_v(at, 1)
                    dve.wait_ge(k_ready, at.count(1, 1))
                    split(at, 1, qk_f[:, 2:4, :], qk_rest[:, 2:4, :], [p[:, 2:4, :] for p in qk_part])
                if not local and old.real:
                    dve.wait_ge(norm_scaled, old.count(1, 1))
                    wait(dve, x_done, old.count(1, 0))
                    norm_scale(lambda tt: tmp[0][:, tt, :], tmp[1], out_moments, out_rstd, norm_ready)
                if local and at.real:
                    split_lat(at)
                    bias_v(at, 1)
                if norms:
                    x_scale(following)
                if measures:
                    x_stats(second)
                    dve.wait_ge(ln_step, second.count(2, 1))
                if prev.real:
                    normalise(prev, 0)
                if measures:
                    norm_moments(moments, stats, ln_step)

            for k in range(2):
                x_stats(At(0, k))
                dve.wait_ge(ln_step, 2 * k + 1)
                norm_moments(moments, stats, ln_step)
                if k == 0:
                    x_scale(At(0, 0))
            pairs(dve, step, 2, ahead=1)

        @block.gpsimd
        def _(pool):
            def x_pair(at):
                return x_sb[:, bass.ds(at.row, 2), :]

            def one_over_deviation(at, moments, var_eps, rstd, step, with_eps, scaled):
                pool.wait_ge(step, at.count(2, 2))
                nc.gpsimd.tensor_tensor(var_eps[:], moments[:, :, 1], eps[:], ALU.add).then_inc(with_eps, 1)
                pool.wait_ge(with_eps, at.count(1, 1))
                nc.gpsimd.tensor_tensor(rstd[:], var_eps[:], minus_half[:], ALU.pow).then_inc(scaled, 1)

            def x_deviation(at):
                one_over_deviation(at, moments, var_eps, rstd, ln_step, ln_eps, ln_scaled)

            def mask_weights(at, g):
                pool.wait_ge(exp_done, at.count(GROUPS, g + 1))
                pool.sem_inc(pool_turn, 1)
                pt = probs_t[g % 4]
                nc.gpsimd.affine_select(out=pt[:], in_=pt[:], pattern=[[0, 4], [1, 128]], compare_op=ALU.is_ge,
                                        fill=0.0, base=-1 if local else 0, channel_multiplier=-1).then_inc(masked, 1)

            def heads(x):
                return x[:].rearrange("p t (h n) -> p (t h) n", n=HD)

            def bias_x(at):
                wait(pool, x_done, at.count(1, 0))
                nc.gpsimd.tensor_tensor(x_bias[:], x_pair(at), b_out[:].unsqueeze(1).to_broadcast([128, 2, D]),
                                        ALU.add).then_inc(xb_ready, 1)

            def less_remote(at):
                pool.wait_ge(attn_ready, at.count(2, 2))
                pool.wait_ge(remote_ready, at.count(1, 1))
                wait(pool, mixed, at.count(1, 0))
                nc.gpsimd.tensor_tensor(tmp[2][:], attn[:], remote[:], ALU.subtract).then_inc(mix_step, 1)

            def mix(at):
                pool.wait_ge(mix_step, at.count(2, 1))
                pool.wait_ge(gate_ready, at.count(1, 1))
                nc.gpsimd.tensor_tensor(heads(tmp[0]), heads(tmp[2]),
                                        gate[:].rearrange("p t h -> p (t h)").unsqueeze(2)
                                        .to_broadcast([128, 2 * H, HD]), ALU.mult).then_inc(mix_step, 1)
                pool.wait_ge(mix_step, at.count(2, 2))
                wait(pool, mixT_filled, at.count(1, 0))
                nc.gpsimd.tensor_tensor(tmp[3][:], tmp[0][:], remote[:], ALU.add).then_inc(mixed, 1)

            def add_normed(at):
                pool.wait_ge(attn_ready, at.count(2, 2))
                pool.wait_ge(qT_ready, at.count(1, 1))
                wait(pool, norm_ready, at.count(1, 0))
                nc.gpsimd.tensor_tensor(tmp[0][:], attn[:], q_tok[at.par][:], ALU.add).then_inc(sum_ready, 1)

            def out_deviation(at):
                one_over_deviation(at, out_moments, out_var_eps, out_rstd, norm_step, norm_eps, norm_scaled)

            def scale_normed(at):
                pool.wait_ge(norm_ready, at.count(1, 1))
                nc.gpsimd.tensor_tensor(tmp[2][:], tmp[1][:], gamma[:].unsqueeze(1).to_broadcast([128, 2, D]),
                                        ALU.mult).then_inc(mix_step, 1)
                pool.wait_ge(mix_step, at.count(2, 1))
                nc.gpsimd.tensor_tensor(tmp[3][:], tmp[2][:], beta[:].unsqueeze(1).to_broadcast([128, 2, D]),
                                        ALU.add).then_inc(mix_step, 1)
                pool.wait_ge(mix_step, at.count(2, 2))
                nc.gpsimd.tensor_tensor(x_pair(at), x_pair(at), tmp[3][:], ALU.add).then_inc(x_done, 1)

            def lat_weights(at):
                pool.wait_ge(lsum_step, at.count(3, 3))
                wait(pool, lpT_filled, at.count(2, 0))
                nc.gpsimd.tensor_tensor(
                    lat_pd[:].rearrange("p t h l r -> p (t h) l r"),
                    lat_p[:].rearrange("p t h l -> p (t h) l").unsqueeze(3).to_broadcast([128, 2 * LH, LAT, 2]),
                    lat_w[:].rearrange("p t h -> p (t h)").unsqueeze(2).unsqueeze(3)
                    .to_broadcast([128, 2 * LH, LAT, 2]), ALU.mult).then_inc(lp_ready, 1)

            def step(at):
                prev, old = at.back(), at.back(2)
                between = {}
                second = At(at.i, at.off + 2)
                if local:
                    if old.real:
                        less_remote(old)
                        mix(old)
                        bias_x(old)
                else:
                    if old.real:
                        add_normed(old)
                    if old.real:
                        out_deviation(old)
                if local and prev.real:
                    between[2] = lambda: lat_weights(prev)
                for g in range(GROUPS):
                    if g in between:
                        between[g]()
                    if prev.real:
                        mask_weights(prev, g)
                if not local and old.real:
                    scale_normed(old)
                if at.real and second.real:
                    x_deviation(second)

            x_deviation(At(0, 0))
            x_deviation(At(0, 1))
            pairs(pool, step, 2, ahead=1)


def slots(nc, scope, sem, a, out, bank, x_sb, ident):
    def sb(name, shape, dt=F32):
        return scope.enter_context(nc.sbuf_tensor(name, shape, dt))

    G = 3 * D
    PS = 2 * SLOTS
    NOT_CHOSEN = -3e38
    w1 = sb("w1", [128, 2 * C, 128])
    b1 = sb("b1", [128, 1])
    w2 = sb("w2", [128, SLOTS])
    b2 = sb("b2", [128, SLOTS])
    tau = sb("tau", [128, 1])
    tau_abs = sb("tau_abs", [128, 1])
    inv_tau = sb("inv_tau", [128, 1])
    w_ih = sb("w_ih", [128, C, G])
    w_hh = sb("w_hh", [128, C, G])
    b_ih = sb("b_ih", [128, G])
    b_hh = sb("b_hh", [128, G])
    wv = sb("wv", [128, C, D])
    wo = sb("wo", [128, C, D])
    bv = sb("bv", [128, C])
    bv_cols = sb("bv_cols", [128, C, 128])
    b_o = sb("b_o", [128, D])
    slot_init = sb("slot_init", [128, D])
    slot_scale = sb("slot_scale", [128, 1])
    slot0 = sb("slot0", [128, D])
    slot0_t = sb("slot0_t", [128, C, PS])
    mean_w = sb("mean_w", [SLOTS, 1])
    slot_mean = sb("slot_mean", [128, C])
    b1_all = sb("b1_all", [128, 1])
    h_gates = sb("h_gates", [128, G])
    rz_const = sb("rz_const", [128, 2 * D])
    half_hn = sb("half_hn", [128, D])
    n_const = sb("n_const", [128, D])
    w_vo = sb("w_vo", [128, C, D])
    b_vo = sb("b_vo", [128, D])

    stats = sb("f_stats", [128, 2, 6])
    moments = sb("f_moments", [128, 2, 2])
    var_eps = sb("f_var_eps", [128, 2])
    rstd = sb("f_rstd", [128, 2])
    minus_half = sb("f_minus_half", [128, 2])
    eps = sb("f_eps", [128, 2])
    XW = D + 1
    xn_all = sb("f_xn", [128, 4, 2, XW])
    xn = [xn_all[:, i, :, :] for i in range(4)]
    xn_t = sb("f_xn_t", [128, C, PT])
    h_t = sb("h_t", [128, PT])
    logits = sb("logits", [128, 2, SLOTS])
    top = sb("top", [128, 2, TOPK])
    rest = sb("rest", [128, 2, SLOTS])
    neg_top = sb("neg_top", [128, 2])
    expd = sb("expd", [128, 2, SLOTS])
    chosen = sb("chosen", [128, 2, SLOTS])
    chosen_sum = sb("chosen_sum", [128, 2])
    chosen_inv = sb("chosen_inv", [128, 2])
    alpha_all = sb("alpha", [128, 2, 2, PS])
    alpha = [alpha_all[:, i, :, :] for i in range(2)]
    alpha_t = [sb(f"alpha_t{i}", [128, 2, 128]) for i in range(4)]
    w_sum = sb("w_sum", [128, 1])
    w_inv = sb("w_inv", [128, 1])
    gi = sb("gi", [128, D])
    gi_t = sb("gi_t", [128, C, PS])
    rz = sb("rz", [128, 2 * D])
    rz_t = sb("rz_t", [128, 2 * D])
    r_hn = sb("r_hn", [128, D])
    r_hn_c = sb("r_hn_c", [128, D])
    n_in = sb("n_in", [128, D])
    n_out = sb("n_out", [128, D])
    h_n = sb("h_n", [128, D])
    z_hn = sb("z_hn", [128, D])
    slot_new = sb("slot_new", [128, D])
    slot_new_t = sb("slot_new_t", [128, C, PS])
    slot_val = sb("slot_val", [128, D])
    x_bias = sb("f_x_bias", [128, 2, D])
    y = [sb(f"y{i}", [128, 2, D]) for i in range(2)]

    loaded = sem("f_weights_loaded")
    prep_v, prep_p = sem("f_prep_dve"), sem("f_prep_pe")

    with nc.Block() as block:
        loads = [(w1, a["ffn_w1"]), (b1, a["ffn_b1"]), (w2, a["ffn_w2"]), (w_ih, a["ffn_w_ih"]), (w_hh, a["ffn_w_hh"]),
                 (wv, a["ffn_wv"]), (wo, a["ffn_wo"]), (bv, a["ffn_bv"])]
        rows = [(b2, a["ffn_b2"]), (tau, a["ffn_tau"]), (b_ih, a["ffn_b_ih"]), (b_hh, a["ffn_b_hh"]), (b_o, a["ffn_bo"])]

        @block.sync
        def _(sp):
            for tile, src in loads:
                sp.dma_start(tile[:], src).then_inc(loaded, 16)
            for tile, src in rows:
                sp.dma_start(tile[:], src.partition_broadcast(128)).then_inc(loaded, 16)
            for k in range(2):
                half = slice(SLOTS * k, SLOTS * k + SLOTS)
                sp.dma_start(slot_init[half, :], a["ffn_slot_init"]).then_inc(loaded, 16)
                sp.dma_start(slot_scale[half, :], a["ffn_slot_scale"]).then_inc(loaded, 16)
            sp.wait_ge(loaded, 16 * (len(loads) + len(rows) + 4))

        @block.vector
        def _(dve):
            nc.vector.memset(minus_half[:], -0.5)
            nc.vector.memset(eps[:], LN_EPS)
            nc.vector.memset(mean_w[:], 1.0 / SLOTS).then_inc(prep_v, 1)
            nc.vector.memset(alpha_all[:], 0.0).then_inc(prep_v, 1)
            nc.vector.memset(xn_all[:, :, :, D:XW], 1.0).then_inc(prep_v, 1)
            dve.wait_ge(loaded, 16 * (len(loads) + len(rows) + 4))
            nc.vector.tensor_scalar(slot0[:], slot_init[:], slot_scale[:, 0:1], None, ALU.mult).then_inc(prep_v, 1)
            nc.vector.tensor_copy(bv_cols[:], bv[:].unsqueeze(2).to_broadcast([128, C, 128])).then_inc(prep_v, 1)
            nc.vector.scalar_tensor_tensor(tau_abs[:], tau[:], -1.0, tau[:], ALU.mult, ALU.max).then_inc(prep_v, 1)
            dve.wait_ge(prep_v, 6)
            nc.vector.tensor_scalar(tau_abs[:], tau_abs[:], 0.1, None, ALU.add).then_inc(prep_v, 1)
            dve.wait_ge(prep_v, 7)
            nc.vector.reciprocal(inv_tau[:], tau_abs[:]).then_inc(prep_v, 1)
            dve.wait_ge(prep_v, 8)
            nc.vector.tensor_scalar(b2[:], b2[:], inv_tau[:, 0:1], None, ALU.mult).then_inc(prep_v, 1)
            dve.wait_ge(prep_p, 1)
            nc.vector.tensor_copy(slot0_t[:].rearrange("p c n -> p (c n)"), bank[0][:, 0:C * PS]).then_inc(prep_v, 1)
            dve.wait_ge(prep_p, 2)
            nc.vector.tensor_copy(slot_mean[:], bank[1][:, 0:C]).then_inc(prep_v, 1)
            dve.wait_ge(prep_p, 3)
            nc.vector.tensor_tensor(b1_all[:], bank[2][:, 0:1], b1[:], ALU.add).then_inc(prep_v, 1)
            dve.wait_ge(prep_p, 4)
            nc.vector.tensor_tensor(h_gates[:, 0:512], bank[3][:], b_hh[:, 0:512], ALU.add).then_inc(prep_v, 1)
            nc.vector.tensor_tensor(h_gates[:, 512:G], bank[4][:, 0:G - 512], b_hh[:, 512:G], ALU.add).then_inc(prep_v, 1)
            dve.wait_ge(prep_v, 14)
            nc.vector.tensor_tensor(rz_const[:], h_gates[:, 0:2 * D], b_ih[:, 0:2 * D], ALU.add).then_inc(prep_v, 1)
            nc.vector.tensor_scalar(half_hn[:], h_gates[:, 2 * D:G], 0.5, None, ALU.mult).then_inc(prep_v, 1)
            dve.wait_ge(prep_v, 16)
            nc.vector.tensor_tensor(n_const[:], half_hn[:], b_ih[:, 2 * D:G], ALU.add).then_inc(prep_v, 1)
            dve.wait_ge(prep_p, 5)
            nc.vector.tensor_copy(w_vo[:].rearrange("p c n -> p (c n)"), bank[5][:, 0:C * D]).then_inc(prep_v, 1)
            nc.vector.tensor_copy(b_vo[:], bank[6][:, 0:D]).then_inc(prep_v, 1)
            dve.wait_ge(prep_v, 19)

        @block.tensor
        def _(pe):
            pe.wait_ge(prep_v, 4)
            for c in range(C):
                mm = pe.transpose(bank[0][:, PS * c:PS * c + PS], slot0[:, 128 * c:128 * c + 128], ident[:])
            mm.then_inc(prep_p, 1)
            for c in range(C):
                mm = pe.matmul(bank[1][:, c:c + 1], slot0[0:SLOTS, 128 * c:128 * c + 128], mean_w[:],
                               start=True, stop=True, skip_group_check=True)
            mm.then_inc(prep_p, 1)
            pe.wait_ge(prep_v, 11)
            for c in range(C):
                mm = pe.matmul(bank[2][:, 0:1], w1[:, C + c, :], slot_mean[:, c:c + 1], start=(c == 0), stop=(c == C - 1))
            mm.then_inc(prep_p, 1)
            for lo, hi, b in ((0, 512, 3), (512, G, 4)):
                for c in range(C):
                    mm = pe.matmul(bank[b][:, 0:hi - lo], slot0_t[:, c, :], w_hh[:, c, lo:hi], start=(c == 0), stop=(c == C - 1))
            mm.then_inc(prep_p, 1)
            for d in range(C):
                for c in range(C):
                    pe.matmul(bank[5][:, D * d:D * d + D], wv[:, c, 128 * d:128 * d + 128], wo[:, c, :],
                              start=(c == 0), stop=(c == C - 1), skip_group_check=True)
            for c in range(C):
                mm = pe.matmul(bank[6][:, 0:D], bv_cols[:, c, :], wo[:, c, :], start=(c == 0), stop=(c == C - 1))
            mm.then_inc(prep_p, 1)

    tr_bank, hid_bank, logit_bank, in_bank, gate_bank, new_bank, out_bank = (
        bank[0], bank[1], bank[2], bank[3], bank[4:6], bank[6], bank[7])

    def s(name):
        return sem(f"f_{name}")

    ln_eps, ln_scaled = s("ln_eps"), s("ln_scaled")
    ln_step, xn_ready, xnT_filled, xnT_ready = s("ln_step"), s("xn_ready"), s("xnT_filled"), s("xnT_ready")
    hid_filled, hid_ready, logit_filled, logit_ready = s("hid_filled"), s("hid_ready"), s("logit_filled"), s("logit_ready")
    top_ready, negtop_ready, exp_ready = s("top_ready"), s("negtop_ready"), s("exp_ready")
    pick_step, alpha_ready, alphaT_filled, alphaT_ready = s("pick_step"), s("alpha_ready"), s("alphaT_filled"), s("alphaT_ready")
    in_filled, in_step, giT_filled, giT_ready = s("in_filled"), s("in_step"), s("giT_filled"), s("giT_ready")
    gate_filled, rz_ready, rz_tanh, rhn_step, rhn_ready = s("gate_filled"), s("rz_ready"), s("rz_tanh"), s("rhn_step"), s("rhn_ready")
    n_in_ready, n_ready, hn_ready, zhn_ready, slot_ready = s("n_in_ready"), s("n_ready"), s("hn_ready"), s("zhn_ready"), s("slot_ready")
    newT_filled, newT_ready, val_filled, val_ready = s("newT_filled"), s("newT_ready"), s("val_filled"), s("val_ready")
    out_filled, xb_ready, y_ready = s("out_filled"), s("xb_ready"), s("y_ready")
    stored = [s(f"stored{i}") for i in range(2)]

    dest = out.rearrange("s p d -> p s d")
    BY = 4
    LAST = 4

    with nc.Block() as block:

        @block.sync
        def _(sp):
            def step(at):
                give = at.back(4)
                if give.real:
                    sp.wait_ge(y_ready, give.count(1, 1))
                    sp.dma_start(dest[:, bass.ds(give.row, 2), :], y[give.par][:]).then_inc(stored[give.par], 16)

            pairs(sp, step, LAST, by=BY)
            for k in range(2):
                sp.wait_ge(stored[k], 16 * (NPAIR // 2))

        @block.tensor
        def _(pe):
            def slot_inputs(at):
                pe.wait_ge(alpha_ready, at.count(2, 2))
                wait(pe, giT_ready, at.count(1, 0))
                for tt in range(2):
                    half = slice(SLOTS * tt, SLOTS * tt + SLOTS)
                    mm = pe.matmul(in_bank[half, 0:XW], alpha[at.par][:, tt, half], xn[at.off % BY][:, tt, :],
                                   start=True, stop=True, skip_group_check=True)
                mm.then_inc(in_filled, 1)

            def route(at):
                pe.wait_ge(hid_ready, at.count(1, 1))
                wait(pe, logit_ready, at.count(1, 0))
                for tt in range(2):
                    mm = pe.matmul(logit_bank[:, SLOTS * tt:SLOTS * tt + SLOTS], h_t[:, S * tt:S * tt + S], w2[:],
                                   start=True, stop=True, skip_group_check=True)
                mm.then_inc(logit_filled, 1)

            def transpose_x(at):
                pe.wait_ge(xn_ready, at.count(1, 1))
                wait(pe, xnT_ready, at.count(1, 0))
                for tt in range(2):
                    for c in range(C):
                        mm = pe.transpose(tr_bank[:, c * PT + tt * S:c * PT + tt * S + S],
                                          xn[at.off % BY][:, tt, 128 * c:128 * c + 128], ident[:])
                mm.then_inc(xnT_filled, 1)

            def hidden(at):
                pe.wait_ge(xnT_ready, at.count(1, 1))
                wait(pe, hid_ready, at.count(1, 0))
                for c in range(C):
                    mm = pe.matmul(hid_bank[:, 0:PT], w1[:, c, :], xn_t[:, c, :], start=(c == 0), stop=(c == C - 1))
                mm.then_inc(hid_filled, 1)

            def transpose_slots(at):
                pe.wait_ge(slot_ready, at.count(1, 1))
                wait(pe, val_ready, at.count(1, 0))
                for c in range(C):
                    mm = pe.transpose(new_bank[:, PS * c:PS * c + PS], slot_new[:, 128 * c:128 * c + 128], ident[:])
                mm.then_inc(newT_filled, 1)

            def slot_values(at):
                pe.wait_ge(newT_ready, at.count(1, 1))
                for c in range(C):
                    mm = pe.matmul(new_bank[:, 0:D], slot_new_t[:, c, :], w_vo[:, c, :], start=(c == 0), stop=(c == C - 1))
                mm.then_inc(val_filled, 1)

            def transpose_alpha(at):
                wait(pe, y_ready, at.count(1, -2))
                for tt in range(2):
                    mm = pe.transpose(out_bank[:, 128 * tt:128 * tt + 128], alpha[at.par][:, tt, :], ident[:])
                mm.then_inc(alphaT_filled, 1)

            def transpose_inputs(at):
                pe.wait_ge(in_step, at.count(3, 3))
                for c in range(C):
                    mm = pe.transpose(in_bank[:, PS * c:PS * c + PS], gi[:, 128 * c:128 * c + 128], ident[:])
                mm.then_inc(giT_filled, 1)

            def gates(at):
                pe.wait_ge(giT_ready, at.count(1, 1))
                wait(pe, n_in_ready, at.count(1, 0))
                for lo, hi, b in ((0, 2 * D, 0), (2 * D, G, 1)):
                    for c in range(C):
                        mm = pe.matmul(gate_bank[b][:, 0:hi - lo], gi_t[:, c, :], w_ih[:, c, lo:hi],
                                       start=(c == 0), stop=(c == C - 1))
                mm.then_inc(gate_filled, 1)

            def give_out(at):
                pe.wait_ge(val_ready, at.count(1, 1))
                later = 3 if at.back(-2).real else 2 if at.back(-1).real else 1
                pe.wait_ge(alphaT_ready, at.count(1, later))
                for tt in range(2):
                    mm = pe.matmul(out_bank[:, D * tt:D * tt + D], alpha_t[at.off % BY][:, tt, :], slot_val[:],
                                   start=True, stop=True, skip_group_check=True)
                mm.then_inc(out_filled, 1)

            def step(at):
                for back, what in ((2, slot_inputs), (1, route), (0, transpose_x), (4, transpose_slots),
                                   (2, transpose_alpha), (2, transpose_inputs), (0, hidden), (4, slot_values),
                                   (2, gates), (4, give_out)):
                    if at.back(back).real:
                        what(at.back(back))

            pairs(pe, step, LAST, by=BY)

        @block.scalar
        def _(act):
            def copy_xn(at):
                act.wait_ge(xnT_filled, at.count(1, 1))
                wait(act, hid_filled, at.count(1, 0))
                nc.scalar.activation(xn_t[:].rearrange("p c t -> p (c t)"), tr_bank[:], ACT.Copy).then_inc(xnT_ready, 1)

            def copy_slots(at):
                act.wait_ge(newT_filled, at.count(1, 1))
                wait(act, val_filled, at.count(1, 0))
                nc.scalar.activation(slot_new_t[:].rearrange("p c n -> p (c n)"), new_bank[:, 0:C * PS],
                                     ACT.Copy).then_inc(newT_ready, 1)

            def gelu(at):
                act.wait_ge(hid_filled, at.count(1, 1))
                wait(act, logit_filled, at.count(1, 0))
                nc.scalar.activation(h_t[:], hid_bank[:, 0:PT], ACT.Gelu, bias=b1_all[:, 0:1]).then_inc(hid_ready, 1)

            def copy_alpha(at):
                act.wait_ge(alphaT_filled, at.count(1, 1))
                wait(act, out_filled, at.count(1, 1 - BY))
                nc.scalar.activation(alpha_t[at.off % BY][:].rearrange("p t n -> p (t n)"), out_bank[:, 0:256],
                                     ACT.Copy).then_inc(alphaT_ready, 1)

            def copy_inputs(at):
                act.wait_ge(giT_filled, at.count(1, 1))
                wait(act, gate_filled, at.count(1, 0))
                nc.scalar.activation(gi_t[:].rearrange("p c n -> p (c n)"), in_bank[:, 0:C * PS],
                                     ACT.Copy).then_inc(giT_ready, 1)

            def exp(at):
                act.wait_ge(negtop_ready, at.count(1, 1))
                wait(act, alpha_ready, at.count(2, 0))
                for tt in range(2):
                    ins = nc.scalar.activation(expd[:, tt, :], logits[:, tt, :], ACT.Exp, bias=neg_top[:, tt:tt + 1])
                ins.then_inc(exp_ready, 1)

            def gates(at):
                act.wait_ge(rz_ready, at.count(1, 1))
                wait(act, slot_ready, at.count(1, 0))
                nc.scalar.activation(rz_t[:], rz[:], ACT.Tanh, scale=0.5).then_inc(rz_tanh, 1)

            def candidate(at):
                act.wait_ge(n_in_ready, at.count(1, 1))
                wait(act, slot_ready, at.count(1, 0))
                nc.scalar.activation(n_out[:], n_in[:], ACT.Tanh).then_inc(n_ready, 1)

            def step(at):
                for back, what in ((3, gates), (0, copy_xn), (4, copy_slots), (2, copy_alpha),
                                   (2, copy_inputs), (3, candidate), (1, exp), (0, gelu)):
                    if at.back(back).real:
                        what(at.back(back))

            pairs(act, step, LAST, by=BY)

        @block.vector
        def _(dve):
            def x_rows(at, tt):
                return x_sb[:, bass.ds(at.row + tt, 1), :].rearrange("p s d -> p (s d)")

            def norm_stats(at):
                for tt in range(2):
                    ins = nc.vector.bn_stats(stats[:, tt, :], x_rows(at, tt))
                ins.then_inc(ln_step, 1)

            def norm_moments():
                for tt in range(2):
                    ins = nc.vector.bn_aggr(moments[:, tt, :], stats[:, tt, :])
                ins.then_inc(ln_step, 1)

            def norm_scale(at):
                dve.wait_ge(ln_scaled, at.count(1, 1))
                wait(dve, in_filled, at.count(1, 1 - BY))
                for tt in range(2):
                    ins = nc.vector.tensor_scalar(xn[at.off % BY][:, tt, 0:D], x_rows(at, tt), moments[:, tt, 0:1],
                                                  rstd[:, tt:tt + 1], ALU.subtract, ALU.mult)
                ins.then_inc(xn_ready, 1)

            def mean_inputs(at):
                dve.wait_ge(in_filled, at.count(1, 1))
                nc.vector.tensor_scalar(w_sum[:], in_bank[:, D:XW], 1e-8, None, ALU.add).then_inc(in_step, 1)
                dve.wait_ge(in_step, at.count(3, 1))
                nc.vector.reciprocal(w_inv[:], w_sum[:]).then_inc(in_step, 1)
                dve.wait_ge(in_step, at.count(3, 2))
                wait(dve, giT_filled, at.count(1, 0))
                nc.vector.tensor_scalar(gi[:], in_bank[:, 0:D], w_inv[:, 0:1], None, ALU.mult).then_inc(in_step, 1)

            def slot_values(at):
                dve.wait_ge(val_filled, at.count(1, 1))
                wait(dve, out_filled, at.count(1, 0))
                nc.vector.tensor_tensor(slot_val[:], new_bank[:, 0:D], b_vo[:], ALU.add).then_inc(val_ready, 1)

            def route_logits(at):
                dve.wait_ge(logit_filled, at.count(1, 1))
                wait(dve, exp_ready, at.count(1, 0))
                nc.vector.scalar_tensor_tensor(logits[:], logit_bank[:, 0:2 * SLOTS].rearrange("p (t n) -> p t n", t=2),
                                               inv_tau[:, 0:1], b2[:].unsqueeze(1).to_broadcast([128, 2, SLOTS]),
                                               ALU.mult, ALU.add).then_inc(logit_ready, 1)

            def route_top(at):
                for tt in range(2):
                    ins = nc.vector.max(top[:, tt, :], logits[:, tt, :])
                ins.then_inc(top_ready, 1)

            def route_mark(at):
                dve.wait_ge(top_ready, at.count(1, 1))
                nc.vector.tensor_scalar(neg_top[:], top[:, :, 0], -1.0, None, ALU.mult).then_inc(negtop_ready, 1)
                for tt in range(2):
                    ins = nc.vector.match_replace(rest[:, tt, :], top[:, tt, :], logits[:, tt, :], NOT_CHOSEN)
                ins.then_inc(pick_step, 1)

            def route_weights(at):
                dve.wait_ge(pick_step, at.count(4, 1))
                dve.wait_ge(exp_ready, at.count(1, 1))
                for tt in range(2):
                    ins = nc.vector.scalar_tensor_tensor(chosen[:, tt, :], rest[:, tt, :], NOT_CHOSEN, expd[:, tt, :],
                                                         ALU.is_le, ALU.mult)
                ins.then_inc(pick_step, 1)
                dve.wait_ge(pick_step, at.count(4, 2))
                nc.vector.tensor_reduce(chosen_sum[:], chosen[:], AX.X, ALU.add).then_inc(pick_step, 1)
                dve.wait_ge(pick_step, at.count(4, 3))
                nc.vector.reciprocal(chosen_inv[:], chosen_sum[:]).then_inc(pick_step, 1)
                dve.wait_ge(pick_step, at.count(4, 4))
                wait(dve, alphaT_filled, at.count(1, -1))
                for tt in range(2):
                    nc.vector.tensor_scalar(alpha[at.par][:, tt, SLOTS * tt:SLOTS * tt + SLOTS], chosen[:, tt, :],
                                            chosen_inv[:, tt:tt + 1], None, ALU.mult).then_inc(alpha_ready, 1)

            def gates(at):
                dve.wait_ge(gate_filled, at.count(1, 1))
                wait(dve, rz_tanh, at.count(1, 0))
                nc.vector.tensor_tensor(rz[:], gate_bank[0][:], rz_const[:], ALU.add).then_inc(rz_ready, 1)

            def output(at):
                dve.wait_ge(out_filled, at.count(1, 1))
                dve.wait_ge(xb_ready, at.count(1, 1))
                wait(dve, stored[at.par], at.turn(16, 0))
                nc.vector.tensor_tensor(y[at.par][:], out_bank[:].rearrange("p (t d) -> p t d", t=2), x_bias[:],
                                        ALU.add).then_inc(y_ready, 1)

            def candidate(at):
                dve.wait_ge(rhn_ready, at.count(1, 1))
                wait(dve, n_ready, at.count(1, 0))
                nc.vector.tensor_tensor(n_in[:], gate_bank[1][:, 0:D], r_hn_c[:], ALU.add).then_inc(n_in_ready, 1)

            def new_slots(at):
                dve.wait_ge(hn_ready, at.count(1, 1))
                nc.vector.scalar_tensor_tensor(z_hn[:], rz_t[:, D:2 * D], 1.0, h_n[:], ALU.add,
                                               ALU.mult).then_inc(zhn_ready, 1)
                dve.wait_ge(zhn_ready, at.count(1, 1))
                wait(dve, newT_filled, at.count(1, 0))
                nc.vector.scalar_tensor_tensor(slot_new[:], z_hn[:], 0.5, n_out[:], ALU.mult,
                                               ALU.add).then_inc(slot_ready, 1)

            def step(at):
                following, second = at.back(-1), at.back(-2)
                norms = at.real and following.real
                routed, fed, updated, given = (at.back(k) for k in (1, 2, 3, 4))
                if norms:
                    dve.wait_ge(ln_step, following.count(2, 1))
                    dve.wait_ge(xn_ready, at.count(1, 1))
                if fed.real:
                    mean_inputs(fed)
                if routed.real:
                    route_logits(routed)
                if norms:
                    norm_moments()
                if updated.real:
                    candidate(updated)
                if routed.real:
                    dve.wait_ge(logit_ready, routed.count(1, 1))
                if at.real and second.real:
                    dve.wait_ge(ln_step, following.count(2, 2))
                    norm_stats(second)
                if routed.real:
                    route_top(routed)
                    route_mark(routed)
                if given.real:
                    slot_values(given)
                if norms:
                    norm_scale(following)
                if updated.real:
                    new_slots(updated)
                if routed.real:
                    route_weights(routed)
                if fed.real:
                    gates(fed)
                if given.real:
                    output(given)

            norm_stats(At(0, 0))
            dve.wait_ge(ln_step, 1)
            norm_moments()
            norm_scale(At(0, 0))
            dve.wait_ge(ln_step, 2)
            norm_stats(At(0, 1))
            pairs(dve, step, LAST, ahead=1, by=BY)

        @block.gpsimd
        def _(pool):
            def one_over_deviation(at):
                pool.wait_ge(ln_step, at.count(2, 2))
                nc.gpsimd.tensor_tensor(var_eps[:], moments[:, :, 1], eps[:], ALU.add).then_inc(ln_eps, 1)
                pool.wait_ge(ln_eps, at.count(1, 1))
                nc.gpsimd.tensor_tensor(rstd[:], var_eps[:], minus_half[:], ALU.pow).then_inc(ln_scaled, 1)

            def reset_gate(at):
                pool.wait_ge(rz_tanh, at.count(1, 1))
                nc.gpsimd.tensor_tensor(r_hn[:], rz_t[:, 0:D], half_hn[:], ALU.mult).then_inc(rhn_step, 1)
                pool.wait_ge(rhn_step, at.count(1, 1))
                wait(pool, n_in_ready, at.count(1, 0))
                nc.gpsimd.tensor_tensor(r_hn_c[:], r_hn[:], n_const[:], ALU.add).then_inc(rhn_ready, 1)

            def old_less_candidate(at):
                pool.wait_ge(n_ready, at.count(1, 1))
                wait(pool, zhn_ready, at.count(1, 0))
                nc.gpsimd.tensor_tensor(h_n[:], slot0[:], n_out[:], ALU.subtract).then_inc(hn_ready, 1)

            def bias_x(at):
                wait(pool, y_ready, at.count(1, 0))
                nc.gpsimd.tensor_tensor(x_bias[:], x_sb[:, bass.ds(at.row, 2), :],
                                        b_o[:].unsqueeze(1).to_broadcast([128, 2, D]), ALU.add).then_inc(xb_ready, 1)

            def step(at):
                if at.back(3).real:
                    reset_gate(at.back(3))
                if at.real and not at.last:
                    one_over_deviation(At(at.i, at.off + 1, at.by))
                if at.back(3).real:
                    old_less_candidate(at.back(3))
                if at.back(4).real:
                    bias_x(at.back(4))

            one_over_deviation(At(0, 0))
            pairs(pool, step, LAST, ahead=1, by=BY)


def kernel(**inputs):
    import numpy as np
    import concourse.bacc as bacc
    from concourse import mybir as mb
    from concourse.bass_utils import run_bass_kernel_spmd

    given = {k: np.asarray(v) for k, v in inputs.items()}

    def attn(name):
        return given["L0_attn_" + name]

    def xattn(name):
        return given["L0_xattn_" + name]

    def ffn(name):
        return given["L0_ffn_" + name]

    def by_heads(w):
        return w.reshape(*w.shape[:-1], H // 2, 2, HD).swapaxes(-3, -2).swapaxes(-2, -1)

    def by_latent_heads(w):
        return w.reshape(*w.shape[:-1], LH, HD).swapaxes(-2, -1).reshape(*w.shape)

    def chunks(w):
        return w.reshape(w.shape[0] // 128, 128, -1).swapaxes(0, 1)

    def qk_weight(wq, wk):
        w = np.stack([by_heads(wq), by_heads(wk)], axis=1)
        return chunks(w.reshape(D, -1)).reshape(128, C, 4, 128)

    def qk_bias(bq, bk):
        return np.stack([by_heads(bq), by_heads(bk)]).reshape(4, 128).T

    w, bias, lat = attn("qkv_w"), attn("qkv_b"), LH * HD
    laid = {
        "x": given["x"], "ctx": given["ctx_1024"],
        "attn_qk_w": qk_weight(w[:, 0:D], w[:, D:2 * D]),
        "attn_qk_b": qk_bias(bias[0:D], bias[D:2 * D]),
        "attn_v_w": chunks(np.concatenate([w[:, 2 * D:], attn("rkv_w")[:, lat:]], axis=1)),
        "attn_v_b": np.concatenate([bias[2 * D:], attn("rkv_b")[lat:]]),
        "lat_w": chunks(np.concatenate([by_latent_heads(attn("rq_w")), by_latent_heads(attn("rkv_w")[:, :lat])], axis=1)),
        "lat_b": np.concatenate([by_latent_heads(attn("rq_b")), by_latent_heads(attn("rkv_b")[:lat])]).reshape(128, 1),
        "attn_rout_w": attn("rout_w"), "attn_rout_b": attn("rout_b"),
        "attn_out_w": chunks(attn("out_w")), "attn_out_b": attn("out_b"),
        "attn_gl_w": attn("gl_w").reshape(-1), "attn_gr_w": attn("gr_w").reshape(-1),
        "xattn_qk_w": qk_weight(xattn("Wq"), xattn("Wk")),
        "xattn_qk_b": qk_bias(xattn("bq"), xattn("bk")),
        "xattn_v_w": chunks(xattn("Wv")), "xattn_v_b": xattn("bv"),
        "xattn_gamma": xattn("gamma"), "xattn_beta": xattn("beta"),
        "ffn_slot_init": ffn("slot_init"), "ffn_slot_scale": ffn("slot_scale"),
        "ffn_w1": chunks(ffn("w1").T), "ffn_b1": ffn("b1").reshape(128, 1),
        "ffn_w2": ffn("w2").T, "ffn_b2": ffn("b2"), "ffn_tau": ffn("tau"),
        "ffn_w_ih": chunks(ffn("gru_wih").T), "ffn_w_hh": chunks(ffn("gru_whh").T),
        "ffn_b_ih": ffn("gru_bih"), "ffn_b_hh": ffn("gru_bhh"),
        "ffn_wv": chunks(ffn("wv")), "ffn_wo": chunks(ffn("wo").T),
        "ffn_bv": ffn("bv").reshape(C, 128).T, "ffn_bo": ffn("bo"),
    }
    nc = bacc.Bacc("TRN2", target_bir_lowering=False, num_devices=1)
    arrays, args = {}, {}
    for name, value in laid.items():
        value = np.ascontiguousarray(value)
        arrays[f"in_{name}"] = value
        args[name] = nc.dram_tensor(f"in_{name}", value.shape, mb.dt.from_np(value.dtype), kind="ExternalInput").ap()
    out = nc.dram_tensor("out", (B, S, D), mb.dt.float32, kind="ExternalOutput").ap()
    decoder(nc, args, out)
    return run_bass_kernel_spmd(nc, [arrays], core_ids=[0]).results[0]["out"]
```
